# Optimizing a Trainium2 kernel written in Bass

```python
import numpy as np
import jax
import jax.numpy as jnp

def _softmax(x, axis=-1):
    return jax.nn.softmax(x, axis=axis)

def _gelu(x):
    return jax.nn.gelu(x, approximate=True)

def _silu(x):
    return jax.nn.silu(x)

def _sigmoid(x):
    return jax.nn.sigmoid(x)

def _layernorm(x, axis=-1, eps=1e-05):
    m = jnp.mean(x, axis=axis, keepdims=True)
    v = jnp.var(x, axis=axis, keepdims=True)
    return (x - m) / jnp.sqrt(v + eps)

def _scatter_add(tgt, idx, src, axis=0):
    return tgt.at[idx].add(src)

def _segment_sum(src, seg, n):
    return jax.ops.segment_sum(src, seg, n)
kernel_name = 'mk_decoder_postln_d2_seqx_r4_b2f7f0'

def setup_inputs(seed: int=0):
    np.random.seed(seed)
    _w = jnp.asarray

    def _rec_inputs():
        import jax
        import jax.numpy as jnp
        _rk = jax.random.key(seed)
        x = -0.0002928 + 1 * jax.random.normal(jax.random.fold_in(_rk, 1), (2, 1024, 256), jnp.float32)
        _lenS = 1024 - jax.random.randint(jax.random.fold_in(_rk, 7), (2,), 0, max(1, 1024 // 4) + 1, jnp.int32)
        _lenS2 = 77 - jax.random.randint(jax.random.fold_in(_rk, 8), (2,), 0, max(1, 77 // 4) + 1, jnp.int32)
        _ctx_1024P = jax.random.normal(jax.random.fold_in(_rk, 11), (2, 16, 256), jnp.float32)
        _ctx_1024c = jax.random.dirichlet(jax.random.fold_in(_rk, 511), 0.3 * jnp.ones((16,), jnp.float32), (2, 77))
        _ctx_1024t = jnp.einsum('bsk,bkd->bsd', _ctx_1024c, _ctx_1024P)
        _ctx_1024t = _ctx_1024t * jax.lax.rsqrt(jnp.mean(jnp.square(_ctx_1024t)) + 1e-12) * 0.953939
        ctx_1024 = -1.39393e-06 + 0.999914 * (_ctx_1024t + 0.3 * jax.random.normal(jax.random.fold_in(_rk, 611), (2, 77, 256), jnp.float32))
        fside_1x16xSxS2_0 = 3.01377e-06 + 0.0200011 * jax.random.normal(jax.random.fold_in(_rk, 13), (1, 16, 1024, 77), jnp.float32)
        _validS = jnp.arange(1024)[None, :] < _lenS[:, None]
        _validS2 = jnp.arange(77)[None, :] < _lenS2[:, None]
        _causal = jnp.tril(jnp.ones((1024, 1024), dtype=bool))
        mask_Bx1xSxS2_ik1 = jnp.where(jnp.broadcast_to(_validS2[:, None, None, :], (2, 1, 1024, 77)), 1, 0).astype(jnp.int32)
        return (x, ctx_1024, fside_1x16xSxS2_0, mask_Bx1xSxS2_ik1)
    x, ctx_1024, fside_1x16xSxS2_0, mask_Bx1xSxS2_ik1 = _rec_inputs()

    def _L0_attn_setup():
        import jax, jax.numpy as jnp
        import numpy as np
        B, N, D = (2, 1024, 256)
        H, Dh = (8, 64)
        INNER = H * Dh
        W = 64
        NQ = NKV = 256

        def _forward(x, gamma_h, wq_h, wkv_h, wo_h, ln_g, ln_b, wqkv_l, wo_l, rt_q, rt_kv):
            b, n, d = x.shape
            scale = Dh ** (-0.5)
            neg = -jnp.finfo(x.dtype).max
            mu = jnp.mean(x, -1, keepdims=True)
            var = jnp.var(x, -1, keepdims=True)
            xl = (x - mu) / jnp.sqrt(var + 1e-05) * ln_g + ln_b
            q, k, v = jnp.split(xl @ wqkv_l, 3, -1)

            def heads(t):
                return t.reshape(b, n, H, Dh).transpose(0, 2, 1, 3)
            q, k, v = (heads(q), heads(k), heads(v))
            nw = n // W
            qw = q.reshape(b, H, nw, W, Dh)

            def look_around(t):
                tw = t.reshape(b, H, nw, W, Dh)
                tp = jnp.pad(tw, ((0, 0), (0, 0), (1, 1), (0, 0), (0, 0)))
                return jnp.concatenate([tp[:, :, s:s + nw] for s in range(3)], axis=3)
            kk, vv = (look_around(k), look_around(v))
            wi = jnp.arange(nw)[:, None]
            sh = jnp.arange(3)[None, :]
            valid = (wi + sh - 1 >= 0) & (wi + sh - 1 < nw)
            valid = jnp.repeat(valid, W, axis=1)
            sim = jnp.einsum('bhnid,bhnjd->bhnij', qw * scale, kk)
            sim = jnp.where(valid[None, None, :, None, :], sim, neg)
            attn = jax.nn.softmax(sim, axis=-1)
            lo = jnp.einsum('bhnij,bhnjd->bhnid', attn, vv)
            light_out = lo.reshape(b, H, n, Dh).transpose(0, 2, 1, 3).reshape(b, n, INNER) @ wo_l

            def route(rt, num):
                scores = jnp.einsum('bnd,d->bn', x, rt)
                idx = jnp.argsort(scores, axis=-1)
                s = jnp.take_along_axis(scores, idx, -1)
                s = s - jax.lax.stop_gradient(jnp.max(s, -1, keepdims=True))
                e = jnp.exp(s)
                cs = e / jnp.clip(jnp.cumsum(e, -1), 1e-06, None)
                sel_s, sel_i = (cs[:, -num:], idx[:, -num:])
                sel_s = sel_s + jax.lax.stop_gradient(1.0 - sel_s)
                return (sel_s, sel_i)
            sq, iq = route(rt_q, NQ)
            skv, ikv = route(rt_kv, NKV)
            rq = jnp.take_along_axis(x, iq[:, :, None], 1)
            rkv = jnp.take_along_axis(x, ikv[:, :, None], 1)

            def rms(t):
                t = t / jnp.clip(jnp.linalg.norm(t, axis=-1, keepdims=True), 1e-12, None)
                return t * d ** 0.5 * gamma_h
            hq = (rms(rq) @ wq_h).reshape(b, NQ, H, Dh).transpose(0, 2, 1, 3)
            hk, hv = jnp.split(rms(rkv) @ wkv_h, 2, -1)
            hk = hk.reshape(b, NKV, H, Dh).transpose(0, 2, 1, 3)
            hv = hv.reshape(b, NKV, H, Dh).transpose(0, 2, 1, 3)
            hv = hv * skv[:, None, :, None]
            hsim = jnp.einsum('bhid,bhjd->bhij', hq * scale, hk)
            hattn = jax.nn.softmax(hsim, axis=-1)
            ho = jnp.einsum('bhij,bhjd->bhid', hattn, hv)
            ho = ho.transpose(0, 2, 1, 3).reshape(b, NQ, INNER) @ wo_h
            ho = ho * sq[:, :, None]
            heavy_out = jnp.zeros_like(x).at[jnp.arange(b)[:, None], iq].set(ho)
            return light_out + heavy_out
        key = jax.random.key(seed)
        ks = jax.random.split(key, 8)
        std = 0.02
        return {'x': jax.random.normal(ks[0], (B, N, D), jnp.float32), 'gamma_h': jnp.ones((D,), jnp.float32), 'wq_h': jax.random.normal(ks[1], (D, INNER), jnp.float32) * std, 'wkv_h': jax.random.normal(ks[2], (D, 2 * INNER), jnp.float32) * std, 'wo_h': jax.random.normal(ks[3], (INNER, D), jnp.float32) * std, 'ln_g': jnp.ones((D,), jnp.float32), 'ln_b': jnp.zeros((D,), jnp.float32), 'wqkv_l': jax.random.normal(ks[4], (D, 3 * INNER), jnp.float32) * std, 'wo_l': jax.random.normal(ks[5], (INNER, D), jnp.float32) * std, 'rt_q': jax.random.normal(ks[6], (D,), jnp.float32), 'rt_kv': jax.random.normal(ks[7], (D,), jnp.float32)}
    _L0_attn_all = _L0_attn_setup()
    _L0_attn_in = {k: v for k, v in _L0_attn_all.items() if k in ('gamma_h', 'wq_h', 'wkv_h', 'wo_h', 'ln_g', 'ln_b', 'wqkv_l', 'wo_l', 'rt_q', 'rt_kv')}
    del _L0_attn_all

    def _L0_xattn_setup():
        import jax, jax.numpy as jnp
        import numpy as np
        HIDDEN = 256
        HEADS = 16
        HEAD_DIM = HIDDEN // HEADS
        SCALE = HEAD_DIM ** (-0.5)
        NEG_INF = -1000000000.0

        def _split_heads(x):
            B, S, _ = x.shape
            return x.reshape(B, S, HEADS, HEAD_DIM).transpose(0, 2, 1, 3)
        key = jax.random.key(seed)
        ks = jax.random.split(key, 12)
        B, Sq, Sk = (2, 512, 512)
        inp = {'query': jax.random.normal(ks[0], (B, Sq, HIDDEN), jnp.float32), 'key': jax.random.normal(ks[1], (B, Sk, HIDDEN), jnp.float32), 'value': jax.random.normal(ks[2], (B, Sk, HIDDEN), jnp.float32), 'mask': jax.random.randint(ks[3], (B, 1, Sq, Sk), 0, 2, jnp.int32), 'Wq': jax.random.normal(ks[4], (HIDDEN, HIDDEN), jnp.float32) * 0.02, 'bq': jax.random.normal(ks[5], (HIDDEN,), jnp.float32) * 0.02, 'Wk': jax.random.normal(ks[6], (HIDDEN, HIDDEN), jnp.float32) * 0.02, 'bk': jax.random.normal(ks[7], (HIDDEN,), jnp.float32) * 0.02, 'Wv': jax.random.normal(ks[8], (HIDDEN, HIDDEN), jnp.float32) * 0.02, 'bv': jax.random.normal(ks[9], (HIDDEN,), jnp.float32) * 0.02, 'Wo': jax.random.normal(ks[10], (HIDDEN, HIDDEN), jnp.float32) * 0.02}
        return inp
    _L0_xattn_all = _L0_xattn_setup()
    _L0_xattn_in = {k: v for k, v in _L0_xattn_all.items() if k in ('Wq', 'bq', 'Wk', 'bk', 'Wv', 'bv', 'Wo')}
    del _L0_xattn_all

    def _L0_ffn_setup():
        import jax, jax.numpy as jnp
        import numpy as np

        def _bitlinear(x, w_latent):
            scale = jax.lax.stop_gradient(jnp.clip(jnp.mean(jnp.abs(w_latent), axis=1, keepdims=True), 1e-05, None))
            tern = jnp.clip(jnp.round(w_latent / scale), -1.0, 1.0)
            w = w_latent + jax.lax.stop_gradient(tern - w_latent)
            return x @ (w * scale).T
        key = jax.random.key(seed)
        ks = jax.random.split(key, 6)
        dim, hidden, rank = (256, 1024, 16)
        B, S = (4, 1024)
        x = jax.random.normal(ks[0], (B, S, dim), dtype=jnp.float32)
        w_fc = 0.02 * jax.random.normal(ks[1], (hidden, dim), dtype=jnp.float32)
        w_proj = 0.02 * jax.random.normal(ks[2], (dim, hidden), dtype=jnp.float32)
        u = 0.02 * jax.random.normal(ks[3], (hidden, rank), dtype=jnp.float32)
        v = 0.02 * jax.random.normal(ks[4], (rank, dim), dtype=jnp.float32)
        fast_b = jax.random.normal(ks[5], (rank, rank), dtype=jnp.float32)
        gate = jnp.float32(0.05)
        return {'x': x, 'fast_b': fast_b, 'w_fc': w_fc, 'w_proj': w_proj, 'u': u, 'v': v, 'gate': gate}
    _L0_ffn_all = _L0_ffn_setup()
    _L0_ffn_in = {k: v for k, v in _L0_ffn_all.items() if k in ('fast_b', 'w_fc', 'w_proj', 'u', 'v', 'gate')}
    del _L0_ffn_all

    def _L1_attn_setup():
        import jax, jax.numpy as jnp
        import numpy as np
        B, N, C, H = (2, 512, 256, 16)
        D = C // H
        EPS = 1e-12

        def l2norm(t):
            n = jnp.linalg.norm(t, axis=-1, keepdims=True)
            return t / jnp.maximum(n, EPS)
        key = jax.random.key(seed)
        k1, k2, k3 = jax.random.split(key, 3)
        x = jax.random.normal(k1, (B, N, C), dtype=jnp.float32)
        qkv_w = jax.random.normal(k2, (3 * C, C), dtype=jnp.float32) * (1.0 / np.sqrt(C))
        temperature = jnp.ones((H, 1, 1), dtype=jnp.float32)
        proj_w = jax.random.normal(k3, (C, C), dtype=jnp.float32) * (1.0 / np.sqrt(C))
        proj_b = jnp.zeros((C,), dtype=jnp.float32)
        return {'x': x, 'qkv_w': qkv_w, 'temperature': temperature, 'proj_w': proj_w, 'proj_b': proj_b}
    _L1_attn_all = _L1_attn_setup()
    _L1_attn_in = {k: v for k, v in _L1_attn_all.items() if k in ('qkv_w', 'temperature', 'proj_w', 'proj_b')}
    del _L1_attn_all

    def _L1_xattn_setup():
        import jax, jax.numpy as jnp
        import numpy as np
        N_HEADS = 16

        def _split_heads(x, n_heads):
            B, S, D = x.shape
            return x.reshape(B, S, n_heads, D // n_heads).transpose(0, 2, 1, 3)
        key = jax.random.key(seed)
        ks = jax.random.split(key, 5)
        B, S, D = (2, 512, 256)
        H = N_HEADS
        return {'queries': jax.random.normal(ks[0], (B, S, D), dtype=jnp.float32), 'keys': jax.random.normal(ks[1], (B, S, D), dtype=jnp.float32), 'values': jax.random.normal(ks[2], (B, S, D), dtype=jnp.float32), 'bias': jax.random.normal(ks[3], (1, H, S, S), dtype=jnp.float32) * 0.02, 'w_out': jax.random.normal(ks[4], (D, D), dtype=jnp.float32) * (1.0 / np.sqrt(D))}
    _L1_xattn_all = _L1_xattn_setup()
    _L1_xattn_in = {k: v for k, v in _L1_xattn_all.items() if k in ('w_out',)}
    del _L1_xattn_all

    def _L1_ffn_setup():
        import jax, jax.numpy as jnp
        import numpy as np

        def _ln(x, w, b):
            m = jnp.mean(x, axis=-1, keepdims=True)
            v = jnp.var(x, axis=-1, keepdims=True)
            return (x - m) / jnp.sqrt(v + 1e-05) * w + b
        B, T, C = (4, 512, 256)
        E_RWKV, E = (2, 3)
        H = 4 * C
        S = 0.02
        key = jax.random.key(seed)
        ks = jax.random.split(key, 20)
        d = {}
        d['x'] = jax.random.normal(ks[0], (B, T, C), jnp.float32)
        d['v_first'] = jax.random.normal(ks[1], (B, T, C), jnp.float32)
        d['capital_shares'] = jax.random.uniform(ks[2], (E,), jnp.float32)
        d['ln1_w'] = jnp.ones((C,), jnp.float32)
        d['ln1_b'] = jnp.zeros((C,), jnp.float32)
        d['ln2_w'] = jnp.ones((C,), jnp.float32)
        d['ln2_b'] = jnp.zeros((C,), jnp.float32)
        d['Wr'] = S * jax.random.normal(ks[3], (C, C), jnp.float32)
        d['Wv'] = S * jax.random.normal(ks[4], (C, C), jnp.float32)
        d['Wo'] = S * jax.random.normal(ks[5], (C, C), jnp.float32)
        d['Ws'] = S * jax.random.normal(ks[6], (C, C), jnp.float32)
        d['K_rwkv'] = S * jax.random.normal(ks[7], (E_RWKV, C, H), jnp.float32)
        d['V_rwkv'] = S * jax.random.normal(ks[8], (E_RWKV, H, C), jnp.float32)
        d['conf_rwkv'] = S * jax.random.normal(ks[9], (E_RWKV, C), jnp.float32)
        d['W1'] = S * jax.random.normal(ks[10], (C, C), jnp.float32)
        d['W2'] = S * jax.random.normal(ks[11], (C, C), jnp.float32)
        d['W3'] = S * jax.random.normal(ks[12], (C, C), jnp.float32)
        d['conf_trans'] = S * jax.random.normal(ks[13], (C,), jnp.float32)
        d['w_diff'] = S * jax.random.normal(ks[14], (C,), jnp.float32)
        d['W_aff'] = S * jax.random.normal(ks[15], (C, E), jnp.float32)
        d['W_bridge'] = S * jax.random.normal(ks[16], (C, C), jnp.float32)
        return d
    _L1_ffn_all = _L1_ffn_setup()
    _L1_ffn_in = {k: v for k, v in _L1_ffn_all.items() if k in ('v_first', 'capital_shares', 'ln1_w', 'ln1_b', 'ln2_w', 'ln2_b', 'Wr', 'Wv', 'Wo', 'Ws', 'K_rwkv', 'V_rwkv', 'conf_rwkv', 'W1', 'W2', 'W3', 'conf_trans', 'w_diff', 'W_aff', 'W_bridge')}
    del _L1_ffn_all
    return {'x': x, 'ctx_1024': ctx_1024, 'fside_1x16xSxS2_0': fside_1x16xSxS2_0, 'mask_Bx1xSxS2_ik1': mask_Bx1xSxS2_ik1, 'L0_attn_gamma_h': _L0_attn_in['gamma_h'], 'L0_attn_wq_h': _L0_attn_in['wq_h'], 'L0_attn_wkv_h': _L0_attn_in['wkv_h'], 'L0_attn_wo_h': _L0_attn_in['wo_h'], 'L0_attn_ln_g': _L0_attn_in['ln_g'], 'L0_attn_ln_b': _L0_attn_in['ln_b'], 'L0_attn_wqkv_l': _L0_attn_in['wqkv_l'], 'L0_attn_wo_l': _L0_attn_in['wo_l'], 'L0_attn_rt_q': _L0_attn_in['rt_q'], 'L0_attn_rt_kv': _L0_attn_in['rt_kv'], 'L0_xattn_Wq': _L0_xattn_in['Wq'], 'L0_xattn_bq': _L0_xattn_in['bq'], 'L0_xattn_Wk': _L0_xattn_in['Wk'], 'L0_xattn_bk': _L0_xattn_in['bk'], 'L0_xattn_Wv': _L0_xattn_in['Wv'], 'L0_xattn_bv': _L0_xattn_in['bv'], 'L0_xattn_Wo': _L0_xattn_in['Wo'], 'L0_ffn_fast_b': _L0_ffn_in['fast_b'], 'L0_ffn_w_fc': _L0_ffn_in['w_fc'], 'L0_ffn_w_proj': _L0_ffn_in['w_proj'], 'L0_ffn_u': _L0_ffn_in['u'], 'L0_ffn_v': _L0_ffn_in['v'], 'L0_ffn_gate': _L0_ffn_in['gate'], 'L1_attn_qkv_w': _L1_attn_in['qkv_w'], 'L1_attn_temperature': _L1_attn_in['temperature'], 'L1_attn_proj_w': _L1_attn_in['proj_w'], 'L1_attn_proj_b': _L1_attn_in['proj_b'], 'L1_xattn_w_out': _L1_xattn_in['w_out'], 'L1_ffn_v_first': _L1_ffn_in['v_first'], 'L1_ffn_capital_shares': _L1_ffn_in['capital_shares'], 'L1_ffn_ln1_w': _L1_ffn_in['ln1_w'], 'L1_ffn_ln1_b': _L1_ffn_in['ln1_b'], 'L1_ffn_ln2_w': _L1_ffn_in['ln2_w'], 'L1_ffn_ln2_b': _L1_ffn_in['ln2_b'], 'L1_ffn_Wr': _L1_ffn_in['Wr'], 'L1_ffn_Wv': _L1_ffn_in['Wv'], 'L1_ffn_Wo': _L1_ffn_in['Wo'], 'L1_ffn_Ws': _L1_ffn_in['Ws'], 'L1_ffn_K_rwkv': _L1_ffn_in['K_rwkv'], 'L1_ffn_V_rwkv': _L1_ffn_in['V_rwkv'], 'L1_ffn_conf_rwkv': _L1_ffn_in['conf_rwkv'], 'L1_ffn_W1': _L1_ffn_in['W1'], 'L1_ffn_W2': _L1_ffn_in['W2'], 'L1_ffn_W3': _L1_ffn_in['W3'], 'L1_ffn_conf_trans': _L1_ffn_in['conf_trans'], 'L1_ffn_w_diff': _L1_ffn_in['w_diff'], 'L1_ffn_W_aff': _L1_ffn_in['W_aff'], 'L1_ffn_W_bridge': _L1_ffn_in['W_bridge']}

def reference(x, ctx_1024, fside_1x16xSxS2_0, mask_Bx1xSxS2_ik1, L0_attn_gamma_h, L0_attn_wq_h, L0_attn_wkv_h, L0_attn_wo_h, L0_attn_ln_g, L0_attn_ln_b, L0_attn_wqkv_l, L0_attn_wo_l, L0_attn_rt_q, L0_attn_rt_kv, L0_xattn_Wq, L0_xattn_bq, L0_xattn_Wk, L0_xattn_bk, L0_xattn_Wv, L0_xattn_bv, L0_xattn_Wo, L0_ffn_fast_b, L0_ffn_w_fc, L0_ffn_w_proj, L0_ffn_u, L0_ffn_v, L0_ffn_gate, L1_attn_qkv_w, L1_attn_temperature, L1_attn_proj_w, L1_attn_proj_b, L1_xattn_w_out, L1_ffn_v_first, L1_ffn_capital_shares, L1_ffn_ln1_w, L1_ffn_ln1_b, L1_ffn_ln2_w, L1_ffn_ln2_b, L1_ffn_Wr, L1_ffn_Wv, L1_ffn_Wo, L1_ffn_Ws, L1_ffn_K_rwkv, L1_ffn_V_rwkv, L1_ffn_conf_rwkv, L1_ffn_W1, L1_ffn_W2, L1_ffn_W3, L1_ffn_conf_trans, L1_ffn_w_diff, L1_ffn_W_aff, L1_ffn_W_bridge):
    import jax
    import jax.numpy as jnp

    def _L0_attn_ref(x, gamma_h, wq_h, wkv_h, wo_h, ln_g, ln_b, wqkv_l, wo_l, rt_q, rt_kv):
        import jax, jax.numpy as jnp
        import numpy as np
        B, N, D = (2, 1024, 256)
        H, Dh = (8, 64)
        INNER = H * Dh
        W = 64
        NQ = NKV = 256

        def _forward(x, gamma_h, wq_h, wkv_h, wo_h, ln_g, ln_b, wqkv_l, wo_l, rt_q, rt_kv):
            b, n, d = x.shape
            scale = Dh ** (-0.5)
            neg = -jnp.finfo(x.dtype).max
            mu = jnp.mean(x, -1, keepdims=True)
            var = jnp.var(x, -1, keepdims=True)
            xl = (x - mu) / jnp.sqrt(var + 1e-05) * ln_g + ln_b
            q, k, v = jnp.split(xl @ wqkv_l, 3, -1)

            def heads(t):
                return t.reshape(b, n, H, Dh).transpose(0, 2, 1, 3)
            q, k, v = (heads(q), heads(k), heads(v))
            nw = n // W
            qw = q.reshape(b, H, nw, W, Dh)

            def look_around(t):
                tw = t.reshape(b, H, nw, W, Dh)
                tp = jnp.pad(tw, ((0, 0), (0, 0), (1, 1), (0, 0), (0, 0)))
                return jnp.concatenate([tp[:, :, s:s + nw] for s in range(3)], axis=3)
            kk, vv = (look_around(k), look_around(v))
            wi = jnp.arange(nw)[:, None]
            sh = jnp.arange(3)[None, :]
            valid = (wi + sh - 1 >= 0) & (wi + sh - 1 < nw)
            valid = jnp.repeat(valid, W, axis=1)
            sim = jnp.einsum('bhnid,bhnjd->bhnij', qw * scale, kk)
            sim = jnp.where(valid[None, None, :, None, :], sim, neg)
            attn = jax.nn.softmax(sim, axis=-1)
            lo = jnp.einsum('bhnij,bhnjd->bhnid', attn, vv)
            light_out = lo.reshape(b, H, n, Dh).transpose(0, 2, 1, 3).reshape(b, n, INNER) @ wo_l

            def route(rt, num):
                scores = jnp.einsum('bnd,d->bn', x, rt)
                idx = jnp.argsort(scores, axis=-1)
                s = jnp.take_along_axis(scores, idx, -1)
                s = s - jax.lax.stop_gradient(jnp.max(s, -1, keepdims=True))
                e = jnp.exp(s)
                cs = e / jnp.clip(jnp.cumsum(e, -1), 1e-06, None)
                sel_s, sel_i = (cs[:, -num:], idx[:, -num:])
                sel_s = sel_s + jax.lax.stop_gradient(1.0 - sel_s)
                return (sel_s, sel_i)
            sq, iq = route(rt_q, NQ)
            skv, ikv = route(rt_kv, NKV)
            rq = jnp.take_along_axis(x, iq[:, :, None], 1)
            rkv = jnp.take_along_axis(x, ikv[:, :, None], 1)

            def rms(t):
                t = t / jnp.clip(jnp.linalg.norm(t, axis=-1, keepdims=True), 1e-12, None)
                return t * d ** 0.5 * gamma_h
            hq = (rms(rq) @ wq_h).reshape(b, NQ, H, Dh).transpose(0, 2, 1, 3)
            hk, hv = jnp.split(rms(rkv) @ wkv_h, 2, -1)
            hk = hk.reshape(b, NKV, H, Dh).transpose(0, 2, 1, 3)
            hv = hv.reshape(b, NKV, H, Dh).transpose(0, 2, 1, 3)
            hv = hv * skv[:, None, :, None]
            hsim = jnp.einsum('bhid,bhjd->bhij', hq * scale, hk)
            hattn = jax.nn.softmax(hsim, axis=-1)
            ho = jnp.einsum('bhij,bhjd->bhid', hattn, hv)
            ho = ho.transpose(0, 2, 1, 3).reshape(b, NQ, INNER) @ wo_h
            ho = ho * sq[:, :, None]
            heavy_out = jnp.zeros_like(x).at[jnp.arange(b)[:, None], iq].set(ho)
            return light_out + heavy_out
        return _forward(x, gamma_h, wq_h, wkv_h, wo_h, ln_g, ln_b, wqkv_l, wo_l, rt_q, rt_kv)

    def _L0_xattn_ref(query, key, value, mask, Wq, bq, Wk, bk, Wv, bv, Wo):
        import jax, jax.numpy as jnp
        import numpy as np
        HIDDEN = 256
        HEADS = 16
        HEAD_DIM = HIDDEN // HEADS
        SCALE = HEAD_DIM ** (-0.5)
        NEG_INF = -1000000000.0

        def _split_heads(x):
            B, S, _ = x.shape
            return x.reshape(B, S, HEADS, HEAD_DIM).transpose(0, 2, 1, 3)
        B, Sq, _ = query.shape
        q = _split_heads(query @ Wq.T + bq)
        k = _split_heads(key @ Wk.T + bk)
        v = _split_heads(value @ Wv.T + bv)
        scores = jnp.einsum('bhqd,bhkd->bhqk', q, k) * SCALE
        scores = jnp.where(mask == 0, NEG_INF, scores)
        attn = jax.nn.silu(scores)
        out = jnp.einsum('bhqk,bhkd->bhqd', attn, v)
        out = out.transpose(0, 2, 1, 3).reshape(B, Sq, HIDDEN)
        return out @ Wo.T

    def _L0_ffn_ref(x, fast_b, w_fc, w_proj, u, v, gate):
        import jax, jax.numpy as jnp
        import numpy as np

        def _bitlinear(x, w_latent):
            scale = jax.lax.stop_gradient(jnp.clip(jnp.mean(jnp.abs(w_latent), axis=1, keepdims=True), 1e-05, None))
            tern = jnp.clip(jnp.round(w_latent / scale), -1.0, 1.0)
            w = w_latent + jax.lax.stop_gradient(tern - w_latent)
            return x @ (w * scale).T
        h = _bitlinear(x, w_fc) + gate * (x @ v.T @ fast_b.T @ u.T)
        r = jnp.maximum(h, 0.0)
        return _bitlinear(r * r, w_proj)

    def _L1_attn_ref(x, qkv_w, temperature, proj_w, proj_b):
        import jax, jax.numpy as jnp
        import numpy as np
        B, N, C, H = (2, 512, 256, 16)
        D = C // H
        EPS = 1e-12

        def l2norm(t):
            n = jnp.linalg.norm(t, axis=-1, keepdims=True)
            return t / jnp.maximum(n, EPS)
        b, n, c = x.shape
        qkv = jnp.einsum('bnc,fc->bnf', x, qkv_w)
        q, k, v = jnp.split(qkv, 3, axis=-1)
        q = l2norm(q)
        k = l2norm(k)
        q = q.reshape(b, n, H, D).transpose(0, 2, 1, 3)
        k = k.reshape(b, n, H, D).transpose(0, 2, 1, 3)
        v = v.reshape(b, n, H, D).transpose(0, 2, 1, 3)
        scale = 1.0 / np.sqrt(D)
        q = q * scale
        k = k * scale
        attn = jnp.einsum('bhnd,bhkd->bhnk', q, k)
        attn = attn / temperature
        attn = jax.nn.softmax(attn, axis=-1)
        out = jnp.einsum('bhnk,bhkd->bhnd', attn, v)
        out = out.transpose(0, 2, 1, 3).reshape(b, n, c)
        out = jnp.einsum('bnc,oc->bno', out, proj_w) + proj_b
        return out

    def _L1_xattn_ref(queries, keys, values, bias, w_out):
        import jax, jax.numpy as jnp
        import numpy as np
        N_HEADS = 16

        def _split_heads(x, n_heads):
            B, S, D = x.shape
            return x.reshape(B, S, n_heads, D // n_heads).transpose(0, 2, 1, 3)
        H = N_HEADS
        q = _split_heads(queries, H)
        k = _split_heads(keys, H)
        v = _split_heads(values, H)
        hd = k.shape[-1]
        logits = jnp.einsum('bhqd,bhkd->bhqk', q, k) + bias
        weights = jax.nn.softmax(logits * (1.0 / np.sqrt(hd)), axis=-1)
        attn = jnp.einsum('bhqk,bhkd->bhqd', weights, v)
        B, _, Sq, _ = attn.shape
        combined = attn.transpose(0, 2, 1, 3).reshape(B, Sq, H * hd)
        return combined @ w_out

    def _L1_ffn_ref(x, v_first, capital_shares, ln1_w, ln1_b, ln2_w, ln2_b, Wr, Wv, Wo, Ws, K_rwkv, V_rwkv, conf_rwkv, W1, W2, W3, conf_trans, w_diff, W_aff, W_bridge):
        import jax, jax.numpy as jnp
        import numpy as np

        def _ln(x, w, b):
            m = jnp.mean(x, axis=-1, keepdims=True)
            v = jnp.var(x, axis=-1, keepdims=True)
            return (x - m) / jnp.sqrt(v + 1e-05) * w + b
        B, T, C = x.shape
        xln = _ln(x, ln1_w, ln1_b)
        att_out = jax.nn.sigmoid(xln @ Wr) * (xln @ Wv) @ Wo
        rwkv_state = xln @ Ws
        x = x + att_out
        h = _ln(x, ln2_w, ln2_b)
        conf_r = jax.nn.sigmoid(jnp.einsum('btc,ec->bte', h, conf_rwkv))
        conf_t = jax.nn.sigmoid(h @ conf_trans)[..., None]
        confidences = jnp.concatenate([conf_r, conf_t], axis=-1)
        E = confidences.shape[-1]
        difficulty = jax.nn.sigmoid(h @ w_diff)[..., None]
        affinity = h @ W_aff
        bids = confidences * capital_shares * difficulty + affinity
        winners = jnp.argmax(bids, axis=-1)
        flat_h = h.reshape(-1, C)
        flat_state = rwkv_state.reshape(-1, C)
        flat_w = winners.reshape(-1)
        flat_conf = confidences.reshape(-1, E)
        win_conf = jnp.take_along_axis(flat_conf, flat_w[:, None], axis=1)
        scale = win_conf / (jax.lax.stop_gradient(win_conf) + 1e-06)
        hr = jnp.square(jax.nn.relu(jnp.einsum('nc,ech->enh', flat_h, K_rwkv)))
        out_rwkv = jnp.einsum('enh,ehc->enc', hr, V_rwkv)
        out_trans = flat_h @ W1 * jax.nn.sigmoid(flat_state @ W2) @ W3
        all_out = jnp.concatenate([out_rwkv, out_trans[None]], axis=0)
        onehot = jax.nn.one_hot(flat_w, E, dtype=flat_h.dtype)
        final = jnp.einsum('ne,enc->nc', onehot, all_out) * scale
        return x + final.reshape(B, T, C)
    x = _layernorm(x + _L0_attn_ref(x, L0_attn_gamma_h, L0_attn_wq_h, L0_attn_wkv_h, L0_attn_wo_h, L0_attn_ln_g, L0_attn_ln_b, L0_attn_wqkv_l, L0_attn_wo_l, L0_attn_rt_q, L0_attn_rt_kv), axis=-1)
    x = _layernorm(x + _L0_xattn_ref(x, ctx_1024, ctx_1024, mask_Bx1xSxS2_ik1, L0_xattn_Wq, L0_xattn_bq, L0_xattn_Wk, L0_xattn_bk, L0_xattn_Wv, L0_xattn_bv, L0_xattn_Wo), axis=-1)
    x = _layernorm(x + _L0_ffn_ref(x, L0_ffn_fast_b, L0_ffn_w_fc, L0_ffn_w_proj, L0_ffn_u, L0_ffn_v, L0_ffn_gate), axis=-1)
    x = _layernorm(x + _L1_attn_ref(x, L1_attn_qkv_w, L1_attn_temperature, L1_attn_proj_w, L1_attn_proj_b), axis=-1)
    x = _layernorm(x + _L1_xattn_ref(x, ctx_1024, ctx_1024, fside_1x16xSxS2_0, L1_xattn_w_out), axis=-1)
    x = _layernorm(x + _L1_ffn_ref(x, L1_ffn_v_first, L1_ffn_capital_shares, L1_ffn_ln1_w, L1_ffn_ln1_b, L1_ffn_ln2_w, L1_ffn_ln2_b, L1_ffn_Wr, L1_ffn_Wv, L1_ffn_Wo, L1_ffn_Ws, L1_ffn_K_rwkv, L1_ffn_V_rwkv, L1_ffn_conf_rwkv, L1_ffn_W1, L1_ffn_W2, L1_ffn_W3, L1_ffn_conf_trans, L1_ffn_w_diff, L1_ffn_W_aff, L1_ffn_W_bridge), axis=-1)
    return x

_drawn_inputs = setup_inputs


def setup_inputs(seed=0):
    import zlib

    import numpy as np

    out = dict(_drawn_inputs(seed))
    spreads = {'L0_attn_gamma_h': (1.0, 0.6),
     'L0_attn_ln_g': (1.0, 0.6),
     'L0_attn_ln_b': (0.0, 0.414),
     'L1_attn_temperature': (1.0, 0.6),
     'L1_attn_proj_b': (0.0, 0.1),
     'L1_ffn_ln1_w': (1.0, 0.6),
     'L1_ffn_ln1_b': (0.0, 0.8),
     'L1_ffn_ln2_w': (1.0, 0.6),
     'L1_ffn_ln2_b': (0.0, 0.458)}
    factors = {'fside_1x16xSxS2_0': 8.0,
     'L0_attn_wq_h': 8.0,
     'L0_attn_wkv_h': 7.49,
     'L0_attn_wo_h': 7.193,
     'L0_attn_rt_q': 8.0,
     'L0_attn_rt_kv': 8.0,
     'L0_xattn_bq': 5.463,
     'L0_xattn_bk': 5.347,
     'L0_xattn_bv': 5.013,
     'L0_ffn_fast_b': 8.0,
     'L0_ffn_u': 8.0,
     'L0_ffn_v': 8.0,
     'L1_ffn_capital_shares': 3.287,
     'L1_ffn_Wr': 8.0,
     'L1_ffn_Ws': 8.0,
     'L1_ffn_conf_rwkv': 6.059,
     'L1_ffn_W1': 4.264,
     'L1_ffn_W2': 8.0,
     'L1_ffn_W3': 4.211,
     'L1_ffn_conf_trans': 8.0,
     'L1_ffn_w_diff': 8.0}
    for name, (base, spread) in spreads.items():
        noise = np.random.default_rng([zlib.crc32(name.encode()), seed]).standard_normal(out[name].shape)
        drawn = base * np.exp(spread * noise) if base else spread * noise
        out[name] = jnp.asarray(drawn.astype(out[name].dtype))
    for name, factor in factors.items():
        out[name] = (out[name] * factor).astype(out[name].dtype)
    return out
```

```python
from contextlib import ExitStack

import concourse.bass as bass
from concourse import mybir

F32 = mybir.dt.float32
BF16 = mybir.dt.bfloat16
I32 = mybir.dt.int32
ALU = mybir.AluOpType
ACT = mybir.ActivationFunctionType
AXX = mybir.AxisListType.X

P = 128
B, N, D = 2, 1024, 256
T = N // P
U = T // 2
DC = D // P
NC = 512
NH = N // NC
PAD = 64
NP = N + 2 * PAD
H0, DH = 8, 64
PAIRS = H0 * DH // P
NSEL = 256
KEYS = 256
H, DK = 16, 16
S2 = 77
HG = 4
HID = 1024
HT = HID // P
RANK = 16
COMB = 6
ROWS = COMB * DK + 1
NEG = -1.0e30
EPS = 1.0e-5

CONSTS = 28
ONCE = 16
PREP = 17
DVE_STEPS = 246
JOBS = {"V": 117, "A": 217, "SR": 40, "TR": 40, "OR": 10, "S1": 128, "O1": 8, "R1": 8}

SIGNALS = {
    "ld_x": 16, "ld_xT": 16, "ld_wqkv": 16, "ld_ctx": 32, "ld_wheavy": 64, "ld_mask": 16, "ld_w1": 16 * (H + 2),
    "ld_wout": 16, "ld_bias0": 16 * T // 2, "ld_bias1": 16 * T // 2, "ld_w7": 16 * 7, "ld_exp": 64,
    "st_out": 16 * U,
    "ve_ready": 9 * U,
    "rstd_ready": 9 * U,
    "xn_ready": 9 * U,
    "kpad_zero": 2,
    "ss0_ready": 1, "rn0_ready": 1,
    "oh_ready": T,
    "nm_ready": PAIRS * (T + 2),
    "rs_ready": T + 2,
    "e_norm": T + 2,
    "projp_zero": 1, "v_zero": 2, "vpad1_zero": 1,
    "mask_ready": 1,
    "sq_ready": NH * HT * 3,
    "ssq_ready": 2 * T, "rqk_ready": T,
    "qs_ready": T,
    "ot_ready": NH * HG,
    "kv1_ready": 1,
    "mx_ready": T, "sc_shift": T, "sc_exp": T, "en_ready": T,
    "lg_ready": 1, "conf_ready": 1,
    "x2_ready": U, "tt_ready": NH,
    "dve_step": DVE_STEPS, "pool_step": T,
}


class Signal:

    def __init__(self, sem, per):
        self.sem, self.per = sem, per


class Ring:

    def __init__(self, name, banks, full, free, jobs):
        self.name, self.banks, self.full, self.free, self.jobs = name, banks, full, free, jobs

    def bank(self, k):
        return self.banks[k % len(self.banks)]


def decoder(nc, a, out):
    ctx = ExitStack()
    with ctx:
        def sb(name, cols, dt=F32, parts=P):
            return ctx.enter_context(nc.sbuf_tensor(name, [parts] + list(cols), dt))

        def sem(name):
            return ctx.enter_context(nc.semaphore(name))

        X = sb("X", [T, D])
        XN = sb("XN", [T, D])
        XT = sb("XT", [DC, NP])
        W1T = sb("W1T", [DC, HID])
        W2T = sb("W2T", [HT, D])
        xw = sb("xw", [4, DC, D])
        kblk0 = sb("kblk0", [DC, 8, S2])
        vpad0 = sb("vpad0", [H, 32], parts=S2)
        ctxT = sb("ctxT", [DC, S2])
        ctxV = sb("ctxV", [D], parts=S2)
        ident = sb("ident", [P])
        identb = sb("identb", [P], BF16)
        ones = sb("ones", [P])
        iota = sb("iota", [NSEL])
        above = sb("above", [P])
        upto = sb("upto", [P])
        maskb = sb("maskb", [3, 2 * KEYS], BF16)
        selden = sb("selden", [P])
        headm = sb("headm", [8])
        half01 = sb("half01", [2])
        rtb = sb("rtb", [2, DC, P])
        cols = sb("cols", [32])
        tinv = sb("tinv", [H])
        negc = sb("negc", [H])
        cap = sb("cap", [3])
        gatew = sb("gatew", [DC, 8])
        bvb = sb("bvb", [D], parts=S2)
        nhalf = sb("nhalf", [32])
        st = sb("st", [T, 6])
        mv = sb("mv", [T, 2])
        ve = sb("ve", [T])
        rstd = sb("rstd", [T])
        scol = sb("scol", [2, T])
        cnt = sb("cnt", [2, T, 4])
        rank = sb("rank", [2, T])
        ss0 = sb("ss0", [T])
        rn0 = sb("rn0", [T])
        mx = sb("mx", [2, H])
        nm = sb("nm", [2, H0])
        sm = sb("sm", [2, H])
        rs = sb("rs", [2, H])
        ssq = sb("ssq", [T, 2])
        rqk = sb("rqk", [T, 2])
        lg = sb("lg", [T, 8])
        bids = sb("bids", [T, 3])
        win = sb("win", [T, 3])
        cc = sb("cc", [T, 3])
        dd = sb("dd", [T, 3])
        R = sb("R", [34816])

        def r(off, *dims, parts=P):
            n = 1
            for d in dims:
                n *= d
            v = R[0:parts, off:off + n]
            if len(dims) == 2:
                return v.rearrange("p (a b) -> p a b", a=dims[0])
            if len(dims) == 3:
                return v.rearrange("p (a b c) -> p a b c", a=dims[0], b=dims[1])
            if len(dims) == 4:
                return v.rearrange("p (a b c d) -> p a b c d", a=dims[0], b=dims[1], c=dims[2])
            return v

        wqkv = r(0, DC, 3 * 512)
        E = r(0, 2, H0, KEYS)
        Srow = r(4096, 2, N)
        OH = r(6144, 2, 3, NSEL)
        junk = R[:, 26624:30720].bitcast(BF16).rearrange("p (i n) -> p i n", i=8)
        PT = r(4096, 2, PAIRS, 4, P)
        wo_l = r(8192, PAIRS, D)
        wq_h = r(9216, DC, 512)
        wkv_h = r(10240, DC, 1024)
        wo_h = r(12288, PAIRS, D)
        qT = r(13312, PAIRS, N)
        kEO = r(17408, PAIRS, 2, NP)
        xT0 = r(17408, DC, N)
        V1 = r(26624, T + 1, 512)
        hqT = r(31232, PAIRS, NSEL)
        hv = r(32256, 2, 512)
        ho = r(33280, 2, D)
        xsel = r(33792, 2, DC, NSEL)
        OHT = XN[:, :, :].rearrange("p (s t) d -> p s (t d)", s=2)

        def hk(p):
            return XT[:, p // 2, PAD + 512 * (p % 2):PAD + 512 * (p % 2) + 512].rearrange("p (e k) -> p e k", e=2)

        maskI = R[0:S2, 28672:29696].bitcast(I32)
        maskN = R[0:S2, 29696:30208].bitcast(BF16)
        qTx = r(8192, DC, N)
        oTx = r(10240, DC, N)
        AT = r(12288, 4, NC, parts=S2)
        Hb = r(0, 2, HT, NC)
        KT = R[:, 0:8192].bitcast(BF16).rearrange("p (h n) -> p h n", h=H)
        QT = R[:, 8192:16384].bitcast(BF16).rearrange("p (h n) -> p h n", h=H)
        V32 = r(16384, T, H, 32)
        Pb = r(20480, 4, 2, NC)
        QS = R[:, 20480:20480 + 776 * 4].bitcast(BF16).rearrange("p (r s h c) -> p r s h c", r=2, s=2, h=H)
        qkn = r(23584, 512)
        OTp = r(24576, 4, N)
        OS = r(28672, NC)
        RC = r(29184, NC)
        r1 = r(29696, 512)
        r2 = r(30208, 512)
        junkf = r(30720, 2, D)
        wqkv1 = r(31232, DC, 3 * D)
        projp = r(32768, 4, D)
        kblk1 = r(0, DC, 8, S2)
        vpad1 = r(1232, H, 32, parts=S2)
        w_out = r(1744, DC, D)
        biasb = r(8192, 2, H, S2)
        SC = r(10656, 2, H, S2)
        PTx = r(13120, H, P, parts=S2)
        oT1 = r(28672, DC, N)
        XP = r(28672, T, D)
        w7 = r(16384, 7, DC, D)
        Krw = r(20480, 2, DC, HID)
        Vrw = r(24576, 2, HT, D)
        SG = r(8192, DC, NC)
        G = r(9216, DC, NC)
        ST = r(10240, DC, NC)
        TT = r(11264, DC, NC)
        SS2 = r(12288, DC, N)

        PS = ctx.enter_context(nc.psum_tensor("PS", [P, 8, 512], F32))
        bk = [PS[:, i, :] for i in range(8)]

        def ring(name, banks, jobs):
            f, g = sem(f"{name}_full"), sem(f"{name}_free")
            return Ring(name, banks, f, g, jobs)

        A = ring("act_bank", [bk[i] for i in (0, 1, 2, 3)], JOBS["A"])
        V = ring("dve_bank", [bk[i] for i in (4, 5, 6, 7)], JOBS["V"])
        SR = ring("score_bank", [bk[i] for i in (4, 5, 6, 7)], JOBS["SR"])
        TR = ring("probT_bank", [bk[i] for i in (1, 2)], JOBS["TR"])
        OR = ring("wout_bank", [bk[i] for i in (0, 3)], JOBS["OR"])
        S1 = ring("self_bank", [PS[:, 2 * i:2 * i + 2, :] for i in range(3)], JOBS["S1"])
        O1 = ring("sout_bank", [bk[6]], JOBS["O1"])
        R1 = ring("den_bank", [bk[7]], JOBS["R1"])

        def signal(name):
            return Signal(sem(name), SIGNALS[name])

        ld_x = signal("ld_x")
        ld_xT = signal("ld_xT")
        ld_wqkv = signal("ld_wqkv")
        ld_ctx = signal("ld_ctx")
        ld_wheavy = signal("ld_wheavy")
        ld_mask = signal("ld_mask")
        ld_w1 = signal("ld_w1")
        ld_wout = signal("ld_wout")
        ld_w7 = signal("ld_w7")
        ld_exp = signal("ld_exp")
        st_out = signal("st_out")
        ve_ready = signal("ve_ready")
        rstd_ready = signal("rstd_ready")
        xn_ready = signal("xn_ready")
        kpad_zero = signal("kpad_zero")
        ss0_ready = signal("ss0_ready")
        rn0_ready = signal("rn0_ready")
        oh_ready = signal("oh_ready")
        nm_ready = signal("nm_ready")
        rs_ready = signal("rs_ready")
        e_norm = signal("e_norm")
        projp_zero = signal("projp_zero")
        v_zero = signal("v_zero")
        vpad1_zero = signal("vpad1_zero")
        mask_ready = signal("mask_ready")
        sq_ready = signal("sq_ready")
        ssq_ready = signal("ssq_ready")
        rqk_ready = signal("rqk_ready")
        qs_ready = signal("qs_ready")
        ot_ready = signal("ot_ready")
        kv1_ready = signal("kv1_ready")
        mx_ready = signal("mx_ready")
        sc_shift = signal("sc_shift")
        sc_exp = signal("sc_exp")
        en_ready = signal("en_ready")
        lg_ready = signal("lg_ready")
        conf_ready = signal("conf_ready")
        x2_ready = signal("x2_ready")
        tt_ready = signal("tt_ready")
        dve_step = signal("dve_step")
        pool_step = signal("pool_step")
        ld_bias = [signal("ld_bias0"), signal("ld_bias1")]
        marks = {}
        carrier = {x: sem(f"carrier_{x}") for x in ("DVE", "Pool", "SP")}
        const_ready = sem("const_ready")
        ld_once = sem("ld_once")
        prep_dve = sem("prep_dve")
        prep_pe = sem("prep_pe")


        block = ctx.enter_context(nc.Block())

        class Eng:

            def __init__(self, e, b):
                self.e, self.b, self.n, self.k = e, b, {}, 0

            def nth(self, sig, k):
                return self.b * sig.per + k

            def step(self):
                self.k += 1
                return 1

            def steps(self):
                return self.b * dve_step.per + self.k

            def plain(self):
                self.e.sem_inc(carrier[self.e.engine.name], 1)

            def job(self, q):
                return self.n.get(q.name, 0)

            def bank(self, q):
                return q.bank(self.job(q) - 1)

            def take(self, q):
                self.n[q.name] = self.job(q) + 1
                return self.b * q.jobs + self.job(q)

            def claim(self, q):
                self.n[q.name] = self.job(q) + 1
                return self.job(q) > len(q.banks)

            def space(self, q):
                return self.b * q.jobs + self.job(q) - len(q.banks)

            def total(self, q, k=None):
                return self.b * q.jobs + (self.job(q) if k is None else k)

        @block.tensor
        def _(pe):
            mm = pe.matmul
            pe.wait_ge(const_ready, CONSTS)
            pe.wait_ge(ld_once, 16 * ONCE)
            pe.wait_ge(prep_dve, 3)
            absW1, absW2 = r(4096, DC, HID), r(6144, HT, D)
            for n in range(NH):
                for c in range(DC):
                    mm(bk[n], ones[:], absW1[:, c, NC * n:NC * n + NC], start=(c == 0), stop=(c == DC - 1))
            for k in range(HT):
                mm(bk[2][:, 0:D], ones[:], absW2[:, k], start=(k == 0), stop=(k == HT - 1))
            mm(bk[3][0:RANK, 0:D], R[0:RANK, 1280:1280 + RANK], R[0:RANK, 0:D], start=True, stop=True).then_inc(prep_pe, 1)
            pe.wait_ge(prep_dve, 4)
            for c in range(DC):
                for n in range(NH):
                    last = mm(bk[4 + 2 * c + n], R[0:RANK, 1536 + P * c:1536 + P * c + P],
                              R[0:RANK, 256 + NC * n:256 + NC * n + NC], start=True, stop=True)
            last.then_inc(prep_pe, 1)
            pe.wait_ge(prep_dve, PREP)
            with pe.Fori(0, B) as b:
                g = Eng(pe, b)
                xn = [0]

                def accumulate(dst, pairs, first=True, last=True):
                    for i, (lhsT, rhs) in enumerate(pairs):
                        ins = mm(dst, lhsT, rhs, start=(first and i == 0), stop=(last and i == len(pairs) - 1))
                    return ins

                def turn(u, src):
                    xn[0] += 1
                    pe.wait_ge(xn_ready.sem, g.nth(xn_ready, xn[0]))
                    if g.claim(A):
                        pe.wait_ge(A.free, g.space(A))
                    s = g.bank(A)
                    for c in range(DC):
                        for j in range(2):
                            ins = pe.transpose(s[:, 256 * c + P * j:256 * c + P * j + P],
                                               src[:, 2 * u + j, P * c:P * c + P], ident[:])
                    ins.then_inc(A.full, 1)

                def xt(c, t):
                    return XT[:, c, PAD + P * t:PAD + P * t + P]

                def xh(c, n):
                    return XT[:, c, PAD + NC * n:PAD + NC * n + NC]

                def mark(name, q):
                    marks.setdefault(name, []).append(g.job(q))

                pe.wait_ge(ld_ctx.sem, g.nth(ld_ctx, 32))
                if g.claim(V):
                    pe.wait_ge(V.free, g.space(V))
                s = g.bank(V)
                for m in range(DC):
                    accumulate(s[:, P * m:P * m + S2], [(xw[:, 1, c, P * m:P * m + P], ctxT[:, c]) for c in range(DC)])
                accumulate(s[0:S2, 256:512], [(ctxT[:, c], xw[:, 2, c]) for c in range(DC)]).then_inc(V.full, 1)
                pe.wait_ge(ld_xT.sem, g.nth(ld_xT, 16))
                for k in range(2):
                    for n in range(NH):
                        if g.claim(A):
                            pe.wait_ge(A.free, g.space(A))
                        s = g.bank(A)
                        accumulate(s, [(rtb[:, k, c], xT0[:, c, NC * n:NC * n + NC]) for c in range(DC)]).then_inc(A.full, 1)
                mark("srow", A)
                for u in range(U):
                    turn(u, XN)
                pe.wait_ge(ld_wqkv.sem, g.nth(ld_wqkv, 16))
                for n in range(NH):
                    pe.wait_ge(A.free, g.total(A, marks["srow"][0] + 2 * n + 2))
                    for m in range(2 * PAIRS):
                        if g.claim(A):
                            pe.wait_ge(A.free, g.space(A))
                        s = g.bank(A)
                        accumulate(s, [(wqkv[:, c, P * m:P * m + P], xh(c, n)) for c in range(DC)]).then_inc(A.full, 1)
                for t in range(T + 1):
                    if g.claim(V):
                        pe.wait_ge(V.free, g.space(V))
                    s = g.bank(V)
                    accumulate(s, [(XT[:, c, P * t:P * t + P], wqkv[:, c, 1024:1536]) for c in range(DC)]).then_inc(V.full, 1)
                banks = []
                for k in range(4):
                    if g.claim(V):
                        pe.wait_ge(V.free, g.space(V))
                    s = g.bank(V)
                    banks.append(s)
                for t in range(T):
                    pe.wait_ge(oh_ready.sem, g.nth(oh_ready, t + 1))
                    for k in range(2):
                        for c in range(DC):
                            ins = mm(banks[2 * k + c][:, 0:NSEL], X[:, t, P * c:P * c + P], OH[:, t % 2, k],
                                     start=(t == 0), stop=(t == T - 1))
                            if t == T - 1:
                                ins.then_inc(V.full, 1)
                    if t % 2 == 0:
                        if g.claim(A):
                            pe.wait_ge(A.free, g.space(A))
                        s = g.bank(A)
                    for h in range(2):
                        ins = pe.transpose(s[:, 256 * h + P * (t % 2):256 * h + P * (t % 2) + P],
                                           OH[:, t % 2, 2, P * h:P * h + P], ident[:])
                    if t % 2 == 1:
                        ins.then_inc(A.full, 1)
                        mark("oh", A)
                pe.wait_ge(V.free, g.total(V))
                pe.wait_ge(ld_wheavy.sem, g.nth(ld_wheavy, 64))
                for m in range(PAIRS):
                    if g.claim(A):
                        pe.wait_ge(A.free, g.space(A))
                    s = g.bank(A)
                    accumulate(s[:, 0:NSEL], [(wq_h[:, c, P * m:P * m + P], xsel[:, 0, c]) for c in range(DC)])
                    accumulate(s[:, NSEL:512], [(wkv_h[:, c, P * m:P * m + P], xsel[:, 1, c]) for c in range(DC)]).then_inc(A.full, 1)
                for h in range(2):
                    if g.claim(V):
                        pe.wait_ge(V.free, g.space(V))
                    s = g.bank(V)
                    accumulate(s, [(xsel[:, 1, c, P * h:P * h + P], wkv_h[:, c, 512:1024]) for c in range(DC)]).then_inc(V.full, 1)
                pe.wait_ge(A.free, g.total(A))
                pe.wait_ge(V.free, g.total(V))
                pe.wait_ge(kpad_zero.sem, g.nth(kpad_zero, 2))

                def scores(i):
                    for p in range(PAIRS):
                        if g.claim(SR):
                            pe.wait_ge(SR.free, g.space(SR))
                        s = g.bank(SR)
                        if i < T:
                            mm(s, qT[:, p, P * i:P * i + P], kEO[:, p, :, P * i:P * i + KEYS], start=True, stop=False)
                            ins = mm(s, identb[:], maskb[:, 0 if i == 0 else 2 if i == T - 1 else 1], start=False, stop=True)
                        else:
                            ins = mm(s, hqT[:, p, P * (i - T):P * (i - T) + P], hk(p), start=True, stop=True)
                        ins.then_inc(SR.full, 1)

                def probs(i):
                    pe.wait_ge(e_norm.sem, g.nth(e_norm, i + 1))
                    for p in range(PAIRS):
                        if g.claim(TR):
                            pe.wait_ge(TR.free, g.space(TR))
                        s = g.bank(TR)
                        for e in range(2):
                            for c in range(2):
                                ins = pe.transpose(s[:, P * (2 * e + c):P * (2 * e + c) + P],
                                                   E[:, i % 2, 2 * p + e, P * c:P * c + P], ident[:])
                        ins.then_inc(TR.full, 1)

                def wout(i):
                    pe.wait_ge(TR.free, g.total(TR, PAIRS * (i + 1)))
                    if g.claim(OR):
                        pe.wait_ge(OR.free, g.space(OR))
                    s = g.bank(OR)
                    for p in range(PAIRS):
                        for e in range(2):
                            h = DH * (2 * p + e)
                            for c in range(2):
                                v = V1[:, i + c, h:h + DH] if i < T else hv[:, c, h:h + DH]
                                ins = mm(s[64 * e:64 * e + 64, P * p:P * p + P], v, PT[:, i % 2, p, 2 * e + c],
                                         start=(c == 0), stop=(c == 1))
                    ins.then_inc(OR.full, 1)

                scores(0)
                for i in range(T + 2):
                    if i + 1 < T + 2:
                        scores(i + 1)
                    probs(i)
                    wout(i)
                pe.wait_ge(OR.free, g.total(OR))
                if g.claim(A):
                    pe.wait_ge(A.free, g.space(A))
                s = g.bank(A)
                for h in range(2):
                    ins = accumulate(s[:, D * h:D * h + D], [(hqT[:, p, P * h:P * h + P], wo_h[:, p]) for p in range(PAIRS)])
                ins.then_inc(A.full, 1)
                pe.wait_ge(A.free, g.total(A))
                for u in range(U):
                    if g.claim(V):
                        pe.wait_ge(V.free, g.space(V))
                    s = g.bank(V)
                    for j in range(2):
                        t = 2 * u + j
                        ins = accumulate(s[:, D * j:D * j + D],
                                         [(qT[:, p, P * t:P * t + P], wo_l[:, p]) for p in range(PAIRS)]
                                         + [(OHT[:, h, P * t:P * t + P], ho[:, h]) for h in range(2)])
                    ins.then_inc(V.full, 1)
                mark("l0", V)
                for u in range(U):
                    turn(u, X)
                base = g.job(A)
                for n in range(NH):
                    pe.wait_ge(A.free, g.total(A, base - 2 + 2 * n))
                    for m in range(DC):
                        if g.claim(A):
                            pe.wait_ge(A.free, g.space(A))
                        s = g.bank(A)
                        accumulate(s, [(xw[:, 0, c, P * m:P * m + P], xh(c, n)) for c in range(DC)]).then_inc(A.full, 1)
                pe.wait_ge(A.free, g.total(A))
                pe.wait_ge(mask_ready.sem, g.nth(mask_ready, 1))
                base, slot = g.job(A), [None]

                def silu_scores(k):
                    n, h = k // H, k % H
                    if g.claim(A):
                        pe.wait_ge(A.free, g.space(A))
                    s = g.bank(A)
                    mm(s[0:S2], kblk0[:, h // 8, h % 8], qTx[:, h // 8, NC * n:NC * n + NC], start=True, stop=False)
                    mm(s[0:S2], identb[0:S2, 0:S2], maskN[:, NC * n:NC * n + NC], start=False, stop=True).then_inc(A.full, 1)

                def silu_out(k):
                    h = k % H
                    if k % 8 == 0:
                        if g.claim(V):
                            pe.wait_ge(V.free, g.space(V))
                        slot[0] = g.bank(V)
                    pe.wait_ge(A.free, g.total(A, base + k + 1))
                    j = 32 * ((h % 8) // 2)
                    ins = mm(slot[0][j:j + 32, :], vpad0[:, h], AT[:, k % 4], start=(h % 2 == 0), stop=(h % 2 == 1))
                    if k % 8 == 7:
                        ins.then_inc(V.full, 1)

                for k in range(NH * H + 2):
                    if k < NH * H:
                        silu_scores(k)
                    if k >= 2:
                        silu_out(k - 2)
                pe.wait_ge(V.free, g.total(V))
                for u in range(U):
                    if g.claim(V):
                        pe.wait_ge(V.free, g.space(V))
                    s = g.bank(V)
                    for j in range(2):
                        t = 2 * u + j
                        ins = accumulate(s[:, D * j:D * j + D], [(oTx[:, c, P * t:P * t + P], xw[:, 3, c]) for c in range(DC)])
                    ins.then_inc(V.full, 1)
                for u in range(U):
                    turn(u, X)
                base = g.job(A)
                for n in range(NH):
                    pe.wait_ge(A.free, g.total(A, base - 2 + 2 * n))
                    for m in range(HT):
                        if g.claim(A):
                            pe.wait_ge(A.free, g.space(A))
                        s = g.bank(A)
                        accumulate(s, [(W1T[:, c, P * m:P * m + P], xh(c, n)) for c in range(DC)]).then_inc(A.full, 1)
                        mark("relu", A)
                for u in range(U):
                    if g.claim(V):
                        pe.wait_ge(V.free, g.space(V))
                    s = g.bank(V)
                    pe.wait_ge(sq_ready.sem, g.nth(sq_ready, HT * (u // 2 + 1)))
                    for j in range(2):
                        q = P * (2 * (u % 2) + j)
                        ins = accumulate(s[:, D * j:D * j + D], [(Hb[:, u // 2, k, q:q + P], W2T[:, k]) for k in range(HT)])
                    ins.then_inc(V.full, 1)
                for u in range(U):
                    turn(u, X)
                pe.wait_ge(ld_w1.sem, g.nth(ld_w1, 16 * (H + 2)))
                base = g.job(A)

                def split_T(t):
                    pe.wait_ge(qs_ready.sem, g.nth(qs_ready, t + 1))
                    for w in range(2):
                        for hh in range(2):
                            if g.claim(A):
                                pe.wait_ge(A.free, g.space(A))
                            s = g.bank(A).bitcast(BF16)
                            for h in range(8):
                                ins = pe.transpose(s[0:ROWS, P * h:P * h + P], QS[:, t % 2, w, 8 * hh + h], identb[:])
                            ins.then_inc(A.full, 1)
                    mark("split", A)

                for t in range(T):
                    if t == 0:
                        pe.wait_ge(A.free, g.total(A, base))
                    if g.claim(V):
                        pe.wait_ge(V.free, g.space(V))
                    s = g.bank(V)
                    accumulate(s, [(xt(c, t), wqkv1[:, c, 0:512]) for c in range(DC)]).then_inc(V.full, 1)
                    mark("qk", V)
                    if t % 2 == 1:
                        if g.claim(V):
                            pe.wait_ge(V.free, g.space(V))
                        s = g.bank(V)
                        for j in range(2):
                            ins = accumulate(s[:, D * j:D * j + D], [(xt(c, t - 1 + j), wqkv1[:, c, 512:768]) for c in range(DC)])
                        ins.then_inc(V.full, 1)
                    if t >= 1:
                        split_T(t - 1)
                split_T(T - 1)
                pe.wait_ge(A.free, g.total(A))
                pe.wait_ge(V.free, g.total(V))
                units = [(n, hg, kt) for n in range(NH) for hg in range(HG) for kt in range(T)]

                def self_scores(k):
                    n, hg, kt = units[k]
                    for pr in range(2):
                        if g.claim(S1):
                            pe.wait_ge(S1.free, g.space(S1))
                        s = g.bank(S1)
                        for e in range(2):
                            h = 4 * hg + 2 * pr + e
                            ins = mm(s[:, e], KT[0:ROWS, h, P * kt:P * kt + P], QT[0:ROWS, h, NC * n:NC * n + NC],
                                     start=True, stop=True)
                        ins.then_inc(S1.full, 1)

                def self_out(k):
                    n, hg, kt = units[k]
                    if kt == 0:
                        if g.claim(O1):
                            pe.wait_ge(O1.free, g.space(O1))
                        slot[0] = g.bank(O1)
                    for pr in range(2):
                        pe.wait_ge(S1.free, g.total(S1, 2 * k + pr + 1))
                        for e in range(2):
                            j = 2 * pr + e
                            ins = mm(slot[0][32 * j:32 * j + 32], V32[:, kt, 4 * hg + j], Pb[:, (2 * k + pr) % 4, e],
                                     start=(kt == 0), stop=(kt == T - 1))
                    if kt == T - 1:
                        ins.then_inc(O1.full, 1)

                def spread(i):
                    pe.wait_ge(O1.free, g.total(O1, i + 1))
                    if g.claim(R1):
                        pe.wait_ge(R1.free, g.space(R1))
                    s = g.bank(R1)
                    mm(s, selden[:], OS, start=True, stop=True).then_inc(R1.full, 1)

                self_scores(0)
                for k in range(len(units)):
                    if k + 1 < len(units):
                        self_scores(k + 1)
                    self_out(k)
                    if k % T == 2 and k > T:
                        spread(k // T - 1)
                spread(NH * HG - 1)
                pe.wait_ge(ot_ready.sem, g.nth(ot_ready, NH * HG))
                pe.wait_ge(S1.free, g.total(S1))
                for u in range(U):
                    if g.claim(V):
                        pe.wait_ge(V.free, g.space(V))
                    s = g.bank(V)
                    for j in range(2):
                        t = 2 * u + j
                        ins = accumulate(s[:, D * j:D * j + D], [(OTp[:, k, P * t:P * t + P], projp[:, k]) for k in range(4)])
                    ins.then_inc(V.full, 1)
                mark("self", V)
                for u in range(U):
                    turn(u, X)
                pe.wait_ge(A.free, g.total(A))
                pe.wait_ge(kv1_ready.sem, g.nth(kv1_ready, 1))

                def cross_scores(t):
                    for m in range(DC):
                        for hh in range(2):
                            if g.claim(V):
                                pe.wait_ge(V.free, g.space(V))
                            s = g.bank(V)
                            mm(s[:, 0:4 * S2], xt(m, t), kblk1[:, m, 4 * hh:4 * hh + 4].rearrange("p h k -> p (h k)"),
                               start=True, stop=True).then_inc(V.full, 1)
                    mark("bias", V)

                cross_scores(0)
                pe.wait_ge(ld_wout.sem, g.nth(ld_wout, 16))
                for t in range(T):
                    if t + 1 < T:
                        cross_scores(t + 1)
                    pe.wait_ge(en_ready.sem, g.nth(en_ready, t + 1))
                    for i in range(4):
                        if g.claim(A):
                            pe.wait_ge(A.free, g.space(A))
                        s = g.bank(A)
                        for h in range(4):
                            ins = pe.transpose(s[0:S2, P * h:P * h + P], SC[:, t % 2, 4 * i + h], ident[:])
                        ins.then_inc(A.full, 1)
                    mark("cp", A)
                    pe.wait_ge(A.free, g.total(A))
                    if g.claim(V):
                        pe.wait_ge(V.free, g.space(V))
                    s = g.bank(V)
                    for h in range(H):
                        m, j = h // 8, 32 * ((h % 8) // 2)
                        ins = mm(s[j:j + 32, P * m:P * m + P], vpad1[:, h], PTx[:, h], start=(h % 2 == 0), stop=(h % 2 == 1))
                    ins.then_inc(V.full, 1)
                    if t % 2 == 1:
                        pe.wait_ge(V.free, g.total(V))
                        if g.claim(V):
                            pe.wait_ge(V.free, g.space(V))
                        s = g.bank(V)
                        for j in range(2):
                            ins = accumulate(s[:, D * j:D * j + D],
                                             [(oT1[:, c, P * (t - 1 + j):P * (t + j)], w_out[:, c]) for c in range(DC)])
                        ins.then_inc(V.full, 1)
                mark("cross", V)
                xn[0] += U
                for u in range(U):
                    turn(u, XN)
                pe.wait_ge(ld_w7.sem, g.nth(ld_w7, 16 * 7))
                Wr, Wv, Wo, Ws, W1, W2, W3 = range(7)

                def wide(q, w, src, m):
                    if g.claim(q):
                        pe.wait_ge(q.free, g.space(q))
                    s = g.bank(q)
                    accumulate(s, [(w7[:, w, c, P * m:P * m + P], src(c)) for c in range(DC)]).then_inc(q.full, 1)

                base = g.job(A)
                for n in range(NH):
                    pe.wait_ge(A.free, g.total(A, base - 2 + 2 * n))
                    for m in range(DC):
                        wide(A, Wr, lambda c: xh(c, n), m)
                    mark("sg", A)
                    for m in range(DC):
                        wide(V, Wv, lambda c: xh(c, n), m)
                    mark("g", V)
                    for m in range(DC):
                        wide(A, Ws, lambda c: xh(c, n), m)
                    pe.wait_ge(A.free, g.total(A))
                    for m in range(DC):
                        wide(A, W2, lambda c: ST[:, c], m)
                    mark("ss2", A)
                    pe.wait_ge(V.free, g.total(V))
                    for u in range(2):
                        if g.claim(V):
                            pe.wait_ge(V.free, g.space(V))
                        s = g.bank(V)
                        for j in range(2):
                            q = P * (2 * u + j)
                            ins = accumulate(s[:, D * j:D * j + D], [(G[:, c, q:q + P], w7[:, Wo, c]) for c in range(DC)])
                        ins.then_inc(V.full, 1)
                for u in range(U):
                    turn(u, XN)
                pe.wait_ge(A.free, g.total(A))
                if g.claim(V):
                    pe.wait_ge(V.free, g.space(V))
                s = g.bank(V)
                for t in range(T):
                    ins = accumulate(s[:, 8 * t:8 * t + 7], [(xt(c, t), gatew[:, c, 0:7]) for c in range(DC)])
                ins.then_inc(V.full, 1)
                pe.wait_ge(ld_exp.sem, g.nth(ld_exp, 64))
                sq = NH * HT
                for n in range(NH):
                    for x in range(2):
                        for m in range(HT):
                            if g.claim(A):
                                pe.wait_ge(A.free, g.space(A))
                            s = g.bank(A)
                            accumulate(s, [(Krw[:, x, c, P * m:P * m + P], xh(c, n)) for c in range(DC)]).then_inc(A.full, 1)
                            mark("relu", A)
                    for m in range(DC):
                        wide(V, W1, lambda c: xh(c, n), m)
                    for x in range(2):
                        sq += HT
                        pe.wait_ge(sq_ready.sem, g.nth(sq_ready, sq))
                        for u in range(2):
                            if g.claim(V):
                                pe.wait_ge(V.free, g.space(V))
                            s = g.bank(V)
                            for j in range(2):
                                q = P * (2 * u + j)
                                ins = accumulate(s[:, D * j:D * j + D], [(Hb[:, x, k, q:q + P], Vrw[:, x, k]) for k in range(HT)])
                            ins.then_inc(V.full, 1)
                    pe.wait_ge(tt_ready.sem, g.nth(tt_ready, n + 1))
                    for u in range(2):
                        if g.claim(V):
                            pe.wait_ge(V.free, g.space(V))
                        s = g.bank(V)
                        for j in range(2):
                            q = P * (2 * u + j)
                            ins = accumulate(s[:, D * j:D * j + D], [(TT[:, c, q:q + P], w7[:, W3, c]) for c in range(DC)])
                        ins.then_inc(V.full, 1)
                mark("end", V)
                pe.wait_ge(V.free, g.total(V))
                pe.wait_ge(A.free, g.total(A))

        @block.sync
        def _(sp):
            for dst, src in (
                (xw[:, 0], a["Wq0"].rearrange("(c p) n -> p c n", p=P)),
                (xw[:, 1], a["Wk0"].rearrange("(c p) n -> p c n", p=P)),
                (xw[:, 2], a["Wv0"].rearrange("(c p) n -> p c n", p=P)),
                (xw[:, 3], a["Wo0"].rearrange("(c p) n -> p c n", p=P)),
                (W1T[:], a["w_fcT"].rearrange("(c p) n -> p c n", p=P)),
                (W2T[:], a["w_projT"].rearrange("(c p) n -> p c n", p=P)),
                (R[0:RANK, 0:D], a["v"]),
                (R[0:RANK, 256:256 + HID], a["uT"]),
                (R[0:RANK, 1280:1280 + RANK], a["fbT"]),
                (cols[:, 12:13], a["gate"].partition_broadcast(P)),
                (cols[:, 0:10], a["vecA"]),
                (cols[:, 14:26], a["vecB"]),
                (bvb[:], a["bv"].partition_broadcast(S2)),
                (tinv[:], a["temp"].partition_broadcast(P)),
                (cap[:], a["capital"].partition_broadcast(P)),
                (gatew[:, :, 0:7], a["gates"].rearrange("(c p) e -> p c e", p=P)),
            ):
                sp.dma_start(dst, src).then_inc(ld_once, 16)
            sp.wait_ge(prep_pe, 2)
            sp.wait_ge(prep_dve, PREP)
            with sp.Fori(0, B) as b:
                g = Eng(sp, b)

                def el(ap, pat, **kw):
                    return ap[bass.ds(b, 1)].rearrange(pat, **kw)

                sp.dma_start(X[:], el(a["x"], "a (t p) d -> p (a t) d", p=P)).then_inc(ld_x.sem, 16)
                sp.dma_start(xT0, el(a["xT"], "a (c p) n -> p (a c) n", p=P)).then_inc(ld_xT.sem, 16)
                sp.dma_start(wqkv, a["wqkv_l"].rearrange("(c p) n -> p c n", p=P)).then_inc(ld_wqkv.sem, 16)
                sp.dma_start(ctxT[:], el(a["ctxT"], "a (c p) n -> p (a c) n", p=P)).then_inc(ld_ctx.sem, 16)
                sp.dma_start(ctxV[:], el(a["ctx"], "a k d -> (a k) d")).then_inc(ld_ctx.sem, 16)
                sp.dma_start(wq_h, a["wq_h"].rearrange("(c p) n -> p c n", p=P)).then_inc(ld_wheavy.sem, 16)
                sp.dma_start(wkv_h, a["wkv_h"].rearrange("(c p) n -> p c n", p=P)).then_inc(ld_wheavy.sem, 16)
                sp.dma_start(wo_h, a["wo_h"].rearrange("(c p) n -> p c n", p=P)).then_inc(ld_wheavy.sem, 16)
                sp.dma_start(wo_l, a["wo_l"].rearrange("(c p) n -> p c n", p=P)).then_inc(ld_wheavy.sem, 16)
                sp.wait_ge(V.full, g.total(V, marks["l0"][0]))
                g.plain()
                sp.dma_start(maskI, el(a["maskT"], "a k n -> (a k) n")).then_inc(ld_mask.sem, 16)
                sp.dma_start(wqkv1, a["qkv1T"].rearrange("(c p) n -> p c n", p=P)).then_inc(ld_w1.sem, 16)
                sp.wait_ge(projp_zero.sem, g.nth(projp_zero, 1))
                for h in range(H):
                    sp.dma_start(projp[32 * (h % HG):32 * (h % HG) + DK, h // HG], a["projT"][DK * h:DK * h + DK, :]).then_inc(ld_w1.sem, 16)
                sp.dma_start(projp[DK:DK + 1, 0], a["proj_b"]).then_inc(ld_w1.sem, 16)
                sp.wait_ge(V.full, g.total(V, marks["self"][0]))
                sp.dma_start(w_out, a["w_out"].rearrange("(c p) n -> p c n", p=P)).then_inc(ld_wout.sem, 16)
                for t in range(T):
                    if t >= 2:
                        sp.wait_ge(V.free, g.total(V, marks["bias"][t - 2]))
                    sp.dma_start(biasb[:, t % 2], a["fside"][0, :, P * t:P * t + P, :].rearrange("h q k -> q h k")).then_inc(ld_bias[t % 2].sem, 16)
                    if t == 1:
                        for i, w in enumerate(("Wr", "Wv", "Wo", "Ws", "W1", "W2", "W3")):
                            sp.dma_start(w7[:, i], a[w].rearrange("(c p) n -> p c n", p=P)).then_inc(ld_w7.sem, 16)
                        for x in range(2):
                            sp.dma_start(Krw[:, x], a["K_rwkv"][x].rearrange("(c p) n -> p c n", p=P)).then_inc(ld_exp.sem, 16)
                            sp.dma_start(Vrw[:, x], a["V_rwkv"][x].rearrange("(c p) n -> p c n", p=P)).then_inc(ld_exp.sem, 16)
                for u in range(U):
                    sp.wait_ge(xn_ready.sem, g.nth(xn_ready, 8 * U + u + 1))
                    sp.dma_start(out[bass.ds(b, 1), 256 * u:256 * u + 256, :].rearrange("a (t p) d -> p (a t) d", p=P), X[:, 2 * u:2 * u + 2]).then_inc(st_out.sem, 16)
                sp.wait_ge(st_out.sem, g.nth(st_out, 16 * U))
                g.plain()
                sp.wait_ge(V.free, g.total(V, marks["end"][0]))
                g.plain()


        @block.gpsimd
        def _(pool):
            steps = [0]

            def seq(ins):
                steps[0] += 1
                ins.then_inc(const_ready, 1)
                pool.wait_ge(const_ready, steps[0])

            def sel(ap, op, fill, base, pattern, cm):
                seq(pool.affine_select(out=ap, in_=ap, compare_op=op, fill=fill, base=base, pattern=pattern,
                                       channel_multiplier=cm))
            seq(pool.memset(ident[:], 0.0))
            sel(ident[:], ALU.not_equal, 1.0, 0, [[-1, P]], 1)
            seq(pool.memset(identb[:], 0.0))
            sel(identb[:], ALU.not_equal, 1.0, 0, [[-1, P]], 1)
            seq(pool.memset(ones[:], 1.0))
            seq(pool.memset(above[:], 1.0))
            sel(above[:], ALU.is_gt, 0.0, 0, [[1, P]], -1)
            seq(pool.memset(upto[:], 1.0))
            sel(upto[:], ALU.is_ge, 0.0, 0, [[-1, P]], 1)
            seq(pool.memset(selden[:], 0.0))
            sel(selden[:].rearrange("p (g m) -> p g m", g=4), ALU.not_equal, 1.0, -DK, [[-32, 4], [0, 32]], 1)
            seq(pool.memset(headm[:], 1.0))
            sel(headm[:], ALU.is_ge, 0.0, 0, [[-DK, 8]], 1)
            sel(headm[:], ALU.is_ge, 0.0, DK - 1, [[DK, 8]], -1)
            seq(pool.memset(half01[0:64, 0:1], 1.0))
            seq(pool.memset(half01[64:128, 0:1], 0.0))
            seq(pool.memset(half01[0:64, 1:2], 0.0))
            seq(pool.memset(half01[64:128, 1:2], 1.0))
            seq(pool.memset(nhalf[:], -0.5))
            seq(pool.iota(iota[:], pattern=[[1, NSEL]], base=0, channel_multiplier=0,
                          allow_small_or_imprecise_dtypes=True))
            seq(pool.memset(XT[:, :, 0:PAD], 0.0))
            seq(pool.memset(XT[:, :, PAD + N:NP], 0.0))
            seq(pool.memset(vpad0[:], 0.0))
            seq(pool.memset(maskb[:], 0.0))
            mk = maskb[:].rearrange("p v (e k) -> p v e k", e=2)
            seq(pool.memset(mk[0:64, :, :, 192:256], NEG))
            seq(pool.memset(mk[64:128, :, :, 0:64], NEG))
            seq(pool.memset(mk[:, 0, :, 0:64], NEG))
            seq(pool.memset(mk[:, 2, :, 192:256], NEG))
            assert steps[0] == CONSTS

            with pool.Fori(0, B) as b:
                g = Eng(pool, b)
                norm = [0]

                def rstd_unit():
                    k = norm[0]
                    norm[0] += 1
                    u = k % U
                    pool.wait_ge(ve_ready.sem, g.nth(ve_ready, k + 1))
                    pool.tensor_tensor(rstd[:, 2 * u:2 * u + 2], ve[:, 2 * u:2 * u + 2], nhalf[:, 0:2], ALU.pow).then_inc(rstd_ready.sem, 1)

                for u in range(U):
                    rstd_unit()
                pool.wait_ge(A.full, g.total(A, marks["srow"][0]))
                g.plain()
                pool.memset(kEO[:, :, :, 0:PAD], 0.0).then_inc(kpad_zero.sem, 1)
                pool.memset(kEO[:, :, :, PAD + N:NP], 0.0).then_inc(kpad_zero.sem, 1)
                pool.wait_ge(ss0_ready.sem, g.nth(ss0_ready, 1))
                pool.tensor_tensor(rn0[:], ss0[:], nhalf[:, 0:T], ALU.pow).then_inc(rn0_ready.sem, 1)
                for i in range(T + 2):
                    pool.wait_ge(rs_ready.sem, g.nth(rs_ready, i + 1))
                    pool.tensor_tensor(E[:, i % 2], E[:, i % 2],
                                             rs[:, i % 2, 0:H0].unsqueeze(2).to_broadcast([P, H0, KEYS]), ALU.mult).then_inc(e_norm.sem, 1)
                for u in range(U):
                    rstd_unit()
                pool.wait_ge(V.full, g.total(V, marks["l0"][0]))
                g.plain()
                pool.memset(projp, 0.0).then_inc(projp_zero.sem, 1)
                pool.memset(V32[:, :, :, DK + 1:32], 0.0).then_inc(v_zero.sem, 1)
                pool.memset(V32[:, :, :, DK:DK + 1], 1.0).then_inc(v_zero.sem, 1)
                for u in range(2 * U):
                    rstd_unit()
                for t in range(T):
                    pool.wait_ge(ssq_ready.sem, g.nth(ssq_ready, 2 * (t + 1)))
                    g.plain()
                    pool.tensor_scalar(rqk[:, t], ssq[:, t], 1e-24, None, ALU.max).then_inc(pool_step.sem, 1)
                    pool.wait_ge(pool_step.sem, g.nth(pool_step, t + 1))
                    pool.tensor_tensor(rqk[:, t], rqk[:, t], nhalf[:, 0:2], ALU.pow).then_inc(rqk_ready.sem, 1)
                for u in range(U):
                    rstd_unit()
                pool.wait_ge(V.full, g.total(V, marks["self"][0]))
                g.plain()
                pool.memset(vpad1, 0.0).then_inc(vpad1_zero.sem, 1)

                def shift(t):
                    pool.wait_ge(mx_ready.sem, g.nth(mx_ready, t + 1))
                    pool.tensor_tensor(SC[:, t % 2], SC[:, t % 2],
                                             mx[:, t % 2].unsqueeze(2).to_broadcast([P, H, S2]), ALU.subtract).then_inc(sc_shift.sem, 1)
                shift(0)
                for t in range(T):
                    if t + 1 < T:
                        shift(t + 1)
                    if t % 2 == 1:
                        rstd_unit()
                for u in range(U):
                    rstd_unit()
                for u in range(U):
                    rstd_unit()
                    pool.tensor_tensor(X[:, 2 * u:2 * u + 2], X[:, 2 * u:2 * u + 2], XP[:, 2 * u:2 * u + 2],
                                             ALU.add).then_inc(x2_ready.sem, 1)
                for u in range(U):
                    rstd_unit()
                assert norm[0] == 9 * U, norm[0]

        @block.scalar
        def _(act):
            act.wait_ge(const_ready, CONSTS)
            act.wait_ge(ld_once, 16 * ONCE)
            with act.Fori(0, B) as b:
                g = Eng(act, b)

                def evac_T(u, scale=None, bias=None):
                    act.wait_ge(A.full, g.take(A))
                    s = g.bank(A).rearrange("p (c n) -> p c n", c=DC)
                    for c in range(DC):
                        dst = XT[:, c, PAD + 256 * u:PAD + 256 * u + 256]
                        if scale is None:
                            ins = act.activation(dst, s[:, c], ACT.Copy)
                        else:
                            ins = act.activation(dst, s[:, c], ACT.Identity, scale=cols[:, scale + c:scale + c + 1],
                                                 bias=cols[:, bias + c:bias + c + 1])
                    ins.then_inc(A.free, 1)

                for k in range(2):
                    for n in range(NH):
                        act.wait_ge(A.full, g.take(A))
                        act.activation(Srow[:, k, NC * n:NC * n + NC], g.bank(A), ACT.Copy).then_inc(A.free, 1)
                for u in range(U):
                    evac_T(u, 0, 2)
                for n in range(NH):
                    for m in range(PAIRS):
                        act.wait_ge(A.full, g.take(A))
                        act.activation(qT[:, m, NC * n:NC * n + NC], g.bank(A), ACT.Copy).then_inc(A.free, 1)
                    for m in range(PAIRS):
                        act.wait_ge(A.full, g.take(A))
                        s = g.bank(A)
                        for e in range(2):
                            ins = act.activation(kEO[:, m, e, PAD + NC * n:PAD + NC * n + NC], s, ACT.Copy,
                                                 scale=half01[:, e:e + 1])
                        ins.then_inc(A.free, 1)
                for u in range(U):
                    act.wait_ge(A.full, g.take(A))
                    s = g.bank(A)
                    act.activation(OHT[:, :, 256 * u:256 * u + 256], s.rearrange("p (h n) -> p h n", h=2),
                                   ACT.Copy).then_inc(A.free, 1)
                for m in range(PAIRS):
                    act.wait_ge(A.full, g.take(A))
                    s = g.bank(A)
                    act.activation(hqT[:, m], s[:, 0:NSEL], ACT.Copy)
                    for e in range(2):
                        ins = act.activation(hk(m)[:, e], s[:, NSEL:2 * NSEL], ACT.Copy, scale=half01[:, e:e + 1])
                    ins.then_inc(A.free, 1)

                def window_exp(i):
                    if i >= 2:
                        act.wait_ge(TR.full, g.total(TR, PAIRS * (i - 1)))
                    for p in range(PAIRS):
                        act.wait_ge(SR.full, g.take(SR))
                        s = g.bank(SR).rearrange("p (e k) -> p e k", e=2)
                        act.wait_ge(nm_ready.sem, g.nth(nm_ready, PAIRS * i + p + 1))
                        for e in range(2):
                            h = 2 * p + e
                            ins = act.activation(E[:, i % 2, h], s[:, e], ACT.Exp, scale=DH ** -0.5,
                                                 bias=nm[:, i % 2, h:h + 1], accum_out=sm[:, i % 2, h:h + 1])
                        ins.then_inc(SR.free, 1)

                def window_out(i):
                    act.wait_ge(OR.full, g.take(OR))
                    s = g.bank(OR).rearrange("p (m q) -> p m q", m=PAIRS)
                    dst = qT[:, :, P * i:P * i + P] if i < T else hqT[:, :, P * (i - T):P * (i - T) + P]
                    act.activation(dst, s, ACT.Copy).then_inc(OR.free, 1)

                for i in range(T + 2):
                    window_exp(i)
                    if i >= 1:
                        window_out(i - 1)
                window_out(T + 1)
                act.wait_ge(A.full, g.take(A))
                s = g.bank(A)
                act.activation(ho, s.rearrange("p (s d) -> p s d", s=2), ACT.Copy).then_inc(A.free, 1)
                for u in range(U):
                    evac_T(u)
                for n in range(NH):
                    for m in range(DC):
                        act.wait_ge(A.full, g.take(A))
                        act.activation(qTx[:, m, NC * n:NC * n + NC], g.bank(A), ACT.Identity,
                                       bias=cols[:, 6 + m:7 + m]).then_inc(A.free, 1)
                for k in range(NH * H):
                    act.wait_ge(A.full, g.take(A))
                    s = g.bank(A)
                    act.activation(AT[:, k % 4], s[0:S2], ACT.Silu, scale=DK ** -0.5).then_inc(A.free, 1)
                for u in range(U):
                    evac_T(u)
                for n in range(NH):
                    for m in range(HT):
                        act.wait_ge(A.full, g.take(A))
                        act.activation(Hb[:, n, m], g.bank(A), ACT.Relu).then_inc(A.free, 1)
                for u in range(U):
                    evac_T(u)
                def squares(t):
                    act.wait_ge(V.full, g.total(V, marks["qk"][t]))
                    s = V.bank(marks["qk"][t] - 1)
                    for w in range(2):
                        k = 2 * t + w
                        if k >= 2:
                            act.wait_ge(ssq_ready.sem, g.nth(ssq_ready, k - 1))
                        ins = act.activation(junkf[:, w], s[:, D * w:D * w + D], ACT.Square, accum_out=ssq[:, t, w:w + 1])
                        ins.then_inc(ssq_ready.sem, 1)

                def split_evac(t):
                    for w in range(2):
                        for hh in range(2):
                            act.wait_ge(A.full, g.take(A))
                            s = g.bank(A).bitcast(BF16).rearrange("p (h n) -> p h n", h=8)
                            dst = (QT, KT)[w][0:ROWS, 8 * hh:8 * hh + 8, P * t:P * t + P]
                            act.activation(dst, s[0:ROWS], ACT.Copy).then_inc(A.free, 1)

                for t in range(T):
                    squares(t)
                    if t >= 1:
                        split_evac(t - 1)
                split_evac(T - 1)
                for k in range(2 * NH * HG * T):
                    act.wait_ge(S1.full, g.take(S1))
                    s = g.bank(S1)
                    act.activation(Pb[:, k % 4], s, ACT.Exp).then_inc(S1.free, 1)
                for u in range(U):
                    evac_T(u)
                def cross_exp(t):
                    act.wait_ge(sc_shift.sem, g.nth(sc_shift, t + 1))
                    act.activation(SC[:, t % 2], SC[:, t % 2], ACT.Exp, scale=DK ** -0.5).then_inc(sc_exp.sem, 1)

                cross_exp(0)
                for t in range(T):
                    if t + 1 < T:
                        cross_exp(t + 1)
                    for i in range(4):
                        act.wait_ge(A.full, g.take(A))
                        s = g.bank(A)
                        act.activation(PTx[:, 4 * i:4 * i + 4], s[0:S2].rearrange("p (h q) -> p h q", h=4),
                                       ACT.Copy).then_inc(A.free, 1)
                for u in range(U):
                    evac_T(u, 18, 20)
                for n in range(NH):
                    if n == 1:
                        act.wait_ge(V.free, g.total(V, marks["g"][0]))
                    for m in range(DC):
                        act.wait_ge(A.full, g.take(A))
                        act.activation(SG[:, m], g.bank(A), ACT.Sigmoid).then_inc(A.free, 1)
                    for m in range(DC):
                        act.wait_ge(A.full, g.take(A))
                        act.activation(ST[:, m], g.bank(A), ACT.Copy).then_inc(A.free, 1)
                    for m in range(DC):
                        act.wait_ge(A.full, g.take(A))
                        act.activation(SS2[:, m, NC * n:NC * n + NC], g.bank(A), ACT.Sigmoid).then_inc(A.free, 1)
                for u in range(U):
                    evac_T(u, 22, 24)
                act.wait_ge(lg_ready.sem, g.nth(lg_ready, 1))
                act.activation(lg[:, :, 0:4], lg[:, :, 0:4], ACT.Sigmoid).then_inc(conf_ready.sem, 1)
                for n in range(NH):
                    for x in range(2):
                        for m in range(HT):
                            act.wait_ge(A.full, g.take(A))
                            act.activation(Hb[:, x, m], g.bank(A), ACT.Relu).then_inc(A.free, 1)

        @block.vector
        def _(dve):
            dve.wait_ge(const_ready, CONSTS)
            dve.wait_ge(ld_once, 16 * ONCE)
            tt, ts, stt = dve.tensor_tensor, dve.tensor_scalar, dve.scalar_tensor_tensor
            steps = [0]

            def seq(ins):
                steps[0] += 1
                ins.then_inc(prep_dve, 1)
                dve.wait_ge(prep_dve, steps[0])
            absW1, absW2 = r(4096, DC, HID), r(6144, HT, D)
            sc1, hi1, lo1, t1 = r(8192, HID), r(9216, HID), r(10240, HID), r(11264, DC, HID)
            sc2, hi2, lo2, t2 = r(13312, D), r(13568, D), r(13824, D), r(14336, HT, D)
            for k in range(2):
                for c in range(DC):
                    last = ts(rtb[:, k, c], ones[:], cols[:, 14 + 2 * k + c:15 + 2 * k + c], None, ALU.mult)
            seq(last)
            seq(stt(absW1, W1T[:], -1.0, W1T[:], ALU.mult, ALU.max))
            seq(stt(absW2, W2T[:], -1.0, W2T[:], ALU.mult, ALU.max))
            dve.wait_ge(prep_pe, 1)
            seq(ts(R[0:RANK, 1536:1536 + D], bk[3][0:RANK, 0:D], cols[0:RANK, 12:13], None, ALU.mult))
            for n in range(NH):
                last = ts(sc1[:, NC * n:NC * n + NC], bk[n], 1.0 / D, 1e-5, ALU.mult, ALU.max)
            ts(sc2, bk[2][:, 0:D], 1.0 / HID, 1e-5, ALU.mult, ALU.max).then_inc(prep_dve, 1)
            steps[0] += 1
            dve.wait_ge(prep_dve, steps[0])
            for (w, sc, hi, lo, tmp, parts) in ((W1T, sc1, hi1, lo1, t1, DC), (W2T, sc2, hi2, lo2, t2, HT)):
                n = sc.shape[-1]

                def over(v):
                    return v.unsqueeze(1).to_broadcast([P, parts, n])
                ts(hi, sc, 0.5, None, ALU.mult)
                seq(ts(lo, sc, -0.5, None, ALU.mult))
                tt(tmp, w[:], over(hi), ALU.is_gt)
                seq(tt(w[:], w[:], over(lo), ALU.is_lt))
                seq(tt(tmp, tmp, w[:], ALU.subtract))
                seq(tt(w[:], tmp, over(sc), ALU.mult))
            dve.wait_ge(prep_pe, 2)
            for c in range(DC):
                for n in range(NH):
                    last = tt(W1T[:, c, NC * n:NC * n + NC], W1T[:, c, NC * n:NC * n + NC], bk[4 + 2 * c + n], ALU.add)
            seq(last)
            seq(dve.reciprocal(tinv[:], tinv[:]))
            seq(ts(tinv[:], tinv[:], 1.0 / DK, None, ALU.mult))
            seq(stt(negc[:], tinv[:], -1.0, tinv[:], ALU.mult, ALU.min))
            assert steps[0] == PREP

            with dve.Fori(0, B) as b:
                g = Eng(dve, b)
                unit = [0]

                def stats(u, q=None, to=X):
                    x = X[:, 2 * u:2 * u + 2]
                    if q is not None:
                        dve.wait_ge(q.full, g.take(q))
                        s = g.bank(q).rearrange("p (t d) -> p t d", t=2)
                        tt(to[:, 2 * u:2 * u + 2], s, x, ALU.add).then_inc(q.free, 1)
                        dve.wait_ge(q.free, g.total(q))
                    for j in range(2):
                        ins = dve.bn_stats(st[:, 2 * u + j], to[:, 2 * u + j])
                    ins.then_inc(dve_step.sem, g.step())
                    dve.wait_ge(dve_step.sem, g.steps())
                    g.plain()
                    for j in range(2):
                        ins = dve.bn_aggr(mv[:, 2 * u + j], st[:, 2 * u + j])
                    ins.then_inc(dve_step.sem, g.step())
                    dve.wait_ge(dve_step.sem, g.steps())
                    ts(ve[:, 2 * u:2 * u + 2], mv[:, 2 * u:2 * u + 2, 1], EPS, None, ALU.add).then_inc(ve_ready.sem, 1)

                def normalise(u, dst, src=X):
                    unit[0] += 1
                    dve.wait_ge(rstd_ready.sem, g.nth(rstd_ready, unit[0]))
                    for t in (2 * u, 2 * u + 1):
                        ins = ts(dst[:, t], src[:, t], mv[:, t, 0:1], rstd[:, t:t + 1], ALU.subtract, ALU.mult)
                    ins.then_inc(xn_ready.sem, 1)

                def norm_all(dst, q=None):
                    for u in range(U):
                        stats(u, q)
                        if u >= 1:
                            normalise(u - 1, dst)
                    normalise(U - 1, dst)

                dve.wait_ge(ld_x.sem, g.nth(ld_x, 16))
                norm_all(XN)
                dve.wait_ge(ld_ctx.sem, g.nth(ld_ctx, 32))
                dve.wait_ge(V.full, g.take(V))
                s = g.bank(V)
                for m in range(DC):
                    stt(kblk0[:, m], s[:, P * m:P * m + S2].unsqueeze(1).to_broadcast([P, 8, S2]), cols[:, 8 + m:9 + m],
                        headm[:].unsqueeze(2).to_broadcast([P, 8, S2]), ALU.add, ALU.mult)
                v = s[0:S2, 256:512].rearrange("p (i e d) -> p i e d", e=2, d=DK)
                bv = bvb[:].rearrange("p (i e d) -> p i e d", e=2, d=DK)
                vp = vpad0[:].rearrange("p (i e) c -> p i e c", e=2)
                for e in range(2):
                    ins = tt(vp[:, :, e, DK * e:DK * e + DK], v[:, :, e], bv[:, :, e], ALU.add)
                ins.then_inc(V.free, 1)
                dve.wait_ge(A.free, g.total(A, marks["srow"][0]))
                scraps = []

                def scrap(n):
                    if len(scraps) >= 8:
                        dve.wait_ge(dve_step.sem, g.nth(dve_step, scraps[-8]))
                    scraps.append(g.k + 1)
                    return junk[:, (len(scraps) - 1) % 8, 0:n]

                for t in range(T):
                    dve.tensor_tensor_reduce(scrap(D), X[:, t], X[:, t], 1.0, 0.0, ALU.mult, ALU.add, ss0[:, t:t + 1]).then_inc(dve_step.sem, g.step())
                dve.wait_ge(dve_step.sem, g.steps())
                ts(ss0[:], ss0[:], 1e-24, None, ALU.max).then_inc(ss0_ready.sem, 1)
                for k in range(2):
                    for t in range(T):
                        dve.tensor_tensor_reduce(scrap(P), Srow[:, k, P * t:P * t + P], ident[:], 1.0, 0.0,
                                                         ALU.mult, ALU.add, scol[:, k, t:t + 1]).then_inc(dve_step.sem, g.step())
                dve.memset(cnt[:], 0.0).then_inc(dve_step.sem, g.step())
                dve.wait_ge(dve_step.sem, g.steps())
                for k in range(2):
                    for t in range(T):
                        me = scol[:, k, t:t + 1]
                        for i, (lo, hi, op) in enumerate(((0, P * t, ALU.is_gt), (P * t + P, N, ALU.is_ge))):
                            if hi > lo:
                                ts(scrap(hi - lo), Srow[:, k, lo:hi], me, 0.0, op, ALU.add,
                                           accum_out=cnt[:, k, t, i:i + 1]).then_inc(dve_step.sem, g.step())
                        d = Srow[:, k, P * t:P * t + P]
                        stt(scrap(P), d, me, above[:], ALU.is_ge, ALU.mult, accum_out=cnt[:, k, t, 2:3]).then_inc(dve_step.sem, g.step())
                        stt(scrap(P), d, me, upto[:], ALU.is_gt, ALU.mult, accum_out=cnt[:, k, t, 3:4]).then_inc(dve_step.sem, g.step())
                dve.wait_ge(dve_step.sem, g.steps())
                dve.tensor_reduce(rank[:], cnt[:], AXX, ALU.add).then_inc(dve_step.sem, g.step())
                for t in range(T + 1):
                    dve.wait_ge(V.full, g.take(V))
                    dve.tensor_copy(V1[:, t], g.bank(V)).then_inc(V.free, 1)
                dve.wait_ge(dve_step.sem, g.steps())
                dve.wait_ge(rn0_ready.sem, g.nth(rn0_ready, 1))
                for t in range(T):
                    if t >= 2:
                        dve.wait_ge(A.full, g.total(A, marks["oh"][t // 2 - 1]))
                    for k in range(2):
                        ts(OH[:, t % 2, k], iota[:], rank[:, k, t:t + 1], rn0[:, t:t + 1], ALU.is_equal, ALU.mult)
                    ts(OH[:, t % 2, 2], iota[:], rank[:, 0, t:t + 1], None, ALU.is_equal).then_inc(oh_ready.sem, 1)
                for k in range(2):
                    for c in range(DC):
                        dve.wait_ge(V.full, g.take(V))
                        ts(xsel[:, k, c], g.bank(V)[:, 0:NSEL], cols[:, 4 + c:5 + c], float(D) ** 0.5, ALU.mult,
                           ALU.mult).then_inc(V.free, 1)
                for h in range(2):
                    dve.wait_ge(V.full, g.take(V))
                    dve.tensor_copy(hv[:, h], g.bank(V)).then_inc(V.free, 1)

                def window_max(i):
                    for p in range(PAIRS):
                        k = PAIRS * i + p
                        dve.wait_ge(SR.full, g.total(SR, k + 1))
                        s = SR.bank(k).rearrange("p (e k) -> p e k", e=2)
                        dve.tensor_reduce(mx[:, i % 2, 2 * p:2 * p + 2], s, AXX, ALU.max).then_inc(dve_step.sem, g.step())
                        dve.wait_ge(dve_step.sem, g.steps())
                        ts(nm[:, i % 2, 2 * p:2 * p + 2], mx[:, i % 2, 2 * p:2 * p + 2], -(DH ** -0.5), None,
                                 ALU.mult).then_inc(nm_ready.sem, 1)

                def window_sum(i):
                    dve.wait_ge(SR.free, g.total(SR, PAIRS * (i + 1)))
                    dve.reciprocal(rs[:, i % 2, 0:H0], sm[:, i % 2, 0:H0]).then_inc(rs_ready.sem, 1)

                window_max(0)
                window_sum(0)
                for i in range(T + 2):
                    if i + 1 < T + 2:
                        window_max(i + 1)
                    if i >= 2:
                        dve.wait_ge(OR.full, g.total(OR, i - 1))
                    for p in range(PAIRS):
                        dve.wait_ge(TR.full, g.take(TR))
                        dve.tensor_copy(PT[:, i % 2, p].rearrange("p a q -> p (a q)"), g.bank(TR)).then_inc(TR.free, 1)
                    if i + 1 < T + 2:
                        window_sum(i + 1)
                norm_all(X, V)
                dve.wait_ge(ld_mask.sem, g.nth(ld_mask, 16))
                ts(maskN, maskI, 0.0, NEG, ALU.is_equal, ALU.mult).then_inc(mask_ready.sem, 1)
                for n in range(NH):
                    for m in range(DC):
                        dve.wait_ge(V.full, g.take(V))
                        dve.tensor_copy(oTx[:, m, NC * n:NC * n + NC], g.bank(V)).then_inc(V.free, 1)
                norm_all(X, V)

                sq = [0]

                def square(buf):
                    for m in range(HT):
                        dve.wait_ge(A.free, g.total(A, marks["relu"][sq[0]]))
                        sq[0] += 1
                        tt(Hb[:, buf, m], Hb[:, buf, m], Hb[:, buf, m], ALU.mult).then_inc(sq_ready.sem, 1)

                square(0)
                square(1)
                norm_all(X, V)
                dve.wait_ge(v_zero.sem, g.nth(v_zero, 2))
                for i in range(2):
                    dve.tensor_copy(QS[:, i, 0, :, 96:97], negc[:].unsqueeze(2))
                    ins = dve.memset(QS[:, i, 1, :, 96:97], 1.0)
                ins.then_inc(dve_step.sem, g.step())
                qkv = qkn.rearrange("p (w h d) -> p w h d", w=2, h=H)
                r1v = r1.rearrange("p (w h d) -> p w h d", w=2, h=H)

                def part(i, w, s, step=1, n=1):
                    v = QS[:, i, w, :, 0:96].rearrange("p h (s d) -> p h s d", d=DK)
                    return v[:, :, s] if n == 1 else v[:, :, s:s + step * (n - 1) + 1:step]

                def rep(v, n):
                    return v.unsqueeze(2).to_broadcast([P, H, n, DK])

                for t in range(T):
                    i = t % 2
                    dve.wait_ge(rqk_ready.sem, g.nth(rqk_ready, t + 1))
                    dve.wait_ge(V.full, g.take(V))
                    s = g.bank(V)
                    stt(qkv[:, 0], s[:, 0:D].rearrange("p (h d) -> p h d", h=H), rqk[:, t, 0:1],
                        tinv[:].unsqueeze(2).to_broadcast([P, H, DK]), ALU.mult, ALU.mult)
                    ts(qkn[:, D:2 * D], s[:, D:2 * D], rqk[:, t, 1:2], None, ALU.mult).then_inc(V.free, 1)
                    dve.wait_ge(V.free, g.total(V))
                    if t % 2 == 1:
                        dve.wait_ge(V.full, g.take(V))
                        s = g.bank(V).rearrange("p (t h d) -> p t h d", t=2, h=H)
                        for j in range(2):
                            ins = dve.tensor_copy(V32[:, t - 1 + j, :, 0:DK], s[:, j])
                        ins.then_inc(V.free, 1)
                    if t >= 2:
                        dve.wait_ge(A.full, g.total(A, marks["split"][t - 2]))
                    dve.tensor_copy(part(i, 0, 1, 2, 3), rep(qkv[:, 0], 3))
                    dve.tensor_copy(part(i, 1, 0, 1, 3), rep(qkv[:, 1], 3)).then_inc(dve_step.sem, g.step())
                    dve.wait_ge(dve_step.sem, g.steps())
                    tt(r1v[:, 0], qkv[:, 0], part(i, 0, 1), ALU.subtract)
                    tt(r1v[:, 1], qkv[:, 1], part(i, 1, 1), ALU.subtract).then_inc(dve_step.sem, g.step())
                    dve.wait_ge(dve_step.sem, g.steps())
                    dve.tensor_copy(part(i, 0, 2, 2, 2), rep(r1v[:, 0], 2))
                    dve.tensor_copy(part(i, 1, 3, 1, 2), rep(r1v[:, 1], 2)).then_inc(dve_step.sem, g.step())
                    dve.wait_ge(dve_step.sem, g.steps())
                    tt(part(i, 0, 0), r1v[:, 0], part(i, 0, 4), ALU.subtract)
                    tt(part(i, 1, 5), r1v[:, 1], part(i, 1, 4), ALU.subtract).then_inc(qs_ready.sem, 1)
                for n in range(NH):
                    for hg in range(HG):
                        if n or hg:
                            dve.wait_ge(ot_ready.sem, g.nth(ot_ready, HG * n + hg))
                        dve.wait_ge(O1.full, g.take(O1))
                        dve.tensor_copy(OS, g.bank(O1)).then_inc(O1.free, 1)
                        dve.wait_ge(R1.full, g.take(R1))
                        dve.reciprocal(RC, g.bank(R1)).then_inc(R1.free, 1)
                        dve.wait_ge(R1.free, g.total(R1))
                        tt(OTp[:, hg, NC * n:NC * n + NC], OS, RC, ALU.mult).then_inc(ot_ready.sem, 1)
                norm_all(X, V)
                dve.wait_ge(vpad1_zero.sem, g.nth(vpad1_zero, 1))
                for m in range(DC):
                    tt(kblk1[:, m], ctxT[:, m].unsqueeze(1).to_broadcast([P, 8, S2]),
                       headm[:].unsqueeze(2).to_broadcast([P, 8, S2]), ALU.mult)
                v = ctxV[:].rearrange("p (i e d) -> p i e d", e=2, d=DK)
                vp = vpad1.rearrange("p (i e) c -> p i e c", e=2)
                for e in range(2):
                    ins = dve.tensor_copy(vp[:, :, e, DK * e:DK * e + DK], v[:, :, e])
                ins.then_inc(kv1_ready.sem, 1)

                def cross_max(t):
                    dve.wait_ge(ld_bias[t % 2].sem, g.nth(ld_bias[t % 2], 16 * (t // 2 + 1)))
                    if t >= 2:
                        dve.wait_ge(A.full, g.total(A, marks["cp"][t - 2]))
                    for i in range(4):
                        dve.wait_ge(V.full, g.take(V))
                        s = g.bank(V)[:, 0:4 * S2].rearrange("p (h k) -> p h k", h=4)
                        tt(SC[:, t % 2, 4 * i:4 * i + 4], s, biasb[:, t % 2, 4 * i:4 * i + 4], ALU.add).then_inc(V.free, 1)
                    dve.wait_ge(V.free, g.total(V))
                    dve.tensor_reduce(mx[:, t % 2], SC[:, t % 2], AXX, ALU.max).then_inc(mx_ready.sem, 1)

                def cross_norm(t):
                    dve.wait_ge(sc_exp.sem, g.nth(sc_exp, t + 1))
                    dve.tensor_reduce(sm[:, t % 2], SC[:, t % 2], AXX, ALU.add).then_inc(dve_step.sem, g.step())
                    dve.wait_ge(dve_step.sem, g.steps())
                    dve.reciprocal(rs[:, t % 2], sm[:, t % 2]).then_inc(dve_step.sem, g.step())
                    dve.wait_ge(dve_step.sem, g.steps())
                    tt(SC[:, t % 2], SC[:, t % 2], rs[:, t % 2].unsqueeze(2).to_broadcast([P, H, S2]), ALU.mult).then_inc(en_ready.sem, 1)

                cross_max(0)
                for t in range(T):
                    if t + 1 < T:
                        cross_max(t + 1)
                    cross_norm(t)
                    dve.wait_ge(V.full, g.take(V))
                    s = g.bank(V)
                    dve.tensor_copy(oT1[:, :, P * t:P * t + P], s[:, 0:2 * P].rearrange("p (m q) -> p m q", m=DC)).then_inc(V.free, 1)
                    if t % 2 == 1:
                        stats(t // 2, V)
                        normalise(t // 2, X)
                norm_all(XN)
                for n in range(NH):
                    dve.wait_ge(A.free, g.total(A, marks["sg"][n]))
                    for m in range(DC):
                        dve.wait_ge(V.full, g.take(V))
                        tt(G[:, m], g.bank(V), SG[:, m], ALU.mult).then_inc(V.free, 1)
                    for u in range(2 * n, 2 * n + 2):
                        stats(u, V, XP)
                        normalise(u, XN, XP)
                dve.wait_ge(V.full, g.take(V))
                s = g.bank(V)[:, 0:8 * T].rearrange("p (t c) -> p t c", c=8)
                dve.tensor_copy(lg[:, :, 0:7], s[:, :, 0:7]).then_inc(V.free, 1)
                dve.wait_ge(V.free, g.total(V))
                dve.memset(lg[:, :, 7:8], 0.0).then_inc(lg_ready.sem, 1)
                dve.wait_ge(conf_ready.sem, g.nth(conf_ready, 1))
                conf = lg[:, :, 0:3]

                def step(ins):
                    ins.then_inc(dve_step.sem, g.step())
                    dve.wait_ge(dve_step.sem, g.steps())
                step(tt(bids[:], conf, cap[:].unsqueeze(1).to_broadcast([P, T, 3]), ALU.mult))
                step(tt(bids[:], bids[:], lg[:, :, 3:4].to_broadcast([P, T, 3]), ALU.mult))
                step(tt(bids[:], bids[:], lg[:, :, 4:7], ALU.add))
                b0, b1, b2 = (bids[:, :, i:i + 1] for i in range(3))
                tt(win[:, :, 0:1], b0, b1, ALU.is_ge)
                tt(cc[:, :, 0:1], b0, b2, ALU.is_ge)
                tt(win[:, :, 1:2], b1, b0, ALU.is_gt)
                tt(cc[:, :, 1:2], b1, b2, ALU.is_ge)
                tt(win[:, :, 2:3], b2, b0, ALU.is_gt)
                tt(cc[:, :, 2:3], b2, b1, ALU.is_gt)
                step(ts(dd[:], conf, 1e-6, None, ALU.add))
                tt(win[:], win[:], cc[:], ALU.mult)
                step(dve.reciprocal(dd[:], dd[:]))
                step(tt(dd[:], dd[:], conf, ALU.mult))
                step(tt(cc[:], dd[:], win[:], ALU.mult))
                for n in range(NH):
                    square(0)
                    square(1)
                    dve.wait_ge(A.free, g.total(A, marks["ss2"][1]))
                    for m in range(DC):
                        dve.wait_ge(V.full, g.take(V))
                        tt(TT[:, m], g.bank(V), SS2[:, m, NC * n:NC * n + NC], ALU.mult).then_inc(V.free, 1)
                    dve.wait_ge(V.free, g.total(V))
                    dve.memset(dd[:, 0:1, 0:1], 0.0).then_inc(tt_ready.sem, 1)
                    for x in range(3):
                        for u in range(2 * n, 2 * n + 2):
                            dve.wait_ge(V.full, g.take(V))
                            s = g.bank(V).rearrange("p (t d) -> p t d", t=2)
                            if x == 0:
                                dve.wait_ge(x2_ready.sem, g.nth(x2_ready, u + 1))
                            else:
                                dve.wait_ge(V.free, g.total(V, g.job(V) - 2))
                            for j in range(2):
                                t = 2 * u + j
                                ins = stt(X[:, t], s[:, j], cc[:, t, x:x + 1], X[:, t], ALU.mult, ALU.add)
                            ins.then_inc(V.free, 1)
                            if x == 2:
                                dve.wait_ge(V.free, g.total(V))
                                stats(u)
                                normalise(u, X)


def kernel(**inputs):
    import numpy as _np
    import concourse.bacc as _bacc
    from concourse import mybir as _mybir
    from concourse.bass_utils import run_bass_kernel_spmd as _run

    def a(name):
        return _np.asarray(inputs[name])

    def columns(*names):
        return _np.concatenate([a(n).reshape(DC, P).T for n in names], 1)

    laid = {
        "x": a("x"), "xT": a("x").transpose(0, 2, 1), "ctx": a("ctx_1024"), "ctxT": a("ctx_1024").transpose(0, 2, 1),
        "fside": a("fside_1x16xSxS2_0"), "maskT": a("mask_Bx1xSxS2_ik1")[:, 0].transpose(0, 2, 1),
        "wq_h": a("L0_attn_wq_h"), "wkv_h": a("L0_attn_wkv_h"), "wo_h": a("L0_attn_wo_h"),
        "wqkv_l": a("L0_attn_wqkv_l"), "wo_l": a("L0_attn_wo_l"),
        "vecA": columns("L0_attn_ln_g", "L0_attn_ln_b", "L0_attn_gamma_h", "L0_xattn_bq", "L0_xattn_bk"),
        "vecB": columns("L0_attn_rt_q", "L0_attn_rt_kv", "L1_ffn_ln1_w", "L1_ffn_ln1_b", "L1_ffn_ln2_w", "L1_ffn_ln2_b"),
        "gates": _np.concatenate([a("L1_ffn_conf_rwkv").T, a("L1_ffn_conf_trans")[:, None], a("L1_ffn_w_diff")[:, None],
                                  a("L1_ffn_W_aff")], 1),
        "Wq0": a("L0_xattn_Wq").T, "Wk0": a("L0_xattn_Wk").T, 
        "Wv0": a("L0_xattn_Wv").T, "bv": a("L0_xattn_bv"), "Wo0": a("L0_xattn_Wo").T,
        "fbT": a("L0_ffn_fast_b").T, "w_fcT": a("L0_ffn_w_fc").T, "w_projT": a("L0_ffn_w_proj").T,
        "uT": a("L0_ffn_u").T, "v": a("L0_ffn_v"), "gate": a("L0_ffn_gate").reshape(1),
        "qkv1T": a("L1_attn_qkv_w").T, "temp": a("L1_attn_temperature").reshape(H), "projT": a("L1_attn_proj_w").T,
        "proj_b": a("L1_attn_proj_b").reshape(1, D), "w_out": a("L1_xattn_w_out"),
        "capital": a("L1_ffn_capital_shares"), "Wr": a("L1_ffn_Wr"), "Wv": a("L1_ffn_Wv"),
        "Wo": a("L1_ffn_Wo"), "Ws": a("L1_ffn_Ws"), "K_rwkv": a("L1_ffn_K_rwkv"), "V_rwkv": a("L1_ffn_V_rwkv"),
        "W1": a("L1_ffn_W1"), "W2": a("L1_ffn_W2"), "W3": a("L1_ffn_W3"),
    }
    nc = _bacc.Bacc("TRN2", target_bir_lowering=False, num_devices=1)
    arrays, aps = {}, {}
    for name, x in laid.items():
        x = _np.ascontiguousarray(x)
        arrays[f"in_{name}_dram"] = x
        aps[name] = nc.dram_tensor(f"in_{name}_dram", x.shape, _mybir.dt.from_np(x.dtype), kind="ExternalInput").ap()
    out = nc.dram_tensor("out_0_dram", (B, N, D), F32, kind="ExternalOutput").ap()
    decoder(nc, aps, out)
    res = _run(nc, [arrays], core_ids=[0])
    return res.results[0]["out_0_dram"]
```

```python
from contextlib import ExitStack

import concourse.bass as bass
from concourse import mybir

F32 = mybir.dt.float32
BF16 = mybir.dt.bfloat16
I32 = mybir.dt.int32
ALU = mybir.AluOpType
ACT = mybir.ActivationFunctionType
AXX = mybir.AxisListType.X

P = 128
B, N, D = 2, 1024, 256
T = N // P
U = T // 2
DC = D // P
NC = 512
NH = N // NC
PAD = 64
NP = N + 2 * PAD
H0, DH = 8, 64
PAIRS = H0 * DH // P
NSEL = 256
KEYS = 256
H, DK = 16, 16
WIN = 64
S2 = 77
HG = 4
HID = 1024
HT = HID // P
RANK = 16
COMB = 6
ROWS = COMB * DK + 1
WP = PAIRS * (T + 2)
LEAD = 6
POOL_PREP = 2
EXPERT = ("Wr", "Wv", "Wo", "Ws", "W1", "W2", "W3")
NEG = -1.0e30
EPS = 1.0e-5

CONSTS = 24
ONCE = 14
PREP = 15
DVE_STEPS = 238
JOBS = {"V": 117, "A": 217, "SR": 40, "TR": 40, "OR": 10, "S1": 128, "O1": 8, "R1": 8}

SIGNALS = {
    "ld_x0": 16, "ld_x1": 16, "ld_x2": 16, "ld_x3": 16, "ld_xT": 16,
    "ld_wqkv": 16, "ld_ctx": 32, "ld_wheavy": 64, "ld_mask": 16, "ld_w1": 16 * (H + 2),
    "ld_wout": 16, "ld_bias0": 48, "ld_bias1": 48, "ld_bias2": 32, "ld_w7": 16 * 7, "ld_exp": 64,
    "st_out": 16 * U,
    "ve_ready": 9 * U,
    "rstd_ready": 9 * U,
    "xn_ready": 9 * U,
    "kpad_zero": 2,
    "ss0_ready": 1, "rn0_ready": 1,
    "oh_ready": T,
    "nm_ready": PAIRS * (T + 2),
    "rs_ready": WP,
    "e_norm": WP,
    "projp_zero": 1, "v_zero": 2, "vpad1_zero": 1,
    "mask_ready": 1, "masked": NH * H,
    "sq_ready": NH * HT * 3,
    "ssq_ready": 2 * T, "rqk_ready": T,
    "qs_ready": T,
    "ot_ready": NH * HG,
    "kv1_ready": 1,
    "sums_ready": T, "mx_ready": T, "sc_shift": T, "sc_exp": T, "en_ready": T,
    "lg_ready": 1, "conf_ready": 1,
    "x2_ready": U,
    "tt_ready": NH,
    "dve_step": DVE_STEPS, "pool_step": T,
}


class Signal:

    def __init__(self, sem, per):
        self.sem, self.per = sem, per


class Ring:

    def __init__(self, name, banks, full, free, jobs):
        self.name, self.banks, self.full, self.free, self.jobs = name, banks, full, free, jobs

    def bank(self, k):
        return self.banks[k % len(self.banks)]


def decoder(nc, a, out):
    ctx = ExitStack()
    with ctx:
        def sb(name, cols, dt=F32, parts=P):
            return ctx.enter_context(nc.sbuf_tensor(name, [parts] + list(cols), dt))

        def sem(name):
            return ctx.enter_context(nc.semaphore(name))

        X = sb("X", [T, D])
        XN = sb("XN", [T, D])
        XT = sb("XT", [DC, NP])
        W1T = sb("W1T", [DC, HID])
        W2T = sb("W2T", [HT, D])
        xw = sb("xw", [4, DC, D])
        kblk0 = sb("kblk0", [DC, 8, S2])
        vpad0 = sb("vpad0", [H, 32], parts=S2)
        ctxT = sb("ctxT", [DC, S2])
        ctxV = sb("ctxV", [D], parts=S2)
        ident = sb("ident", [P])
        identb = sb("identb", [P], BF16)
        ones = sb("ones", [P])
        iota = sb("iota", [NSEL])
        above = sb("above", [P])
        upto = sb("upto", [P])
        unseen = sb("unseen", [2, WIN], BF16)
        selden = sb("selden", [P])
        headm = sb("headm", [8])
        half01 = sb("half01", [2])
        rtb = sb("rtb", [2, DC, P])
        cols = sb("cols", [32])
        tinv = sb("tinv", [H])
        negc = sb("negc", [H])
        cap = sb("cap", [3])
        gatew = sb("gatew", [DC, 8])
        bvb = sb("bvb", [D], parts=S2)
        nhalf = sb("nhalf", [32])
        st = sb("st", [T, 6])
        mv = sb("mv", [T, 2])
        ve = sb("ve", [T])
        rstd = sb("rstd", [T])
        scol = sb("scol", [2, T])
        cnt = sb("cnt", [2, T, 4])
        rank = sb("rank", [2, T])
        ss0 = sb("ss0", [T])
        rn0 = sb("rn0", [T])
        mx = sb("mx", [2, H])
        nm = sb("nm", [2, H0])
        sm = sb("sm", [2, H])
        rs = sb("rs", [2, H])
        ssq = sb("ssq", [T, 2])
        rqk = sb("rqk", [T, 2])
        lg = sb("lg", [T, 8])
        bids = sb("bids", [T, 3])
        win = sb("win", [T, 3])
        cc = sb("cc", [T, 3])
        dd = sb("dd", [T, 3])
        R = sb("R", [34816])

        def r(off, *dims, parts=P):
            n = 1
            for d in dims:
                n *= d
            v = R[0:parts, off:off + n]
            if len(dims) == 2:
                return v.rearrange("p (a b) -> p a b", a=dims[0])
            if len(dims) == 3:
                return v.rearrange("p (a b c) -> p a b c", a=dims[0], b=dims[1])
            if len(dims) == 4:
                return v.rearrange("p (a b c d) -> p a b c d", a=dims[0], b=dims[1], c=dims[2])
            return v

        wqkv = r(0, DC, 3 * 512)
        E = r(0, 2, H0, KEYS)
        Srow = r(4096, 2, N)
        OH = r(4096, 4, 3, NSEL)
        junk = R[:, 26624:30720].bitcast(BF16).rearrange("p (i n) -> p i n", i=8)
        PT = r(4096, 2, PAIRS, 4, P)
        wo_l = r(8192, PAIRS, D)
        wq_h = r(9216, DC, 512)
        wkv_h = r(10240, DC, 1024)
        wo_h = r(12288, PAIRS, D)
        qT = r(13312, PAIRS, N)
        kEO = r(17408, PAIRS, 2, NP)
        xT0 = r(17408, DC, N)
        V1 = r(26624, T + 1, 512)
        hqT = r(31232, PAIRS, NSEL)
        hv = r(32256, 2, 512)
        ho = r(33280, 2, D)
        xsel = r(33792, 2, DC, NSEL)
        OHT = XN[:, :, :].rearrange("p (s t) d -> p s (t d)", s=2)

        def hk(p):
            return XT[:, p // 2, PAD + 512 * (p % 2):PAD + 512 * (p % 2) + 512].rearrange("p (e k) -> p e k", e=2)

        maskI = R[0:S2, 28672:29696].bitcast(I32)
        maskN = r(29696, N, parts=S2)
        qTx = r(8192, DC, N)
        oTx = r(10240, DC, N)
        AT = r(12288, 6, NC, parts=S2)
        Hb = r(0, 2, HT, NC)
        KT = R[:, 0:8192].bitcast(BF16).rearrange("p (h n) -> p h n", h=H)
        QT = R[:, 8192:16384].bitcast(BF16).rearrange("p (h n) -> p h n", h=H)
        V32 = r(16384, T, H, 32)
        Pb = r(20480, 4, 2, NC)
        QS = R[:, 20480:20480 + 776 * 4].bitcast(BF16).rearrange("p (r s h c) -> p r s h c", r=2, s=2, h=H)
        qkn = r(23584, 512)
        OTp = r(24576, 4, N)
        OS = r(28672, NC)
        RC = r(29184, NC)
        r1 = r(29696, 512)
        r2 = r(30208, 512)
        junkf = r(30720, 2, D)
        wqkv1 = r(31232, DC, 3 * D)
        projp = r(32768, 4, D)
        kblk1 = r(0, DC, 8, S2)
        vpad1 = r(1232, H, 32, parts=S2)
        w_out = r(1744, DC, D)
        biasb = r(8192, 3, H, S2)
        SC = r(2256, 3, H, S2)
        PTx = r(11888, 2, H, P, parts=S2)
        oT1 = r(28672, DC, N)
        XP = r(28672, T, D)
        w7 = r(16384, 7, DC, D)
        Krw = r(20480, 2, DC, HID)
        Vrw = r(24576, 2, HT, D)
        SG = r(8192, DC, NC)
        G = r(9216, DC, NC)
        ST = r(10240, DC, NC)
        TT = r(11264, DC, NC)
        SS2 = r(12288, DC, N)

        PS = ctx.enter_context(nc.psum_tensor("PS", [P, 8, 512], F32))
        bk = [PS[:, i, :] for i in range(8)]

        def ring(name, banks, jobs):
            f, g = sem(f"{name}_full"), sem(f"{name}_free")
            return Ring(name, banks, f, g, jobs)

        A = ring("act_bank", [bk[i] for i in (0, 1, 2, 3)], JOBS["A"])
        V = ring("dve_bank", [bk[i] for i in (4, 5, 6, 7)], JOBS["V"])
        SR = ring("score_bank", [bk[i] for i in (4, 5, 6, 7)], JOBS["SR"])
        TR = ring("probT_bank", [bk[i] for i in (1, 2)], JOBS["TR"])
        OR = ring("wout_bank", [bk[i] for i in (0, 3)], JOBS["OR"])
        S1 = ring("self_bank", [PS[:, 2 * i:2 * i + 2, :] for i in range(3)], JOBS["S1"])
        O1 = ring("sout_bank", [bk[6]], JOBS["O1"])
        R1 = ring("den_bank", [bk[7]], JOBS["R1"])

        def signal(name):
            return Signal(sem(name), SIGNALS[name])

        ld_xT = signal("ld_xT")
        ld_wqkv = signal("ld_wqkv")
        ld_ctx = signal("ld_ctx")
        ld_wheavy = signal("ld_wheavy")
        ld_mask = signal("ld_mask")
        ld_w1 = signal("ld_w1")
        ld_wout = signal("ld_wout")
        ld_w7 = signal("ld_w7")
        ld_exp = signal("ld_exp")
        st_out = signal("st_out")
        ve_ready = signal("ve_ready")
        rstd_ready = signal("rstd_ready")
        xn_ready = signal("xn_ready")
        kpad_zero = signal("kpad_zero")
        ss0_ready = signal("ss0_ready")
        rn0_ready = signal("rn0_ready")
        oh_ready = signal("oh_ready")
        nm_ready = signal("nm_ready")
        rs_ready = signal("rs_ready")
        e_norm = signal("e_norm")
        projp_zero = signal("projp_zero")
        v_zero = signal("v_zero")
        vpad1_zero = signal("vpad1_zero")
        mask_ready = signal("mask_ready")
        masked = signal("masked")
        sq_ready = signal("sq_ready")
        ssq_ready = signal("ssq_ready")
        rqk_ready = signal("rqk_ready")
        qs_ready = signal("qs_ready")
        ot_ready = signal("ot_ready")
        kv1_ready = signal("kv1_ready")
        sums_ready = signal("sums_ready")
        mx_ready = signal("mx_ready")
        sc_shift = signal("sc_shift")
        sc_exp = signal("sc_exp")
        en_ready = signal("en_ready")
        lg_ready = signal("lg_ready")
        conf_ready = signal("conf_ready")
        x2_ready = signal("x2_ready")
        tt_ready = signal("tt_ready")
        dve_step = signal("dve_step")
        pool_step = signal("pool_step")
        ld_x = [signal(f"ld_x{u}") for u in range(U)]
        ld_bias = [signal("ld_bias0"), signal("ld_bias1"), signal("ld_bias2")]
        marks = {}
        carrier = {x: sem(f"carrier_{x}") for x in ("DVE", "Pool", "SP")}
        const_ready = sem("const_ready")
        ld_once = sem("ld_once")
        ld_fc, ld_proj = sem("ld_fc"), sem("ld_proj")
        prep_dve = sem("prep_dve")
        prep_pe = sem("prep_pe")
        prep_pool = sem("prep_pool")


        block = ctx.enter_context(nc.Block())

        class Eng:

            def __init__(self, e, b):
                self.e, self.b, self.n, self.k = e, b, {}, 0

            def nth(self, sig, k):
                return self.b * sig.per + k

            def step(self):
                self.k += 1
                return 1

            def steps(self):
                return self.b * dve_step.per + self.k

            def plain(self):
                self.e.sem_inc(carrier[self.e.engine.name], 1)

            def job(self, q):
                return self.n.get(q.name, 0)

            def bank(self, q):
                return q.bank(self.job(q) - 1)

            def take(self, q):
                self.n[q.name] = self.job(q) + 1
                return self.b * q.jobs + self.job(q)

            def claim(self, q):
                self.n[q.name] = self.job(q) + 1
                return self.job(q) > len(q.banks)

            def space(self, q):
                return self.b * q.jobs + self.job(q) - len(q.banks)

            def total(self, q, k=None):
                return self.b * q.jobs + (self.job(q) if k is None else k)

        @block.tensor
        def _(pe):
            mm = pe.matmul
            pe.wait_ge(const_ready, CONSTS)
            pe.wait_ge(prep_dve, 1)
            absW1, absW2 = r(4096, DC, HID), r(6144, HT, D)
            for n in range(NH):
                for c in range(DC):
                    mm(bk[n], ones[:], absW1[:, c, NC * n:NC * n + NC], start=(c == 0), stop=(c == DC - 1))
            pe.wait_ge(prep_dve, 2)
            for k in range(HT):
                mm(bk[2][:, 0:D], ones[:], absW2[:, k], start=(k == 0), stop=(k == HT - 1))
            pe.wait_ge(ld_once, 16 * ONCE)
            mm(bk[3][0:RANK, 0:D], R[0:RANK, 1280:1280 + RANK], R[0:RANK, 0:D], start=True, stop=True).then_inc(prep_pe, 1)
            pe.wait_ge(prep_dve, 4)
            for c in range(DC):
                for n in range(NH):
                    last = mm(bk[4 + 2 * c + n], R[0:RANK, 1536 + P * c:1536 + P * c + P],
                              R[0:RANK, 256 + NC * n:256 + NC * n + NC], start=True, stop=True)
            last.then_inc(prep_pe, 1)
            pe.wait_ge(prep_dve, 5)
            with pe.Fori(0, B) as b:
                g = Eng(pe, b)
                xn = [0]

                def accumulate(dst, pairs, first=True, last=True):
                    for i, (lhsT, rhs) in enumerate(pairs):
                        ins = mm(dst, lhsT, rhs, start=(first and i == 0), stop=(last and i == len(pairs) - 1))
                    return ins

                def turn(u, src, k=None):
                    xn[0] += 1
                    pe.wait_ge(xn_ready.sem, g.nth(xn_ready, k or xn[0]))
                    if g.claim(A):
                        pe.wait_ge(A.free, g.space(A))
                    s = g.bank(A)
                    for c in range(DC):
                        for j in range(2):
                            ins = pe.transpose(s[:, 256 * c + P * j:256 * c + P * j + P],
                                               src[:, 2 * u + j, P * c:P * c + P], ident[:])
                    ins.then_inc(A.full, 1)

                def xt(c, t):
                    return XT[:, c, PAD + P * t:PAD + P * t + P]

                def xh(c, n):
                    return XT[:, c, PAD + NC * n:PAD + NC * n + NC]

                def mark(name, q):
                    marks.setdefault(name, []).append(g.job(q))

                pe.wait_ge(ld_xT.sem, g.nth(ld_xT, 16))
                for k in range(2):
                    for n in range(NH):
                        if g.claim(A):
                            pe.wait_ge(A.free, g.space(A))
                        s = g.bank(A)
                        accumulate(s, [(rtb[:, k, c], xT0[:, c, NC * n:NC * n + NC]) for c in range(DC)]).then_inc(A.full, 1)
                mark("srow", A)
                pe.wait_ge(prep_dve, PREP)
                pe.wait_ge(prep_pool, POOL_PREP)
                pe.wait_ge(ld_ctx.sem, g.nth(ld_ctx, 32))
                if g.claim(V):
                    pe.wait_ge(V.free, g.space(V))
                s = g.bank(V)
                for m in range(DC):
                    accumulate(s[:, P * m:P * m + S2], [(xw[:, 1, c, P * m:P * m + P], ctxT[:, c]) for c in range(DC)])
                accumulate(s[0:S2, 256:512], [(ctxT[:, c], xw[:, 2, c]) for c in range(DC)]).then_inc(V.full, 1)
                turn(0, XN)
                turn(1, XN)
                half = g.job(A)
                pe.wait_ge(ld_wqkv.sem, g.nth(ld_wqkv, 16))
                for n in range(NH):
                    pe.wait_ge(A.free, g.total(A, half))
                    for m in range(2 * PAIRS):
                        if n == 0 and m == 2 * PAIRS - 2:
                            turn(2, XN)
                            turn(3, XN)
                            half = g.job(A)
                        if g.claim(A):
                            pe.wait_ge(A.free, g.space(A))
                        s = g.bank(A)
                        accumulate(s, [(wqkv[:, c, P * m:P * m + P], xh(c, n)) for c in range(DC)]).then_inc(A.full, 1)
                for t in range(T + 1):
                    if g.claim(V):
                        pe.wait_ge(V.free, g.space(V))
                    s = g.bank(V)
                    accumulate(s, [(XT[:, c, P * t:P * t + P], wqkv[:, c, 1024:1536]) for c in range(DC)]).then_inc(V.full, 1)
                banks = []
                for k in range(4):
                    if g.claim(V):
                        pe.wait_ge(V.free, g.space(V))
                    s = g.bank(V)
                    banks.append(s)
                for t in range(T):
                    pe.wait_ge(oh_ready.sem, g.nth(oh_ready, t + 1))
                    for k in range(2):
                        for c in range(DC):
                            ins = mm(banks[2 * k + c][:, 0:NSEL], X[:, t, P * c:P * c + P], OH[:, t % 4, k],
                                     start=(t == 0), stop=(t == T - 1))
                            if t == T - 1:
                                ins.then_inc(V.full, 1)
                    if t % 2 == 0:
                        if g.claim(A):
                            pe.wait_ge(A.free, g.space(A))
                        s = g.bank(A)
                    for h in range(2):
                        ins = pe.transpose(s[:, 256 * h + P * (t % 2):256 * h + P * (t % 2) + P],
                                           OH[:, t % 4, 2, P * h:P * h + P], ident[:])
                    if t % 2 == 1:
                        ins.then_inc(A.full, 1)
                        mark("oh", A)
                pe.wait_ge(V.free, g.total(V))
                pe.wait_ge(ld_wheavy.sem, g.nth(ld_wheavy, 64))
                for m in range(PAIRS):
                    if g.claim(A):
                        pe.wait_ge(A.free, g.space(A))
                    s = g.bank(A)
                    accumulate(s[:, 0:NSEL], [(wq_h[:, c, P * m:P * m + P], xsel[:, 0, c]) for c in range(DC)])
                    accumulate(s[:, NSEL:512], [(wkv_h[:, c, P * m:P * m + P], xsel[:, 1, c]) for c in range(DC)]).then_inc(A.full, 1)
                for h in range(2):
                    if g.claim(V):
                        pe.wait_ge(V.free, g.space(V))
                    s = g.bank(V)
                    accumulate(s, [(xsel[:, 1, c, P * h:P * h + P], wkv_h[:, c, 512:1024]) for c in range(DC)]).then_inc(V.full, 1)
                pe.wait_ge(A.free, g.total(A))
                pe.wait_ge(V.free, g.total(V))
                pe.wait_ge(kpad_zero.sem, g.nth(kpad_zero, 2))

                def scores(k):
                    i, p = k // PAIRS, k % PAIRS
                    if g.claim(SR):
                        pe.wait_ge(SR.free, g.space(SR))
                    s = g.bank(SR)
                    if i < T:
                        s = s.rearrange("p (e k) -> p e k", e=2)
                        for w in range(2):
                            q = P * i + WIN * w
                            lo = WIN if (i, w) == (0, 0) else WIN * w
                            hi = KEYS - WIN if (i, w) == (T - 1, 1) else WIN * w + 3 * WIN
                            rows = s[WIN * w:WIN * w + WIN]
                            mm(rows[:, :, lo:hi], qT[:, p, q:q + WIN], kEO[:, p, :, P * i + lo:P * i + hi], start=True, stop=True)
                            for k in range(0, KEYS, WIN):
                                if not lo <= k < hi:
                                    ins = mm(rows[:, :, k:k + WIN], identb[:, 0:WIN], unseen[:], start=True, stop=True)
                    else:
                        ins = mm(s, hqT[:, p, P * (i - T):P * (i - T) + P], hk(p), start=True, stop=True)
                    ins.then_inc(SR.full, 1)

                def probs(k):
                    i, p = k // PAIRS, k % PAIRS
                    pe.wait_ge(e_norm.sem, g.nth(e_norm, k + 1))
                    if g.claim(TR):
                        pe.wait_ge(TR.free, g.space(TR))
                    s = g.bank(TR)
                    for e in range(2):
                        for c in range(2):
                            ins = pe.transpose(s[:, P * (2 * e + c):P * (2 * e + c) + P],
                                               E[:, i % 2, 2 * p + e, P * c:P * c + P], ident[:])
                    ins.then_inc(TR.full, 1)

                def wout(k):
                    i, p = k // PAIRS, k % PAIRS
                    if p == 0:
                        if g.claim(OR):
                            pe.wait_ge(OR.free, g.space(OR))
                        wbank[0] = g.bank(OR)
                    pe.wait_ge(TR.free, g.total(TR, k + 1))
                    for e in range(2):
                        h = DH * (2 * p + e)
                        for c in range(2):
                            v = V1[:, i + c, h:h + DH] if i < T else hv[:, c, h:h + DH]
                            ins = mm(wbank[0][64 * e:64 * e + 64, P * p:P * p + P], v, PT[:, i % 2, p, 2 * e + c],
                                     start=(c == 0), stop=(c == 1))
                    if p == PAIRS - 1:
                        ins.then_inc(OR.full, 1)

                wbank = [None]
                for k in range(-LEAD, WP + 1):
                    if k + LEAD < WP:
                        scores(k + LEAD)
                    if 0 <= k < WP:
                        probs(k)
                    if k >= 1:
                        wout(k - 1)
                pe.wait_ge(OR.free, g.total(OR))
                if g.claim(A):
                    pe.wait_ge(A.free, g.space(A))
                s = g.bank(A)
                for h in range(2):
                    ins = accumulate(s[:, D * h:D * h + D], [(hqT[:, p, P * h:P * h + P], wo_h[:, p]) for p in range(PAIRS)])
                ins.then_inc(A.full, 1)
                pe.wait_ge(A.free, g.total(A))
                for u in range(U):
                    if u == U - 1:
                        turn(0, X)
                    if g.claim(V):
                        pe.wait_ge(V.free, g.space(V))
                    s = g.bank(V)
                    for j in range(2):
                        if (u, j) == (U - 1, 1):
                            turn(1, X)
                        t = 2 * u + j
                        ins = accumulate(s[:, D * j:D * j + D],
                                         [(qT[:, p, P * t:P * t + P], wo_l[:, p]) for p in range(PAIRS)]
                                         + [(OHT[:, h, P * t:P * t + P], ho[:, h]) for h in range(2)])
                    ins.then_inc(V.full, 1)
                mark("l0", V)
                half = g.job(A)
                for n in range(NH):
                    pe.wait_ge(A.free, g.total(A, half))
                    for m in range(DC):
                        if n == 0 and m == DC - 1:
                            turn(2, X)
                            turn(3, X)
                            half = g.job(A)
                        if g.claim(A):
                            pe.wait_ge(A.free, g.space(A))
                        s = g.bank(A)
                        accumulate(s, [(xw[:, 0, c, P * m:P * m + P], xh(c, n)) for c in range(DC)]).then_inc(A.full, 1)
                    mark("q", A)
                pe.wait_ge(A.free, g.total(A, marks["q"][0]))
                slot = [None]
                mark("silu", A)

                def silu_scores(k):
                    n, h = k // H, k % H
                    if k == H:
                        pe.wait_ge(A.free, g.total(A, marks["q"][1]))
                    if g.claim(A):
                        pe.wait_ge(A.free, g.space(A))
                    s = g.bank(A)
                    mm(s[0:S2], kblk0[:, h // 8, h % 8], qTx[:, h // 8, NC * n:NC * n + NC], start=True, stop=True).then_inc(A.full, 1)

                def silu_out(k):
                    h = k % H
                    if k % 8 == 0:
                        if g.claim(V):
                            pe.wait_ge(V.free, g.space(V))
                        slot[0] = g.bank(V)
                    pe.wait_ge(masked.sem, g.nth(masked, k + 1))
                    j = 32 * ((h % 8) // 2)
                    ins = mm(slot[0][j:j + 32, :], vpad0[:, h], AT[:, k % 6], start=(h % 2 == 0), stop=(h % 2 == 1))
                    if k % 8 == 7:
                        ins.then_inc(V.full, 1)

                for k in range(NH * H + 4):
                    if k < NH * H:
                        silu_scores(k)
                    if k >= 4:
                        silu_out(k - 4)
                pe.wait_ge(V.free, g.total(V))
                for u in range(U):
                    if g.claim(V):
                        pe.wait_ge(V.free, g.space(V))
                    s = g.bank(V)
                    for j in range(2):
                        t = 2 * u + j
                        ins = accumulate(s[:, D * j:D * j + D], [(oTx[:, c, P * t:P * t + P], xw[:, 3, c]) for c in range(DC)])
                    ins.then_inc(V.full, 1)
                turn(0, X)
                turn(1, X)
                half = g.job(A)
                for n in range(NH):
                    pe.wait_ge(A.free, g.total(A, half))
                    for m in range(HT):
                        if n == 0 and m == HT - 2:
                            turn(2, X)
                            turn(3, X)
                            half = g.job(A)
                        if g.claim(A):
                            pe.wait_ge(A.free, g.space(A))
                        s = g.bank(A)
                        accumulate(s, [(W1T[:, c, P * m:P * m + P], xh(c, n)) for c in range(DC)]).then_inc(A.full, 1)
                        mark("relu", A)
                turned = []
                for u in range(U):
                    if u == U - 1:
                        turn(0, X)
                        turned.append(g.job(A))
                    if g.claim(V):
                        pe.wait_ge(V.free, g.space(V))
                    s = g.bank(V)
                    pe.wait_ge(sq_ready.sem, g.nth(sq_ready, HT * (u // 2 + 1)))
                    for j in range(2):
                        q = P * (2 * (u % 2) + j)
                        ins = accumulate(s[:, D * j:D * j + D], [(Hb[:, u // 2, k, q:q + P], W2T[:, k]) for k in range(HT)])
                    ins.then_inc(V.full, 1)
                turn(1, X)
                turned.append(g.job(A))
                pe.wait_ge(ld_w1.sem, g.nth(ld_w1, 16 * (H + 2)))

                def split_T(t):
                    pe.wait_ge(qs_ready.sem, g.nth(qs_ready, t + 1))
                    for w in range(2):
                        for hh in range(2):
                            if g.claim(A):
                                pe.wait_ge(A.free, g.space(A))
                            s = g.bank(A).bitcast(BF16)
                            for h in range(8):
                                ins = pe.transpose(s[0:ROWS, P * h:P * h + P], QS[:, t % 2, w, 8 * hh + h], identb[:])
                            ins.then_inc(A.full, 1)
                    mark("split", A)

                def project_T(t):
                    if t in (2, 4):
                        turn(t // 2 + 1, X)
                        turned.append(g.job(A))
                    if t % 2 == 0:
                        pe.wait_ge(A.free, g.total(A, turned[t // 2]))
                    if g.claim(V):
                        pe.wait_ge(V.free, g.space(V))
                    s = g.bank(V)
                    accumulate(s, [(xt(c, t), wqkv1[:, c, 0:512]) for c in range(DC)]).then_inc(V.full, 1)
                    mark("qk", V)
                    if t % 2 == 1:
                        if g.claim(V):
                            pe.wait_ge(V.free, g.space(V))
                        s = g.bank(V)
                        for j in range(2):
                            ins = accumulate(s[:, D * j:D * j + D], [(xt(c, t - 1 + j), wqkv1[:, c, 512:768]) for c in range(DC)])
                        ins.then_inc(V.full, 1)

                for t in range(T + 2):
                    if t < T:
                        project_T(t)
                    if t >= 2:
                        split_T(t - 2)
                pe.wait_ge(A.free, g.total(A))
                pe.wait_ge(V.free, g.total(V))
                units = [(n, hg, kt) for n in range(NH) for hg in range(HG) for kt in range(T)]

                def self_scores(k):
                    n, hg, kt = units[k]
                    for pr in range(2):
                        if g.claim(S1):
                            pe.wait_ge(S1.free, g.space(S1))
                        s = g.bank(S1)
                        for e in range(2):
                            h = 4 * hg + 2 * pr + e
                            ins = mm(s[:, e], KT[0:ROWS, h, P * kt:P * kt + P], QT[0:ROWS, h, NC * n:NC * n + NC],
                                     start=True, stop=True)
                        ins.then_inc(S1.full, 1)

                def self_out(k):
                    n, hg, kt = units[k]
                    if kt == 0:
                        if g.claim(O1):
                            pe.wait_ge(O1.free, g.space(O1))
                        slot[0] = g.bank(O1)
                    for pr in range(2):
                        pe.wait_ge(S1.free, g.total(S1, 2 * k + pr + 1))
                        for e in range(2):
                            j = 2 * pr + e
                            ins = mm(slot[0][32 * j:32 * j + 32], V32[:, kt, 4 * hg + j], Pb[:, (2 * k + pr) % 4, e],
                                     start=(kt == 0), stop=(kt == T - 1))
                    if kt == T - 1:
                        ins.then_inc(O1.full, 1)

                def spread(i):
                    pe.wait_ge(O1.free, g.total(O1, i + 1))
                    if g.claim(R1):
                        pe.wait_ge(R1.free, g.space(R1))
                    s = g.bank(R1)
                    mm(s, selden[:], OS, start=True, stop=True).then_inc(R1.full, 1)

                self_scores(0)
                for k in range(len(units)):
                    if k + 1 < len(units):
                        self_scores(k + 1)
                    self_out(k)
                    if k % T == 2 and k > T:
                        spread(k // T - 1)
                pe.wait_ge(S1.free, g.total(S1))
                for u in range(U):
                    if u == 1:
                        spread(NH * HG - 1)
                    pe.wait_ge(ot_ready.sem, g.nth(ot_ready, HG if u < 2 else NH * HG))
                    if u == U - 1:
                        turn(0, X)
                    if g.claim(V):
                        pe.wait_ge(V.free, g.space(V))
                    s = g.bank(V)
                    for j in range(2):
                        t = 2 * u + j
                        ins = accumulate(s[:, D * j:D * j + D], [(OTp[:, k, P * t:P * t + P], projp[:, k]) for k in range(4)])
                    ins.then_inc(V.full, 1)
                mark("self", V)
                turn(1, X)
                pe.wait_ge(A.free, g.total(A))
                pe.wait_ge(kv1_ready.sem, g.nth(kv1_ready, 1))

                def cross_scores(t):
                    for m in range(DC):
                        for hh in range(2):
                            if g.claim(V):
                                pe.wait_ge(V.free, g.space(V))
                            s = g.bank(V)
                            mm(s[:, 0:4 * S2], xt(m, t), kblk1[:, m, 4 * hh:4 * hh + 4].rearrange("p h k -> p (h k)"),
                               start=True, stop=True).then_inc(V.full, 1)
                    mark("bias", V)

                def cross_probs(t):
                    pe.wait_ge(en_ready.sem, g.nth(en_ready, t + 1))
                    for i in range(4):
                        if g.claim(A):
                            pe.wait_ge(A.free, g.space(A))
                        s = g.bank(A)
                        for h in range(4):
                            ins = pe.transpose(s[0:S2, P * h:P * h + P], SC[:, t % 3, 4 * i + h], ident[:])
                        ins.then_inc(A.full, 1)
                    mark("cp", A)

                def cross_values(t):
                    pe.wait_ge(A.free, g.total(A, marks["cp"][t]))
                    if g.claim(V):
                        pe.wait_ge(V.free, g.space(V))
                    s = g.bank(V)
                    for h in range(H):
                        m, j = h // 8, 32 * ((h % 8) // 2)
                        ins = mm(s[j:j + 32, P * m:P * m + P], vpad1[:, h], PTx[:, t % 2, h], start=(h % 2 == 0), stop=(h % 2 == 1))
                    ins.then_inc(V.full, 1)
                    mark("cv", V)

                def cross_out(u):
                    pe.wait_ge(V.free, g.total(V, marks["cv"][2 * u + 1]))
                    if g.claim(V):
                        pe.wait_ge(V.free, g.space(V))
                    s = g.bank(V)
                    for j in range(2):
                        t = 2 * u + j
                        ins = accumulate(s[:, D * j:D * j + D], [(oT1[:, c, P * t:P * t + P], w_out[:, c]) for c in range(DC)])
                    ins.then_inc(V.full, 1)

                Wr, Wv, Wo, Ws, W1, W2, W3 = range(7)

                def wide(q, w, src, m):
                    if g.claim(q):
                        pe.wait_ge(q.free, g.space(q))
                    s = g.bank(q)
                    accumulate(s, [(w7[:, w, c, P * m:P * m + P], src(c)) for c in range(DC)]).then_inc(q.full, 1)

                halves = [0, 0]

                def turn_half(n, normed=None):
                    for u in (2 * n, 2 * n + 1):
                        turn(u, XN, None if normed is None else normed + 2 * u + 2)
                    halves[n] = g.job(A)

                def gate_state(n):
                    if n == 0:
                        turn_half(0, norms)
                        pe.wait_ge(ld_w7.sem, g.nth(ld_w7, 16 * 7))
                    pe.wait_ge(A.free, g.total(A, halves[n]))
                    for m in range(DC):
                        wide(A, Wr, lambda c: xh(c, n), m)
                    mark("sg", A)
                    for m in range(DC):
                        wide(A, Ws, lambda c: xh(c, n), m)
                    mark("st", A)

                cross_scores(0)
                turn(2, X)
                turn(3, X)
                cross_scores(1)
                pe.wait_ge(A.free, g.total(A))
                pe.wait_ge(ld_wout.sem, g.nth(ld_wout, 16))
                for t in range(T):
                    if t >= 1:
                        cross_values(t - 1)
                    if t + 2 < T:
                        cross_scores(t + 2)
                    cross_probs(t)
                    if t >= 2 and t % 2 == 0:
                        cross_out(t // 2 - 1)
                norms = xn[0]
                xn[0] += U
                gate_state(0)
                cross_values(T - 1)
                cross_out(U - 1)
                mark("cross", V)
                for n in range(NH):
                    if n == 1:
                        gate_state(1)
                    for m in range(DC):
                        wide(V, Wv, lambda c: xh(c, n), m)
                    mark("g", V)
                    pe.wait_ge(A.free, g.total(A, marks["st"][n]))
                    for m in range(DC):
                        wide(A, W2, lambda c: ST[:, c], m)
                    mark("ss2", A)
                    if n == 0:
                        turn_half(1, norms)
                    else:
                        turn_half(0)
                    pe.wait_ge(V.free, g.total(V, marks["g"][n]))
                    for u in range(2):
                        if g.claim(V):
                            pe.wait_ge(V.free, g.space(V))
                        s = g.bank(V)
                        for j in range(2):
                            q = P * (2 * u + j)
                            ins = accumulate(s[:, D * j:D * j + D], [(G[:, c, q:q + P], w7[:, Wo, c]) for c in range(DC)])
                        ins.then_inc(V.full, 1)
                pe.wait_ge(ld_exp.sem, g.nth(ld_exp, 64))
                sq = NH * HT
                pe.wait_ge(A.free, g.total(A, halves[0]))
                for n in range(NH):
                    for x in range(2):
                        if n == 0 and x == 1:
                            turn_half(1)
                        for m in range(HT):
                            if g.claim(A):
                                pe.wait_ge(A.free, g.space(A))
                            s = g.bank(A)
                            accumulate(s, [(Krw[:, x, c, P * m:P * m + P], xh(c, n)) for c in range(DC)]).then_inc(A.full, 1)
                            mark("relu", A)
                    if n == 0:
                        pe.wait_ge(A.free, g.total(A, halves[1]))
                        if g.claim(V):
                            pe.wait_ge(V.free, g.space(V))
                        s = g.bank(V)
                        for t in range(T):
                            ins = accumulate(s[:, 8 * t:8 * t + 7], [(xt(c, t), gatew[:, c, 0:7]) for c in range(DC)])
                        ins.then_inc(V.full, 1)
                    for m in range(DC):
                        wide(V, W1, lambda c: xh(c, n), m)
                    for x in range(2):
                        sq += HT
                        pe.wait_ge(sq_ready.sem, g.nth(sq_ready, sq))
                        for u in range(2):
                            if g.claim(V):
                                pe.wait_ge(V.free, g.space(V))
                            s = g.bank(V)
                            for j in range(2):
                                q = P * (2 * u + j)
                                ins = accumulate(s[:, D * j:D * j + D], [(Hb[:, x, k, q:q + P], Vrw[:, x, k]) for k in range(HT)])
                            ins.then_inc(V.full, 1)
                        mark("expert", V)
                    pe.wait_ge(tt_ready.sem, g.nth(tt_ready, n + 1))
                    for u in range(2):
                        if g.claim(V):
                            pe.wait_ge(V.free, g.space(V))
                        s = g.bank(V)
                        for j in range(2):
                            q = P * (2 * u + j)
                            ins = accumulate(s[:, D * j:D * j + D], [(TT[:, c, q:q + P], w7[:, W3, c]) for c in range(DC)])
                        ins.then_inc(V.full, 1)
                mark("end", V)
                pe.wait_ge(V.free, g.total(V))
                pe.wait_ge(A.free, g.total(A))

        @block.sync
        def _(sp):
            sp.dma_start(W1T[:], a["w_fcT"].rearrange("(c p) n -> p c n", p=P)).then_inc(ld_fc, 16)
            sp.dma_start(W2T[:], a["w_projT"].rearrange("(c p) n -> p c n", p=P)).then_inc(ld_proj, 16)
            for dst, src in (
                (R[0:RANK, 0:D], a["v"]),
                (R[0:RANK, 256:256 + HID], a["uT"]),
                (R[0:RANK, 1280:1280 + RANK], a["fbT"]),
                (cols[:, 12:13], a["gate"].partition_broadcast(P)),
                (cols[:, 0:10], a["vecA"]),
                (cols[:, 14:26], a["vecB"]),
                (bvb[:], a["bv"].partition_broadcast(S2)),
                (tinv[:], a["temp"].partition_broadcast(P)),
                (cap[:], a["capital"].partition_broadcast(P)),
                (gatew[:, :, 0:7], a["gates"].rearrange("(c p) e -> p c e", p=P)),
                (xw[:, 0], a["Wq0"].rearrange("(c p) n -> p c n", p=P)),
                (xw[:, 1], a["Wk0"].rearrange("(c p) n -> p c n", p=P)),
                (xw[:, 2], a["Wv0"].rearrange("(c p) n -> p c n", p=P)),
                (xw[:, 3], a["Wo0"].rearrange("(c p) n -> p c n", p=P)),
            ):
                sp.dma_start(dst, src).then_inc(ld_once, 16)
            with sp.Fori(0, B) as b:
                g = Eng(sp, b)

                def el(ap, pat, **kw):
                    return ap[bass.ds(b, 1)].rearrange(pat, **kw)

                for u in range(U):
                    sp.dma_start(X[:, 2 * u:2 * u + 2], a["x"][bass.ds(b, 1), 256 * u:256 * u + 256, :].rearrange("a (t p) d -> p (a t) d", p=P)).then_inc(ld_x[u].sem, 16)
                sp.wait_ge(V.full, g.total(V, marks["l0"][0]))
                g.plain()
                sp.dma_start(maskI, el(a["maskT"], "a k n -> (a k) n")).then_inc(ld_mask.sem, 16)
                sp.dma_start(wqkv1, a["qkv1T"].rearrange("(c p) n -> p c n", p=P)).then_inc(ld_w1.sem, 16)
                sp.wait_ge(projp_zero.sem, g.nth(projp_zero, 1))
                for h in range(H):
                    sp.dma_start(projp[32 * (h % HG):32 * (h % HG) + DK, h // HG], a["projT"][DK * h:DK * h + DK, :]).then_inc(ld_w1.sem, 16)
                sp.dma_start(projp[DK:DK + 1, 0], a["proj_b"]).then_inc(ld_w1.sem, 16)
                sp.wait_ge(V.full, g.total(V, marks["self"][0]))
                sp.dma_start(w_out, a["w_out"].rearrange("(c p) n -> p c n", p=P)).then_inc(ld_wout.sem, 16)
                for t in range(T):
                    if t >= 3:
                        sp.wait_ge(V.free, g.total(V, marks["bias"][t - 3]))
                    sp.dma_start(biasb[:, t % 3], a["fside"][0, :, P * t:P * t + P, :].rearrange("h q k -> q h k")).then_inc(ld_bias[t % 3].sem, 16)
                    if t >= 3:
                        for w in ("Wr", "Wv", "Ws", "W2", "Wo", "W1", "W3")[2 * (t - 3):2 * (t - 2)]:
                            sp.dma_start(w7[:, EXPERT.index(w)], a[w].rearrange("(c p) n -> p c n", p=P)).then_inc(ld_w7.sem, 16)
                for x in range(2):
                    sp.dma_start(Krw[:, x], a["K_rwkv"][x].rearrange("(c p) n -> p c n", p=P)).then_inc(ld_exp.sem, 16)
                    sp.dma_start(Vrw[:, x], a["V_rwkv"][x].rearrange("(c p) n -> p c n", p=P)).then_inc(ld_exp.sem, 16)
                for u in range(U):
                    sp.wait_ge(xn_ready.sem, g.nth(xn_ready, 8 * U + u + 1))
                    sp.dma_start(out[bass.ds(b, 1), 256 * u:256 * u + 256, :].rearrange("a (t p) d -> p (a t) d", p=P), X[:, 2 * u:2 * u + 2]).then_inc(st_out.sem, 16)
                sp.wait_ge(st_out.sem, g.nth(st_out, 16 * U))
                g.plain()
                sp.wait_ge(V.free, g.total(V, marks["end"][0]))
                g.plain()


        @block.gpsimd
        def _(pool):
            steps = [0]

            def seq(ins):
                steps[0] += 1
                ins.then_inc(const_ready, 1)
                pool.wait_ge(const_ready, steps[0])

            def sel(ap, op, fill, base, pattern, cm):
                seq(pool.affine_select(out=ap, in_=ap, compare_op=op, fill=fill, base=base, pattern=pattern,
                                       channel_multiplier=cm))
            seq(pool.memset(ident[:], 0.0))
            sel(ident[:], ALU.not_equal, 1.0, 0, [[-1, P]], 1)
            seq(pool.memset(identb[:], 0.0))
            sel(identb[:], ALU.not_equal, 1.0, 0, [[-1, P]], 1)
            seq(pool.memset(ones[:], 1.0))
            seq(pool.memset(above[:], 1.0))
            sel(above[:], ALU.is_gt, 0.0, 0, [[1, P]], -1)
            seq(pool.memset(upto[:], 1.0))
            sel(upto[:], ALU.is_ge, 0.0, 0, [[-1, P]], 1)
            seq(pool.memset(selden[:], 0.0))
            sel(selden[:].rearrange("p (g m) -> p g m", g=4), ALU.not_equal, 1.0, -DK, [[-32, 4], [0, 32]], 1)
            seq(pool.memset(headm[:], 1.0))
            sel(headm[:], ALU.is_ge, 0.0, 0, [[-DK, 8]], 1)
            sel(headm[:], ALU.is_ge, 0.0, DK - 1, [[DK, 8]], -1)
            seq(pool.memset(half01[0:64, 0:1], 1.0))
            seq(pool.memset(half01[64:128, 0:1], 0.0))
            seq(pool.memset(half01[0:64, 1:2], 0.0))
            seq(pool.memset(half01[64:128, 1:2], 1.0))
            seq(pool.memset(nhalf[:], -0.5))
            seq(pool.iota(iota[:], pattern=[[1, NSEL]], base=0, channel_multiplier=0,
                          allow_small_or_imprecise_dtypes=True))
            seq(pool.memset(XT[:, :, 0:PAD], 0.0))
            seq(pool.memset(XT[:, :, PAD + N:NP], 0.0))
            seq(pool.memset(vpad0[:], 0.0))
            seq(pool.memset(unseen[:], NEG))
            assert steps[0] == CONSTS

            sc2, t2 = r(13312, D), r(14336, HT, D)
            pool.wait_ge(prep_dve, 7)
            pool.tensor_tensor(t2, t2, W2T[:], ALU.subtract).then_inc(prep_pool, 1)
            pool.wait_ge(prep_pool, 1)
            pool.tensor_tensor(W2T[:], t2, sc2.unsqueeze(1).to_broadcast([P, HT, D]), ALU.mult).then_inc(prep_pool, 1)

            with pool.Fori(0, B) as b:
                g = Eng(pool, b)
                norm = [0]

                def rstd_unit(u=None):
                    k = norm[0]
                    norm[0] += 1
                    u = k % U if u is None else u
                    pool.wait_ge(ve_ready.sem, g.nth(ve_ready, k + 1))
                    pool.tensor_tensor(rstd[:, 2 * u:2 * u + 2], ve[:, 2 * u:2 * u + 2], nhalf[:, 0:2], ALU.pow).then_inc(rstd_ready.sem, 1)

                for u in range(U):
                    rstd_unit()
                pool.wait_ge(A.full, g.total(A, marks["srow"][0]))
                g.plain()
                pool.memset(kEO[:, :, :, 0:PAD], 0.0).then_inc(kpad_zero.sem, 1)
                pool.memset(kEO[:, :, :, PAD + N:NP], 0.0).then_inc(kpad_zero.sem, 1)
                pool.wait_ge(ss0_ready.sem, g.nth(ss0_ready, 1))
                pool.tensor_tensor(rn0[:], ss0[:], nhalf[:, 0:T], ALU.pow).then_inc(rn0_ready.sem, 1)
                for k in range(WP):
                    pool.wait_ge(rs_ready.sem, g.nth(rs_ready, k + 1))
                    i, h = k // PAIRS, 2 * (k % PAIRS)
                    pool.tensor_tensor(E[:, i % 2, h:h + 2], E[:, i % 2, h:h + 2],
                                             rs[:, i % 2, h:h + 2].unsqueeze(2).to_broadcast([P, 2, KEYS]), ALU.mult).then_inc(e_norm.sem, 1)
                for u in range(U):
                    rstd_unit()
                pool.wait_ge(V.full, g.total(V, marks["l0"][0]))
                g.plain()
                pool.memset(projp, 0.0).then_inc(projp_zero.sem, 1)
                pool.memset(V32[:, :, :, DK + 1:32], 0.0).then_inc(v_zero.sem, 1)
                pool.memset(V32[:, :, :, DK:DK + 1], 1.0).then_inc(v_zero.sem, 1)
                for u in range(2 * U):
                    rstd_unit()
                for t in range(T):
                    pool.wait_ge(ssq_ready.sem, g.nth(ssq_ready, 2 * (t + 1)))
                    g.plain()
                    pool.tensor_scalar(rqk[:, t], ssq[:, t], 1e-24, None, ALU.max).then_inc(pool_step.sem, 1)
                    pool.wait_ge(pool_step.sem, g.nth(pool_step, t + 1))
                    pool.tensor_tensor(rqk[:, t], rqk[:, t], nhalf[:, 0:2], ALU.pow).then_inc(rqk_ready.sem, 1)
                pool.wait_ge(R1.full, g.total(R1, R1.jobs))
                g.plain()
                pool.memset(vpad1, 0.0).then_inc(vpad1_zero.sem, 1)
                for u in range(U):
                    rstd_unit()

                def shift(t):
                    pool.wait_ge(mx_ready.sem, g.nth(mx_ready, t + 1))
                    pool.tensor_tensor(SC[:, t % 3], SC[:, t % 3],
                                             mx[:, t % 2].unsqueeze(2).to_broadcast([P, H, S2]), ALU.subtract).then_inc(sc_shift.sem, 1)

                def divide(t):
                    pool.wait_ge(sums_ready.sem, g.nth(sums_ready, t + 1))
                    pool.tensor_tensor(SC[:, t % 3], SC[:, t % 3],
                                             rs[:, t % 2].unsqueeze(2).to_broadcast([P, H, S2]), ALU.mult).then_inc(en_ready.sem, 1)
                shift(0)
                shift(1)
                divide(0)
                for t in range(T + 1):
                    if t + 2 < T:
                        shift(t + 2)
                    if t + 1 < T:
                        divide(t + 1)
                    if t >= 3 and t % 2 == 1:
                        rstd_unit((t - 3) // 2)
                    if t >= 2 and t % 2 == 0:
                        rstd_unit(t // 2 - 1)
                rstd_unit(U - 1)
                for u in range(U):
                    rstd_unit()
                    pool.tensor_tensor(X[:, 2 * u:2 * u + 2], X[:, 2 * u:2 * u + 2], XP[:, 2 * u:2 * u + 2],
                                             ALU.add).then_inc(x2_ready.sem, 1)
                for u in range(U):
                    rstd_unit()
                assert norm[0] == 9 * U, norm[0]

        @block.scalar
        def _(act):
            act.wait_ge(const_ready, CONSTS)
            act.wait_ge(ld_once, 16 * ONCE)
            with act.Fori(0, B) as b:
                g = Eng(act, b)

                def el(ap, pat, **kw):
                    return ap[bass.ds(b, 1)].rearrange(pat, **kw)

                act.dma_start(ctxT[:], el(a["ctxT"], "a (c p) n -> p (a c) n", p=P)).then_inc(ld_ctx.sem, 16)
                act.dma_start(ctxV[:], el(a["ctx"], "a k d -> (a k) d")).then_inc(ld_ctx.sem, 16)
                act.dma_start(xT0, el(a["xT"], "a (c p) n -> p (a c) n", p=P)).then_inc(ld_xT.sem, 16)
                act.wait_ge(prep_pe, 2)
                act.dma_start(wqkv, a["wqkv_l"].rearrange("(c p) n -> p c n", p=P)).then_inc(ld_wqkv.sem, 16)

                def evac_T(u, scale=None, bias=None):
                    act.wait_ge(A.full, g.take(A))
                    s = g.bank(A).rearrange("p (c n) -> p c n", c=DC)
                    for c in range(DC):
                        dst = XT[:, c, PAD + 256 * u:PAD + 256 * u + 256]
                        if scale is None:
                            ins = act.activation(dst, s[:, c], ACT.Copy)
                        else:
                            ins = act.activation(dst, s[:, c], ACT.Identity, scale=cols[:, scale + c:scale + c + 1],
                                                 bias=cols[:, bias + c:bias + c + 1])
                    ins.then_inc(A.free, 1)

                for k in range(2):
                    for n in range(NH):
                        act.wait_ge(A.full, g.take(A))
                        act.activation(Srow[:, k, NC * n:NC * n + NC], g.bank(A), ACT.Copy).then_inc(A.free, 1)
                act.wait_ge(prep_dve, PREP)
                act.wait_ge(prep_pool, POOL_PREP)
                act.dma_start(wq_h, a["wq_h"].rearrange("(c p) n -> p c n", p=P)).then_inc(ld_wheavy.sem, 16)
                act.dma_start(wkv_h, a["wkv_h"].rearrange("(c p) n -> p c n", p=P)).then_inc(ld_wheavy.sem, 16)
                act.dma_start(wo_h, a["wo_h"].rearrange("(c p) n -> p c n", p=P)).then_inc(ld_wheavy.sem, 16)
                act.dma_start(wo_l, a["wo_l"].rearrange("(c p) n -> p c n", p=P)).then_inc(ld_wheavy.sem, 16)
                evac_T(0, 0, 2)
                evac_T(1, 0, 2)
                for n in range(NH):
                    for m in range(PAIRS):
                        act.wait_ge(A.full, g.take(A))
                        act.activation(qT[:, m, NC * n:NC * n + NC], g.bank(A), ACT.Copy).then_inc(A.free, 1)
                    for m in range(PAIRS):
                        if n == 0 and m == PAIRS - 2:
                            evac_T(2, 0, 2)
                            evac_T(3, 0, 2)
                        act.wait_ge(A.full, g.take(A))
                        s = g.bank(A)
                        for e in range(2):
                            ins = act.activation(kEO[:, m, e, PAD + NC * n:PAD + NC * n + NC], s, ACT.Copy,
                                                 scale=half01[:, e:e + 1])
                        ins.then_inc(A.free, 1)
                for u in range(U):
                    act.wait_ge(A.full, g.take(A))
                    s = g.bank(A)
                    act.activation(OHT[:, :, 256 * u:256 * u + 256], s.rearrange("p (h n) -> p h n", h=2),
                                   ACT.Copy).then_inc(A.free, 1)
                for m in range(PAIRS):
                    act.wait_ge(A.full, g.take(A))
                    s = g.bank(A)
                    act.activation(hqT[:, m], s[:, 0:NSEL], ACT.Copy)
                    for e in range(2):
                        ins = act.activation(hk(m)[:, e], s[:, NSEL:2 * NSEL], ACT.Copy, scale=half01[:, e:e + 1])
                    ins.then_inc(A.free, 1)

                def window_exp(k):
                    i, p = k // PAIRS, k % PAIRS
                    if i >= 2:
                        act.wait_ge(TR.full, g.total(TR, k + 1 - 2 * PAIRS))
                    act.wait_ge(SR.full, g.take(SR))
                    s = g.bank(SR).rearrange("p (e k) -> p e k", e=2)
                    act.wait_ge(nm_ready.sem, g.nth(nm_ready, k + 1))
                    for e in range(2):
                        h = 2 * p + e
                        ins = act.activation(E[:, i % 2, h], s[:, e], ACT.Exp, scale=DH ** -0.5,
                                             bias=nm[:, i % 2, h:h + 1], accum_out=sm[:, i % 2, h:h + 1])
                    ins.then_inc(SR.free, 1)

                def window_out(i):
                    act.wait_ge(OR.full, g.take(OR))
                    s = g.bank(OR).rearrange("p (m q) -> p m q", m=PAIRS)
                    dst = qT[:, :, P * i:P * i + P] if i < T else hqT[:, :, P * (i - T):P * (i - T) + P]
                    act.activation(dst, s, ACT.Copy).then_inc(OR.free, 1)

                for k in range(-LEAD, WP + 1):
                    if k + LEAD < WP:
                        window_exp(k + LEAD)
                    if k >= PAIRS and k % PAIRS == 0:
                        window_out(k // PAIRS - 1)
                act.wait_ge(A.full, g.take(A))
                s = g.bank(A)
                act.activation(ho, s.rearrange("p (s d) -> p s d", s=2), ACT.Copy).then_inc(A.free, 1)
                evac_T(0)
                evac_T(1)
                for n in range(NH):
                    for m in range(DC):
                        if n == 0 and m == DC - 1:
                            evac_T(2)
                            evac_T(3)
                        act.wait_ge(A.full, g.take(A))
                        act.activation(qTx[:, m, NC * n:NC * n + NC], g.bank(A), ACT.Identity,
                                       bias=cols[:, 6 + m:7 + m]).then_inc(A.free, 1)
                for k in range(NH * H):
                    act.wait_ge(A.full, g.take(A))
                    s = g.bank(A)
                    if k >= 6:
                        act.wait_ge(masked.sem, g.nth(masked, k - 5))
                    act.activation(AT[:, k % 6], s[0:S2], ACT.Silu, scale=DK ** -0.5).then_inc(A.free, 1)
                evac_T(0)
                evac_T(1)
                for n in range(NH):
                    for m in range(HT):
                        if n == 0 and m == HT - 2:
                            evac_T(2)
                            evac_T(3)
                        act.wait_ge(A.full, g.take(A))
                        act.activation(Hb[:, n, m], g.bank(A), ACT.Relu).then_inc(A.free, 1)
                evac_T(0)
                evac_T(1)
                def squares(t):
                    act.wait_ge(V.full, g.total(V, marks["qk"][t]))
                    s = V.bank(marks["qk"][t] - 1)
                    for w in range(2):
                        k = 2 * t + w
                        if k >= 2:
                            act.wait_ge(ssq_ready.sem, g.nth(ssq_ready, k - 1))
                        ins = act.activation(junkf[:, w], s[:, D * w:D * w + D], ACT.Square, accum_out=ssq[:, t, w:w + 1])
                        ins.then_inc(ssq_ready.sem, 1)

                def split_evac(t):
                    for w in range(2):
                        for hh in range(2):
                            act.wait_ge(A.full, g.take(A))
                            s = g.bank(A).bitcast(BF16).rearrange("p (h n) -> p h n", h=8)
                            dst = (QT, KT)[w][0:ROWS, 8 * hh:8 * hh + 8, P * t:P * t + P]
                            act.activation(dst, s[0:ROWS], ACT.Copy).then_inc(A.free, 1)

                for t in range(T + 2):
                    if t in (2, 4):
                        evac_T(t // 2 + 1)
                    if t < T:
                        squares(t)
                    if t >= 2:
                        split_evac(t - 2)
                for k in range(2 * NH * HG * T):
                    act.wait_ge(S1.full, g.take(S1))
                    s = g.bank(S1)
                    act.activation(Pb[:, k % 4], s, ACT.Exp).then_inc(S1.free, 1)
                for u in range(U):
                    evac_T(u)
                def cross_exp(t):
                    act.wait_ge(sc_shift.sem, g.nth(sc_shift, t + 1))
                    act.activation(SC[:, t % 3], SC[:, t % 3], ACT.Exp, scale=DK ** -0.5).then_inc(sc_exp.sem, 1)

                cross_exp(0)
                cross_exp(1)
                for t in range(T):
                    for i in range(4):
                        act.wait_ge(A.full, g.take(A))
                        s = g.bank(A)
                        act.activation(PTx[:, t % 2, 4 * i:4 * i + 4], s[0:S2].rearrange("p (h q) -> p h q", h=4),
                                       ACT.Copy).then_inc(A.free, 1)
                    if t + 2 < T:
                        cross_exp(t + 2)
                evac_T(0, 18, 20)
                evac_T(1, 18, 20)
                for n in range(NH):
                    if n == 1:
                        act.wait_ge(V.free, g.total(V, marks["g"][0]))
                    for m in range(DC):
                        act.wait_ge(A.full, g.take(A))
                        act.activation(SG[:, m], g.bank(A), ACT.Sigmoid).then_inc(A.free, 1)
                    for m in range(DC):
                        act.wait_ge(A.full, g.take(A))
                        act.activation(ST[:, m], g.bank(A), ACT.Copy).then_inc(A.free, 1)
                    for m in range(DC):
                        act.wait_ge(A.full, g.take(A))
                        act.activation(SS2[:, m, NC * n:NC * n + NC], g.bank(A), ACT.Sigmoid).then_inc(A.free, 1)
                    if n == 0:
                        evac_T(2, 18, 20)
                        evac_T(3, 18, 20)
                evac_T(0, 22, 24)
                evac_T(1, 22, 24)
                for n in range(NH):
                    for x in range(2):
                        if n == 0 and x == 1:
                            evac_T(2, 22, 24)
                            evac_T(3, 22, 24)
                        for m in range(HT):
                            act.wait_ge(A.full, g.take(A))
                            act.activation(Hb[:, x, m], g.bank(A), ACT.Relu).then_inc(A.free, 1)
                    if n == 0:
                        act.wait_ge(lg_ready.sem, g.nth(lg_ready, 1))
                        act.activation(lg[:, :, 0:4], lg[:, :, 0:4], ACT.Sigmoid).then_inc(conf_ready.sem, 1)
                act.wait_ge(V.full, g.total(V, marks["expert"][2 * (NH - 1)]))

        @block.vector
        def _(dve):
            tt, ts, stt = dve.tensor_tensor, dve.tensor_scalar, dve.scalar_tensor_tensor
            steps = [0]

            def seq(ins):
                steps[0] += 1
                ins.then_inc(prep_dve, 1)
                dve.wait_ge(prep_dve, steps[0])
            absW1, absW2 = r(4096, DC, HID), r(6144, HT, D)
            sc1, hi1, lo1, t1 = r(8192, HID), r(9216, HID), r(10240, HID), r(11264, DC, HID)
            sc2, hi2, lo2, t2 = r(13312, D), r(13568, D), r(13824, D), r(14336, HT, D)
            dve.wait_ge(ld_fc, 16)
            seq(stt(absW1, W1T[:], -1.0, W1T[:], ALU.mult, ALU.max))
            dve.wait_ge(ld_proj, 16)
            seq(stt(absW2, W2T[:], -1.0, W2T[:], ALU.mult, ALU.max))
            dve.wait_ge(const_ready, CONSTS)
            dve.wait_ge(ld_once, 16 * ONCE)
            for k in range(2):
                for c in range(DC):
                    last = ts(rtb[:, k, c], ones[:], cols[:, 14 + 2 * k + c:15 + 2 * k + c], None, ALU.mult)
            seq(last)
            dve.wait_ge(prep_pe, 1)
            seq(ts(R[0:RANK, 1536:1536 + D], bk[3][0:RANK, 0:D], cols[0:RANK, 12:13], None, ALU.mult))
            for n in range(NH):
                last = ts(sc1[:, NC * n:NC * n + NC], bk[n], 1.0 / D, 1e-5, ALU.mult, ALU.max)
            ts(sc2, bk[2][:, 0:D], 1.0 / HID, 1e-5, ALU.mult, ALU.max).then_inc(prep_dve, 1)
            steps[0] += 1
            dve.wait_ge(prep_dve, steps[0])
            ts(hi2, sc2, 0.5, None, ALU.mult)
            seq(ts(lo2, sc2, -0.5, None, ALU.mult))

            def over2(v):
                return v.unsqueeze(1).to_broadcast([P, HT, D])
            tt(t2, W2T[:], over2(hi2), ALU.is_gt)
            seq(tt(W2T[:], W2T[:], over2(lo2), ALU.is_lt))
            ts(hi1, sc1, 0.5, None, ALU.mult)
            seq(ts(lo1, sc1, -0.5, None, ALU.mult))

            def over1(v):
                return v.unsqueeze(1).to_broadcast([P, DC, HID])
            tt(t1, W1T[:], over1(hi1), ALU.is_gt)
            seq(tt(W1T[:], W1T[:], over1(lo1), ALU.is_lt))
            seq(tt(t1, t1, W1T[:], ALU.subtract))
            seq(tt(W1T[:], t1, over1(sc1), ALU.mult))
            dve.wait_ge(prep_pe, 2)
            for c in range(DC):
                for n in range(NH):
                    last = tt(W1T[:, c, NC * n:NC * n + NC], W1T[:, c, NC * n:NC * n + NC], bk[4 + 2 * c + n], ALU.add)
            seq(last)
            seq(dve.reciprocal(tinv[:], tinv[:]))
            seq(ts(tinv[:], tinv[:], 1.0 / DK, None, ALU.mult))
            seq(stt(negc[:], tinv[:], -1.0, tinv[:], ALU.mult, ALU.min))
            assert steps[0] == PREP

            with dve.Fori(0, B) as b:
                g = Eng(dve, b)
                unit = [0]

                def stats(u, q=None, to=X):
                    x = X[:, 2 * u:2 * u + 2]
                    if q is not None:
                        dve.wait_ge(q.full, g.take(q))
                        s = g.bank(q).rearrange("p (t d) -> p t d", t=2)
                        tt(to[:, 2 * u:2 * u + 2], s, x, ALU.add).then_inc(q.free, 1)
                        dve.wait_ge(q.free, g.total(q))
                    for j in range(2):
                        ins = dve.bn_stats(st[:, 2 * u + j], to[:, 2 * u + j])
                    ins.then_inc(dve_step.sem, g.step())
                    dve.wait_ge(dve_step.sem, g.steps())
                    g.plain()
                    for j in range(2):
                        ins = dve.bn_aggr(mv[:, 2 * u + j], st[:, 2 * u + j])
                    ins.then_inc(dve_step.sem, g.step())
                    dve.wait_ge(dve_step.sem, g.steps())
                    ts(ve[:, 2 * u:2 * u + 2], mv[:, 2 * u:2 * u + 2, 1], EPS, None, ALU.add).then_inc(ve_ready.sem, 1)

                def normalise(u, dst, src=X):
                    unit[0] += 1
                    dve.wait_ge(rstd_ready.sem, g.nth(rstd_ready, unit[0]))
                    for t in (2 * u, 2 * u + 1):
                        ins = ts(dst[:, t], src[:, t], mv[:, t, 0:1], rstd[:, t:t + 1], ALU.subtract, ALU.mult)
                    ins.then_inc(xn_ready.sem, 1)

                def norm_all(dst, q=None, loaded=False):
                    for u in range(U):
                        if loaded:
                            dve.wait_ge(ld_x[u].sem, g.nth(ld_x[u], 16))
                        stats(u, q)
                        if u >= 1:
                            normalise(u - 1, dst)
                    normalise(U - 1, dst)

                norm_all(XN, loaded=True)
                dve.wait_ge(ld_ctx.sem, g.nth(ld_ctx, 32))
                dve.wait_ge(V.full, g.take(V))
                s = g.bank(V)
                for m in range(DC):
                    stt(kblk0[:, m], s[:, P * m:P * m + S2].unsqueeze(1).to_broadcast([P, 8, S2]), cols[:, 8 + m:9 + m],
                        headm[:].unsqueeze(2).to_broadcast([P, 8, S2]), ALU.add, ALU.mult)
                v = s[0:S2, 256:512].rearrange("p (i e d) -> p i e d", e=2, d=DK)
                bv = bvb[:].rearrange("p (i e d) -> p i e d", e=2, d=DK)
                vp = vpad0[:].rearrange("p (i e) c -> p i e c", e=2)
                for e in range(2):
                    ins = tt(vp[:, :, e, DK * e:DK * e + DK], v[:, :, e], bv[:, :, e], ALU.add)
                ins.then_inc(V.free, 1)
                dve.wait_ge(A.free, g.total(A, marks["srow"][0]))
                scraps = []

                def scrap(n):
                    if len(scraps) >= 8:
                        dve.wait_ge(dve_step.sem, g.nth(dve_step, scraps[-8]))
                    scraps.append(g.k + 1)
                    return junk[:, (len(scraps) - 1) % 8, 0:n]

                for t in range(T):
                    dve.tensor_tensor_reduce(scrap(D), X[:, t], X[:, t], 1.0, 0.0, ALU.mult, ALU.add, ss0[:, t:t + 1]).then_inc(dve_step.sem, g.step())
                dve.wait_ge(dve_step.sem, g.steps())
                ts(ss0[:], ss0[:], 1e-24, None, ALU.max).then_inc(ss0_ready.sem, 1)
                for k in range(2):
                    for t in range(T):
                        dve.tensor_tensor_reduce(scrap(P), Srow[:, k, P * t:P * t + P], ident[:], 1.0, 0.0,
                                                         ALU.mult, ALU.add, scol[:, k, t:t + 1]).then_inc(dve_step.sem, g.step())
                dve.memset(cnt[:], 0.0).then_inc(dve_step.sem, g.step())
                dve.wait_ge(dve_step.sem, g.steps())
                for k in range(2):
                    for t in range(T):
                        me = scol[:, k, t:t + 1]
                        for i, (lo, hi, op) in enumerate(((0, P * t, ALU.is_gt), (P * t + P, N, ALU.is_ge))):
                            if hi > lo:
                                ts(scrap(hi - lo), Srow[:, k, lo:hi], me, 0.0, op, ALU.add,
                                           accum_out=cnt[:, k, t, i:i + 1]).then_inc(dve_step.sem, g.step())
                        d = Srow[:, k, P * t:P * t + P]
                        stt(scrap(P), d, me, above[:], ALU.is_ge, ALU.mult, accum_out=cnt[:, k, t, 2:3]).then_inc(dve_step.sem, g.step())
                        stt(scrap(P), d, me, upto[:], ALU.is_gt, ALU.mult, accum_out=cnt[:, k, t, 3:4]).then_inc(dve_step.sem, g.step())
                dve.wait_ge(dve_step.sem, g.steps())
                dve.tensor_reduce(rank[:], cnt[:], AXX, ALU.add).then_inc(dve_step.sem, g.step())
                for t in range(T + 1):
                    dve.wait_ge(V.full, g.take(V))
                    dve.tensor_copy(V1[:, t], g.bank(V)).then_inc(V.free, 1)
                dve.wait_ge(dve_step.sem, g.steps())
                dve.wait_ge(rn0_ready.sem, g.nth(rn0_ready, 1))
                for t in range(T):
                    if t >= 4:
                        dve.wait_ge(A.full, g.total(A, marks["oh"][t // 2 - 2]))
                    for k in range(2):
                        ts(OH[:, t % 4, k], iota[:], rank[:, k, t:t + 1], rn0[:, t:t + 1], ALU.is_equal, ALU.mult)
                    ts(OH[:, t % 4, 2], iota[:], rank[:, 0, t:t + 1], None, ALU.is_equal).then_inc(oh_ready.sem, 1)
                for k in range(2):
                    for c in range(DC):
                        dve.wait_ge(V.full, g.take(V))
                        ts(xsel[:, k, c], g.bank(V)[:, 0:NSEL], cols[:, 4 + c:5 + c], float(D) ** 0.5, ALU.mult,
                           ALU.mult).then_inc(V.free, 1)
                for h in range(2):
                    dve.wait_ge(V.full, g.take(V))
                    dve.tensor_copy(hv[:, h], g.bank(V)).then_inc(V.free, 1)

                def window_max(k):
                    i, p = k // PAIRS, k % PAIRS
                    dve.wait_ge(SR.full, g.total(SR, k + 1))
                    s = SR.bank(k).rearrange("p (e k) -> p e k", e=2)
                    dve.tensor_reduce(mx[:, i % 2, 2 * p:2 * p + 2], s, AXX, ALU.max).then_inc(dve_step.sem, g.step())
                    dve.wait_ge(dve_step.sem, g.steps())
                    ts(nm[:, i % 2, 2 * p:2 * p + 2], mx[:, i % 2, 2 * p:2 * p + 2], -(DH ** -0.5), None,
                             ALU.mult).then_inc(nm_ready.sem, 1)

                def window_sum(k):
                    i, p = k // PAIRS, k % PAIRS
                    dve.wait_ge(SR.free, g.total(SR, k + 1))
                    dve.reciprocal(rs[:, i % 2, 2 * p:2 * p + 2], sm[:, i % 2, 2 * p:2 * p + 2]).then_inc(rs_ready.sem, 1)

                for k in range(-LEAD, WP):
                    if k + LEAD < WP:
                        window_max(k + LEAD)
                    if 0 <= k:
                        i, p = k // PAIRS, k % PAIRS
                        if i >= 2 and p == 0:
                            dve.wait_ge(OR.full, g.total(OR, i - 1))
                        dve.wait_ge(TR.full, g.take(TR))
                        dve.tensor_copy(PT[:, i % 2, p].rearrange("p a q -> p (a q)"), g.bank(TR)).then_inc(TR.free, 1)
                    if 0 < k + LEAD <= WP:
                        window_sum(k + LEAD - 1)
                norm_all(X, V)
                dve.wait_ge(ld_mask.sem, g.nth(ld_mask, 16))
                ts(maskN, maskI, 0.0, None, ALU.not_equal).then_inc(mask_ready.sem, 1)
                dve.wait_ge(mask_ready.sem, g.nth(mask_ready, 1))
                for n in range(NH):
                    for m in range(DC):
                        for k in range(H * n + 8 * m, H * n + 8 * m + 8):
                            dve.wait_ge(A.free, g.total(A, marks["silu"][0] + k + 1))
                            tt(AT[:, k % 6], AT[:, k % 6], maskN[:, NC * n:NC * n + NC], ALU.mult).then_inc(masked.sem, 1)
                        dve.wait_ge(V.full, g.take(V))
                        dve.tensor_copy(oTx[:, m, NC * n:NC * n + NC], g.bank(V)).then_inc(V.free, 1)
                norm_all(X, V)

                sq = [0]

                def square(buf):
                    for m in range(HT):
                        dve.wait_ge(A.free, g.total(A, marks["relu"][sq[0]]))
                        sq[0] += 1
                        tt(Hb[:, buf, m], Hb[:, buf, m], Hb[:, buf, m], ALU.mult).then_inc(sq_ready.sem, 1)

                square(0)
                square(1)
                norm_all(X, V)
                dve.wait_ge(v_zero.sem, g.nth(v_zero, 2))
                for i in range(2):
                    dve.tensor_copy(QS[:, i, 0, :, 96:97], negc[:].unsqueeze(2))
                    ins = dve.memset(QS[:, i, 1, :, 96:97], 1.0)
                ins.then_inc(dve_step.sem, g.step())
                qkv = qkn.rearrange("p (w h d) -> p w h d", w=2, h=H)
                r1v = r1.rearrange("p (w h d) -> p w h d", w=2, h=H)

                def part(i, w, s, step=1, n=1):
                    v = QS[:, i, w, :, 0:96].rearrange("p h (s d) -> p h s d", d=DK)
                    return v[:, :, s] if n == 1 else v[:, :, s:s + step * (n - 1) + 1:step]

                def rep(v, n):
                    return v.unsqueeze(2).to_broadcast([P, H, n, DK])

                for t in range(T):
                    i = t % 2
                    dve.wait_ge(rqk_ready.sem, g.nth(rqk_ready, t + 1))
                    dve.wait_ge(V.full, g.take(V))
                    s = g.bank(V)
                    stt(qkv[:, 0], s[:, 0:D].rearrange("p (h d) -> p h d", h=H), rqk[:, t, 0:1],
                        tinv[:].unsqueeze(2).to_broadcast([P, H, DK]), ALU.mult, ALU.mult)
                    ts(qkn[:, D:2 * D], s[:, D:2 * D], rqk[:, t, 1:2], None, ALU.mult).then_inc(V.free, 1)
                    dve.wait_ge(V.free, g.total(V))
                    if t % 2 == 1:
                        dve.wait_ge(V.full, g.take(V))
                        s = g.bank(V).rearrange("p (t h d) -> p t h d", t=2, h=H)
                        for j in range(2):
                            ins = dve.tensor_copy(V32[:, t - 1 + j, :, 0:DK], s[:, j])
                        ins.then_inc(V.free, 1)
                    if t >= 2:
                        dve.wait_ge(A.full, g.total(A, marks["split"][t - 2]))
                    dve.tensor_copy(part(i, 0, 1, 2, 3), rep(qkv[:, 0], 3))
                    dve.tensor_copy(part(i, 1, 0, 1, 3), rep(qkv[:, 1], 3)).then_inc(dve_step.sem, g.step())
                    dve.wait_ge(dve_step.sem, g.steps())
                    tt(r1v[:, 0], qkv[:, 0], part(i, 0, 1), ALU.subtract)
                    tt(r1v[:, 1], qkv[:, 1], part(i, 1, 1), ALU.subtract).then_inc(dve_step.sem, g.step())
                    dve.wait_ge(dve_step.sem, g.steps())
                    dve.tensor_copy(part(i, 0, 2, 2, 2), rep(r1v[:, 0], 2))
                    dve.tensor_copy(part(i, 1, 3, 1, 2), rep(r1v[:, 1], 2)).then_inc(dve_step.sem, g.step())
                    dve.wait_ge(dve_step.sem, g.steps())
                    tt(part(i, 0, 0), r1v[:, 0], part(i, 0, 4), ALU.subtract)
                    tt(part(i, 1, 5), r1v[:, 1], part(i, 1, 4), ALU.subtract).then_inc(qs_ready.sem, 1)
                for n in range(NH):
                    for hg in range(HG):
                        if n or hg:
                            dve.wait_ge(ot_ready.sem, g.nth(ot_ready, HG * n + hg))
                        dve.wait_ge(O1.full, g.take(O1))
                        dve.tensor_copy(OS, g.bank(O1)).then_inc(O1.free, 1)
                        dve.wait_ge(R1.full, g.take(R1))
                        dve.reciprocal(RC, g.bank(R1)).then_inc(R1.free, 1)
                        dve.wait_ge(R1.free, g.total(R1))
                        tt(OTp[:, hg, NC * n:NC * n + NC], OS, RC, ALU.mult).then_inc(ot_ready.sem, 1)
                dve.wait_ge(R1.full, g.total(R1))
                dve.wait_ge(vpad1_zero.sem, g.nth(vpad1_zero, 1))
                for m in range(DC):
                    tt(kblk1[:, m], ctxT[:, m].unsqueeze(1).to_broadcast([P, 8, S2]),
                       headm[:].unsqueeze(2).to_broadcast([P, 8, S2]), ALU.mult)
                v = ctxV[:].rearrange("p (i e d) -> p i e d", e=2, d=DK)
                vp = vpad1.rearrange("p (i e) c -> p i e c", e=2)
                for e in range(2):
                    ins = dve.tensor_copy(vp[:, :, e, DK * e:DK * e + DK], v[:, :, e])
                ins.then_inc(kv1_ready.sem, 1)
                norm_all(X, V)

                def cross_max(t):
                    dve.wait_ge(ld_bias[t % 3].sem, g.nth(ld_bias[t % 3], 16 * (t // 3 + 1)))
                    if t >= 3:
                        dve.wait_ge(A.full, g.total(A, marks["cp"][t - 3]))
                    for i in range(4):
                        dve.wait_ge(V.full, g.take(V))
                        s = g.bank(V)[:, 0:4 * S2].rearrange("p (h k) -> p h k", h=4)
                        tt(SC[:, t % 3, 4 * i:4 * i + 4], s, biasb[:, t % 3, 4 * i:4 * i + 4], ALU.add).then_inc(V.free, 1)
                    dve.wait_ge(V.free, g.total(V))
                    dve.tensor_reduce(mx[:, t % 2], SC[:, t % 3], AXX, ALU.max).then_inc(mx_ready.sem, 1)

                def cross_sum(t):
                    dve.wait_ge(sc_exp.sem, g.nth(sc_exp, t + 1))
                    dve.tensor_reduce(sm[:, t % 2], SC[:, t % 3], AXX, ALU.add).then_inc(dve_step.sem, g.step())
                    dve.wait_ge(dve_step.sem, g.steps())
                    dve.reciprocal(rs[:, t % 2], sm[:, t % 2]).then_inc(sums_ready.sem, 1)

                cross_max(0)
                cross_max(1)
                cross_sum(0)
                for t in range(T + 1):
                    if t >= 1:
                        dve.wait_ge(V.full, g.take(V))
                        s = g.bank(V)
                        dve.tensor_copy(oT1[:, :, P * t - P:P * t], s[:, 0:2 * P].rearrange("p (m q) -> p m q", m=DC)).then_inc(V.free, 1)
                    if t + 2 < T:
                        cross_max(t + 2)
                    if t + 1 < T:
                        cross_sum(t + 1)
                    if t >= 3 and t % 2 == 1:
                        u = (t - 3) // 2
                        normalise(u, X)
                        dve.wait_ge(xn_ready.sem, g.nth(xn_ready, unit[0]))
                        stats(u)
                    if t >= 2 and t % 2 == 0:
                        if t >= 4:
                            normalise(t // 2 - 2, XN)
                        stats(t // 2 - 1, V)
                normalise(U - 1, X)
                dve.wait_ge(xn_ready.sem, g.nth(xn_ready, unit[0]))
                stats(U - 1)
                normalise(U - 1, XN)
                for n in range(NH):
                    dve.wait_ge(A.free, g.total(A, marks["sg"][n]))
                    for m in range(DC):
                        dve.wait_ge(V.full, g.take(V))
                        tt(G[:, m], g.bank(V), SG[:, m], ALU.mult).then_inc(V.free, 1)
                    for u in range(2 * n, 2 * n + 2):
                        stats(u, V, XP)
                        normalise(u, XN, XP)
                def shares():
                    dve.wait_ge(V.full, g.take(V))
                    s = g.bank(V)[:, 0:8 * T].rearrange("p (t c) -> p t c", c=8)
                    dve.tensor_copy(lg[:, :, 0:7], s[:, :, 0:7]).then_inc(V.free, 1)
                    dve.wait_ge(V.free, g.total(V))
                    dve.memset(lg[:, :, 7:8], 0.0).then_inc(lg_ready.sem, 1)
                    dve.wait_ge(conf_ready.sem, g.nth(conf_ready, 1))
                    conf = lg[:, :, 0:3]

                    def step(ins):
                        ins.then_inc(dve_step.sem, g.step())
                        dve.wait_ge(dve_step.sem, g.steps())
                    step(tt(bids[:], conf, cap[:].unsqueeze(1).to_broadcast([P, T, 3]), ALU.mult))
                    step(tt(bids[:], bids[:], lg[:, :, 3:4].to_broadcast([P, T, 3]), ALU.mult))
                    step(tt(bids[:], bids[:], lg[:, :, 4:7], ALU.add))
                    b0, b1, b2 = (bids[:, :, i:i + 1] for i in range(3))
                    tt(win[:, :, 0:1], b0, b1, ALU.is_ge)
                    tt(cc[:, :, 0:1], b0, b2, ALU.is_ge)
                    tt(win[:, :, 1:2], b1, b0, ALU.is_gt)
                    tt(cc[:, :, 1:2], b1, b2, ALU.is_ge)
                    tt(win[:, :, 2:3], b2, b0, ALU.is_gt)
                    tt(cc[:, :, 2:3], b2, b1, ALU.is_gt)
                    step(ts(dd[:], conf, 1e-6, None, ALU.add))
                    tt(win[:], win[:], cc[:], ALU.mult)
                    step(dve.reciprocal(dd[:], dd[:]))
                    step(tt(dd[:], dd[:], conf, ALU.mult))
                    step(tt(cc[:], dd[:], win[:], ALU.mult))

                for n in range(NH):
                    square(0)
                    square(1)
                    if n == 0:
                        shares()
                    dve.wait_ge(A.free, g.total(A, marks["ss2"][1]))
                    for m in range(DC):
                        dve.wait_ge(V.full, g.take(V))
                        tt(TT[:, m], g.bank(V), SS2[:, m, NC * n:NC * n + NC], ALU.mult).then_inc(V.free, 1)
                    dve.wait_ge(V.free, g.total(V))
                    dve.memset(dd[:, 0:1, 0:1], 0.0).then_inc(tt_ready.sem, 1)
                    for x in range(3):
                        for u in range(2 * n, 2 * n + 2):
                            dve.wait_ge(V.full, g.take(V))
                            s = g.bank(V).rearrange("p (t d) -> p t d", t=2)
                            if x == 0:
                                dve.wait_ge(x2_ready.sem, g.nth(x2_ready, u + 1))
                            else:
                                dve.wait_ge(V.free, g.total(V, g.job(V) - 2))
                            for j in range(2):
                                t = 2 * u + j
                                ins = stt(X[:, t], s[:, j], cc[:, t, x:x + 1], X[:, t], ALU.mult, ALU.add)
                            ins.then_inc(V.free, 1)
                            if x == 2:
                                dve.wait_ge(V.free, g.total(V))
                                stats(u)
                                normalise(u, X)


def kernel(**inputs):
    import numpy as _np
    import concourse.bacc as _bacc
    from concourse import mybir as _mybir
    from concourse.bass_utils import run_bass_kernel_spmd as _run

    def a(name):
        return _np.asarray(inputs[name])

    def columns(*names):
        return _np.concatenate([a(n).reshape(DC, P).T for n in names], 1)

    laid = {
        "x": a("x"), "xT": a("x").transpose(0, 2, 1), "ctx": a("ctx_1024"), "ctxT": a("ctx_1024").transpose(0, 2, 1),
        "fside": a("fside_1x16xSxS2_0"), "maskT": a("mask_Bx1xSxS2_ik1")[:, 0].transpose(0, 2, 1),
        "wq_h": a("L0_attn_wq_h"), "wkv_h": a("L0_attn_wkv_h"), "wo_h": a("L0_attn_wo_h"),
        "wqkv_l": a("L0_attn_wqkv_l"), "wo_l": a("L0_attn_wo_l"),
        "vecA": columns("L0_attn_ln_g", "L0_attn_ln_b", "L0_attn_gamma_h", "L0_xattn_bq", "L0_xattn_bk"),
        "vecB": columns("L0_attn_rt_q", "L0_attn_rt_kv", "L1_ffn_ln1_w", "L1_ffn_ln1_b", "L1_ffn_ln2_w", "L1_ffn_ln2_b"),
        "gates": _np.concatenate([a("L1_ffn_conf_rwkv").T, a("L1_ffn_conf_trans")[:, None], a("L1_ffn_w_diff")[:, None],
                                  a("L1_ffn_W_aff")], 1),
        "Wq0": a("L0_xattn_Wq").T, "Wk0": a("L0_xattn_Wk").T, 
        "Wv0": a("L0_xattn_Wv").T, "bv": a("L0_xattn_bv"), "Wo0": a("L0_xattn_Wo").T,
        "fbT": a("L0_ffn_fast_b").T, "w_fcT": a("L0_ffn_w_fc").T, "w_projT": a("L0_ffn_w_proj").T,
        "uT": a("L0_ffn_u").T, "v": a("L0_ffn_v"), "gate": a("L0_ffn_gate").reshape(1),
        "qkv1T": a("L1_attn_qkv_w").T, "temp": a("L1_attn_temperature").reshape(H), "projT": a("L1_attn_proj_w").T,
        "proj_b": a("L1_attn_proj_b").reshape(1, D), "w_out": a("L1_xattn_w_out"),
        "capital": a("L1_ffn_capital_shares"), "Wr": a("L1_ffn_Wr"), "Wv": a("L1_ffn_Wv"),
        "Wo": a("L1_ffn_Wo"), "Ws": a("L1_ffn_Ws"), "K_rwkv": a("L1_ffn_K_rwkv"), "V_rwkv": a("L1_ffn_V_rwkv"),
        "W1": a("L1_ffn_W1"), "W2": a("L1_ffn_W2"), "W3": a("L1_ffn_W3"),
    }
    nc = _bacc.Bacc("TRN2", target_bir_lowering=False, num_devices=1)
    arrays, aps = {}, {}
    for name, x in laid.items():
        x = _np.ascontiguousarray(x)
        arrays[f"in_{name}_dram"] = x
        aps[name] = nc.dram_tensor(f"in_{name}_dram", x.shape, _mybir.dt.from_np(x.dtype), kind="ExternalInput").ap()
    out = nc.dram_tensor("out_0_dram", (B, N, D), F32, kind="ExternalOutput").ap()
    decoder(nc, aps, out)
    res = _run(nc, [arrays], core_ids=[0])
    return res.results[0]["out_0_dram"]
```
